# Optimizing a Trainium2 kernel written in Bass

```python
import numpy as np
import jax
import jax.numpy as jnp

def _softmax(x, axis=-1):
    return jax.nn.softmax(x, axis=axis)

def _gelu(x):
    return jax.nn.gelu(x, approximate=True)

def _silu(x):
    return jax.nn.silu(x)

def _sigmoid(x):
    return jax.nn.sigmoid(x)

def _layernorm(x, axis=-1, eps=1e-05):
    m = jnp.mean(x, axis=axis, keepdims=True)
    v = jnp.var(x, axis=axis, keepdims=True)
    return (x - m) / jnp.sqrt(v + eps)

def _scatter_add(tgt, idx, src, axis=0):
    return tgt.at[idx].add(src)

def _segment_sum(src, seg, n):
    return jax.ops.segment_sum(src, seg, n)
kernel_name = 'mk_recurrent_d4_jaxref_r8_7c1c13'

def setup_inputs(seed: int=0):
    np.random.seed(seed)
    _w = jnp.asarray

    def _L0_attn_setup():
        import jax, jax.numpy as jnp
        import numpy as np
        import math
        NUM_HEADS = 16
        HIDDEN = 128
        HEAD_DIM = HIDDEN // NUM_HEADS
        WIN = 64
        B, S = (2, 256)
        LN_EPS = 1e-05
        key = jax.random.key(seed)
        ks = jax.random.split(key, 8)
        sd = 1.0 / math.sqrt(HIDDEN)
        return {'x': jax.random.normal(ks[0], (B, S, HIDDEN), jnp.float32), 'Wq': jax.random.normal(ks[1], (HIDDEN, HIDDEN), jnp.float32) * sd, 'bq': jnp.zeros((HIDDEN,), jnp.float32), 'Wk': jax.random.normal(ks[2], (HIDDEN, HIDDEN), jnp.float32) * sd, 'bk': jnp.zeros((HIDDEN,), jnp.float32), 'Wv': jax.random.normal(ks[3], (HIDDEN, HIDDEN), jnp.float32) * sd, 'bv': jnp.zeros((HIDDEN,), jnp.float32), 'Wo': jax.random.normal(ks[4], (HIDDEN, HIDDEN), jnp.float32) * sd, 'bo': jnp.zeros((HIDDEN,), jnp.float32), 'relpos_table': jax.random.normal(ks[5], (WIN, HIDDEN), jnp.float32), 'ln_gamma': jnp.ones((HIDDEN,), jnp.float32), 'ln_beta': jnp.zeros((HIDDEN,), jnp.float32), 'Wrk': jax.random.normal(ks[6], (HIDDEN, HIDDEN), jnp.float32) * sd, 'brk': jnp.zeros((HIDDEN,), jnp.float32), 'Wrq': jax.random.normal(ks[7], (HIDDEN, HIDDEN), jnp.float32) * sd, 'brq': jnp.zeros((HIDDEN,), jnp.float32)}
    _L0_attn_in = _L0_attn_setup()

    def _L0_ffn_setup():
        import jax, jax.numpy as jnp
        import numpy as np
        D_MODEL = 128
        EXPANSION = 4
        D_HIDDEN = D_MODEL * EXPANSION
        NUM_STAGES = int(np.log2(D_HIDDEN))

        def butterfly(y, weights, dim):
            lead = y.shape[:-1]
            for stage in range(weights.shape[0]):
                s = 2 ** stage
                nb = dim // (2 * s)
                yr = y.reshape(*lead, nb, 2, s)
                a = yr[..., 0, :]
                b = yr[..., 1, :]
                w = weights[stage].reshape(nb, s, 2, 2)
                na = w[..., 0, 0] * a + w[..., 0, 1] * b
                nb2 = w[..., 1, 0] * a + w[..., 1, 1] * b
                y = jnp.stack([na, nb2], axis=-2).reshape(*lead, dim)
            return y
        key = jax.random.key(seed)
        ks = jax.random.split(key, 6)
        B, S = (4, 256)
        x = jax.random.normal(ks[0], (B, S, D_MODEL), jnp.float32)
        W_exp = jax.random.normal(ks[1], (D_MODEL, D_HIDDEN), jnp.float32) * 0.02
        b_exp = jnp.zeros((D_HIDDEN,), jnp.float32)
        up_weights = jax.random.normal(ks[2], (NUM_STAGES, D_HIDDEN // 2, 2, 2), jnp.float32) * 0.02
        up_bias = jnp.zeros((D_HIDDEN,), jnp.float32)
        down_weights = jax.random.normal(ks[3], (NUM_STAGES, D_HIDDEN // 2, 2, 2), jnp.float32) * 0.02
        W_con = jax.random.normal(ks[4], (D_HIDDEN, D_MODEL), jnp.float32) * 0.02
        b_con = jnp.zeros((D_MODEL,), jnp.float32)
        down_bias = jnp.zeros((D_MODEL,), jnp.float32)
        return dict(x=x, W_exp=W_exp, b_exp=b_exp, up_weights=up_weights, up_bias=up_bias, down_weights=down_weights, W_con=W_con, b_con=b_con, down_bias=down_bias)
    _L0_ffn_in = _L0_ffn_setup()

    def _L1_attn_setup():
        import jax, jax.numpy as jnp
        import numpy as np
        EPS = 1e-12

        def _l2norm(t):
            n = jnp.linalg.norm(t, axis=-1, keepdims=True)
            return t / jnp.maximum(n, EPS)
        key = jax.random.key(seed)
        kx, kq, kk, kv = jax.random.split(key, 4)
        B, N, D = (8, 512, 128)
        s = 1.0 / np.sqrt(D)
        return {'x': jax.random.normal(kx, (B, N, D), dtype=jnp.float32), 'W_q': jax.random.normal(kq, (D, D), dtype=jnp.float32) * s, 'W_k': jax.random.normal(kk, (D, D), dtype=jnp.float32) * s, 'W_v': jax.random.normal(kv, (D, D), dtype=jnp.float32) * s}
    _L1_attn_in = _L1_attn_setup()

    def _L1_ffn_setup():
        import jax, jax.numpy as jnp
        import numpy as np
        B, T, D = (8, 512, 128)
        NUM_SLOTS = 64
        TOP_K = 8
        DQ = D // 4
        DH = D // 2

        def _forward(x, slot_init, w1, b1, w2, b2, tau, Wih, Whh, bih, bhh, wq, bq, wk, bk, wv, bv, ln_g, ln_b, wvp, bvp, wo, bo):
            Bx, Tx, Dx = x.shape
            S = jnp.broadcast_to(slot_init[None], (Bx, NUM_SLOTS, Dx)).astype(x.dtype)
            slot_mean = jnp.broadcast_to(S.mean(axis=1, keepdims=True), (Bx, Tx, Dx))
            ctx = jnp.concatenate([x, slot_mean], axis=-1)
            h = jax.nn.gelu(ctx @ w1 + b1, approximate=False)
            route_logits = (h @ w2 + b2) / (jnp.abs(tau) + 0.1)
            topk_vals, topk_idx = jax.lax.top_k(route_logits, TOP_K)
            topk_w = jax.nn.softmax(topk_vals, axis=-1)
            alpha = (jax.nn.one_hot(topk_idx, NUM_SLOTS, dtype=x.dtype) * topk_w[..., None]).sum(axis=-2)
            slot_input = jnp.einsum('bts,btd->bsd', alpha, x)
            denom = alpha.sum(axis=1) + 1e-08
            si = slot_input / denom[..., None]
            gi = si @ Wih.T + bih
            gh = S @ Whh.T + bhh
            i_r, i_z, i_n = jnp.split(gi, 3, axis=-1)
            h_r, h_z, h_n = jnp.split(gh, 3, axis=-1)
            r = jax.nn.sigmoid(i_r + h_r)
            z = jax.nn.sigmoid(i_z + h_z)
            n = jnp.tanh(i_n + r * h_n)
            S_new = (1.0 - z) * n + z * S
            q = S_new @ wq + bq
            k = S_new @ wk + bk
            v = S_new @ wv + bv
            scale = DQ ** (-0.5)
            attn = jax.nn.softmax(jnp.einsum('bsq,btq->bst', q, k) * scale, axis=-1)
            S_comm = jnp.einsum('bst,btd->bsd', attn, v)
            y = S_new + S_comm
            mu = y.mean(axis=-1, keepdims=True)
            var = y.var(axis=-1, keepdims=True)
            y = (y - mu) * jax.lax.rsqrt(var + 1e-05) * ln_g + ln_b
            slot_values = y @ wvp + bvp
            out = jnp.einsum('bts,bsd->btd', alpha, slot_values)
            return out @ wo + bo
        key = jax.random.key(seed)
        ks = jax.random.split(key, 24)
        n = lambda k, shp, s=0.02: jax.random.normal(k, shp, dtype=jnp.float32) * s
        return {'x': jax.random.normal(ks[0], (B, T, D), dtype=jnp.float32), 'slot_init': n(ks[1], (NUM_SLOTS, D)), 'w1': n(ks[2], (2 * D, DH)), 'b1': jnp.zeros((DH,)), 'w2': n(ks[3], (DH, NUM_SLOTS)), 'b2': jnp.zeros((NUM_SLOTS,)), 'tau': jnp.ones((1,)), 'Wih': n(ks[4], (3 * D, D)), 'Whh': n(ks[5], (3 * D, D)), 'bih': jnp.zeros((3 * D,)), 'bhh': jnp.zeros((3 * D,)), 'wq': n(ks[6], (D, DQ)), 'bq': jnp.zeros((DQ,)), 'wk': n(ks[7], (D, DQ)), 'bk': jnp.zeros((DQ,)), 'wv': n(ks[8], (D, D)), 'bv': jnp.zeros((D,)), 'ln_g': jnp.ones((D,)), 'ln_b': jnp.zeros((D,)), 'wvp': n(ks[9], (D, D)), 'bvp': jnp.zeros((D,)), 'wo': n(ks[10], (D, D)), 'bo': jnp.zeros((D,))}
    _L1_ffn_in = _L1_ffn_setup()

    def _L2_attn_setup():
        import jax, jax.numpy as jnp
        import numpy as np
        B, S, H, N, D = (2, 256, 128, 16, 64)
        PAD = -30000.0
        key = jax.random.key(seed)
        kx, kqkv, kout, krpe = jax.random.split(key, 4)
        x = jax.random.normal(kx, (B, S, H), jnp.float32)
        qkv = jax.random.normal(kqkv, (H, 3, N, D), jnp.float32) * H ** (-0.5)
        out_w = jax.random.normal(kout, (N, D, H), jnp.float32) * (N * D) ** (-0.5)
        rpe_bias = jax.random.normal(krpe, (N, S), jnp.float32) * 0.02
        return {'x': x, 'qkv': qkv, 'out_w': out_w, 'rpe_bias': rpe_bias}
    _L2_attn_in = _L2_attn_setup()

    def _L2_ffn_setup():
        import jax, jax.numpy as jnp
        import numpy as np
        D = 128
        H = 16
        HD = D // H
        E = 32
        ES = 128
        K = 4
        B, S = (2, 128)
        ROPE_BASE = 10000.0

        def _layernorm(x, g, b):
            m = x.mean(-1, keepdims=True)
            v = ((x - m) ** 2).mean(-1, keepdims=True)
            return (x - m) * jax.lax.rsqrt(v + 1e-05) * g + b

        def _forward(src, wq, wk, wv, wp, wo, ln1_g, ln1_b, ln2_g, ln2_b, sel_w, keys, values):
            Bs, Ss, Ds = src.shape
            scale = 1.0 / jnp.sqrt(jnp.array(HD, dtype=src.dtype))
            x = _layernorm(src, ln1_g, ln1_b)
            q = (x @ wq).reshape(Bs, Ss, H, HD)
            k = (x @ wk).reshape(Bs, Ss, H, HD)
            v = (x @ wv).reshape(Bs, Ss, H, HD)
            pos = jnp.arange(Ss - 1, -Ss, -1, dtype=src.dtype)
            inv_freq = 1.0 / ROPE_BASE ** (jnp.arange(0, Ds, 2, dtype=src.dtype) / Ds)
            ang = pos[:, None] * inv_freq[None, :]
            pe = jnp.concatenate([jnp.sin(ang), jnp.cos(ang)], axis=-1)
            p = (pe @ wp).reshape(2 * Ss - 1, H, HD)
            ac = jnp.einsum('bihd,bjhd->bhij', q, k)
            bd_full = jnp.einsum('bihd,phd->bhip', q, p)
            rel = jnp.arange(Ss)[:, None] - jnp.arange(Ss)[None, :] + (Ss - 1)
            bd = bd_full[:, :, jnp.arange(Ss)[:, None], rel]
            att = jax.nn.softmax((ac + bd) * scale, axis=-1)
            attn_out = jnp.einsum('bhij,bjhd->bihd', att, v).reshape(Bs, Ss, Ds) @ wo
            src = src + attn_out
            x2 = _layernorm(src, ln2_g, ln2_b)
            sel = jax.nn.sigmoid(x2 @ sel_w)
            scores, idx = jax.lax.top_k(sel, K)
            gate = (jax.nn.one_hot(idx, E, dtype=sel.dtype) * scores[..., None]).sum(-2)
            h = jax.nn.relu(jnp.einsum('bsd,edh->bseh', x2, keys))
            moe_out = jnp.einsum('bseh,ehd,bse->bsd', h, values, gate)
            return src + moe_out
        key = jax.random.key(seed)
        ks = jax.random.split(key, 10)
        std_scale = np.sqrt(2.0 / 18)
        w_std = std_scale / np.sqrt(D)
        return {'src': jax.random.normal(ks[0], (B, S, D), jnp.float32), 'wq': jax.random.normal(ks[1], (D, H * HD), jnp.float32) * w_std, 'wk': jax.random.normal(ks[2], (D, H * HD), jnp.float32) * w_std, 'wv': jax.random.normal(ks[3], (D, H * HD), jnp.float32) * w_std, 'wp': jax.random.normal(ks[4], (D, H * HD), jnp.float32) * w_std, 'wo': jax.random.normal(ks[5], (H * HD, D), jnp.float32) * w_std, 'ln1_g': jnp.ones((D,), jnp.float32), 'ln1_b': jnp.zeros((D,), jnp.float32), 'ln2_g': jnp.ones((D,), jnp.float32), 'ln2_b': jnp.zeros((D,), jnp.float32), 'sel_w': jax.random.normal(ks[6], (D, E), jnp.float32) / np.sqrt(D), 'keys': jax.random.normal(ks[7], (E, D, ES), jnp.float32) * w_std, 'values': jax.random.normal(ks[8], (E, ES, D), jnp.float32) * (std_scale / np.sqrt(ES))}
    _L2_ffn_in = _L2_ffn_setup()

    def _L3_attn_setup():
        import jax, jax.numpy as jnp
        import numpy as np

        def _layernorm(x, g, b, eps=1e-05):
            m = x.mean(-1, keepdims=True)
            v = x.var(-1, keepdims=True)
            return (x - m) * jax.lax.rsqrt(v + eps) * g + b

        def _mamba(x, in_w, conv_w, conv_b, xproj_w, dt_w, dt_b, A_log, D, out_w):
            Bsz, L, _ = x.shape
            d_state = A_log.shape[1]
            dt_rank = dt_w.shape[1]
            d_conv = conv_w.shape[1]
            u, z = jnp.split(x @ in_w.T, 2, axis=-1)
            u_pad = jnp.pad(u, ((0, 0), (d_conv - 1, 0), (0, 0)))
            u = sum((u_pad[:, k:k + L, :] * conv_w[:, k] for k in range(d_conv))) + conv_b
            u = jax.nn.silu(u)
            dbc = u @ xproj_w.T
            dt = jax.nn.softplus(dbc[..., :dt_rank] @ dt_w.T + dt_b)
            Bm = dbc[..., dt_rank:dt_rank + d_state]
            Cm = dbc[..., dt_rank + d_state:]
            A = -jnp.exp(A_log)
            dA = jnp.exp(dt[..., None] * A)
            dBu = (dt * u)[..., None] * Bm[:, :, None, :]

            def step(h, inp):
                dA_t, dBu_t, C_t = inp
                h = dA_t * h + dBu_t
                return (h, jnp.einsum('bdn,bn->bd', h, C_t))
            h0 = jnp.zeros((Bsz, u.shape[-1], d_state), x.dtype)
            _, ys = jax.lax.scan(step, h0, (dA.swapaxes(0, 1), dBu.swapaxes(0, 1), Cm.swapaxes(0, 1)))
            y = ys.swapaxes(0, 1) + u * D
            return y * jax.nn.silu(z) @ out_w.T
        key = jax.random.key(seed)
        ks = jax.random.split(key, 3)
        d_model, d_state, d_conv, d_inner, dt_rank = (128, 16, 4, 256, 64)
        B, L = (2, 128)

        def mk(k, shape, s=0.02):
            return jax.random.normal(k, shape, jnp.float32) * s

        def mamba_params(kb):
            k = jax.random.split(kb, 6)
            return {'in_w': mk(k[0], (2 * d_inner, d_model)), 'conv_w': mk(k[1], (d_inner, d_conv), 0.2), 'conv_b': jnp.zeros((d_inner,), jnp.float32), 'xproj_w': mk(k[2], (dt_rank + 2 * d_state, d_inner)), 'dt_w': mk(k[3], (d_inner, dt_rank), 0.1), 'dt_b': jnp.full((d_inner,), -4.0, jnp.float32) + mk(k[4], (d_inner,), 0.5), 'Alog': jnp.log(jnp.tile(jnp.arange(1, d_state + 1, dtype=jnp.float32), (d_inner, 1))), 'D': jnp.ones((d_inner,), jnp.float32), 'out_w': mk(k[5], (d_model, d_inner))}
        pf = mamba_params(ks[0])
        pb = mamba_params(ks[1])
        inp = {'x': jax.random.normal(ks[2], (B, L, d_model), jnp.float32), 'ln_g': jnp.ones((d_model,), jnp.float32), 'ln_b': jnp.zeros((d_model,), jnp.float32)}
        for pre, p in (('f_', pf), ('b_', pb)):
            for nm, v in p.items():
                inp[pre + nm] = v
        return inp
    _L3_attn_in = _L3_attn_setup()

    def _L3_ffn_setup():
        import jax, jax.numpy as jnp
        import numpy as np
        B, S, D = (1, 256, 128)
        F = 176
        E = 16
        K = 2
        CAP_FACTOR = 1.25

        def _mlp(h, wg, wu, wd):
            return jax.nn.silu(h @ wg) * (h @ wu) @ wd
        key = jax.random.key(seed)
        ks = jax.random.split(key, 10)
        sd = 0.02
        return {'x': jax.random.normal(ks[0], (B, S, D), jnp.float32), 'router_w': jax.random.normal(ks[1], (D, E), jnp.float32) * sd, 'router_b': jnp.zeros((E,), jnp.float32), 'w_gate': jax.random.normal(ks[2], (E, D, F), jnp.float32) * sd, 'w_up': jax.random.normal(ks[3], (E, D, F), jnp.float32) * sd, 'w_down': jax.random.normal(ks[4], (E, F, D), jnp.float32) * sd, 'sw_gate': jax.random.normal(ks[5], (D, F), jnp.float32) * sd, 'sw_up': jax.random.normal(ks[6], (D, F), jnp.float32) * sd, 'sw_down': jax.random.normal(ks[7], (F, D), jnp.float32) * sd}
    _L3_ffn_in = _L3_ffn_setup()
    _d = {'L0_attn_x': _L0_attn_in['x'], 'L0_attn_Wq': _L0_attn_in['Wq'], 'L0_attn_bq': _L0_attn_in['bq'], 'L0_attn_Wk': _L0_attn_in['Wk'], 'L0_attn_bk': _L0_attn_in['bk'], 'L0_attn_Wv': _L0_attn_in['Wv'], 'L0_attn_bv': _L0_attn_in['bv'], 'L0_attn_Wo': _L0_attn_in['Wo'], 'L0_attn_bo': _L0_attn_in['bo'], 'L0_attn_relpos_table': _L0_attn_in['relpos_table'], 'L0_attn_ln_gamma': _L0_attn_in['ln_gamma'], 'L0_attn_ln_beta': _L0_attn_in['ln_beta'], 'L0_attn_Wrk': _L0_attn_in['Wrk'], 'L0_attn_brk': _L0_attn_in['brk'], 'L0_attn_Wrq': _L0_attn_in['Wrq'], 'L0_attn_brq': _L0_attn_in['brq'], 'L0_ffn_W_exp': _L0_ffn_in['W_exp'], 'L0_ffn_b_exp': _L0_ffn_in['b_exp'], 'L0_ffn_up_weights': _L0_ffn_in['up_weights'], 'L0_ffn_up_bias': _L0_ffn_in['up_bias'], 'L0_ffn_down_weights': _L0_ffn_in['down_weights'], 'L0_ffn_W_con': _L0_ffn_in['W_con'], 'L0_ffn_b_con': _L0_ffn_in['b_con'], 'L0_ffn_down_bias': _L0_ffn_in['down_bias'], 'L1_attn_W_q': _L1_attn_in['W_q'], 'L1_attn_W_k': _L1_attn_in['W_k'], 'L1_attn_W_v': _L1_attn_in['W_v'], 'L1_ffn_slot_init': _L1_ffn_in['slot_init'], 'L1_ffn_w1': _L1_ffn_in['w1'], 'L1_ffn_b1': _L1_ffn_in['b1'], 'L1_ffn_w2': _L1_ffn_in['w2'], 'L1_ffn_b2': _L1_ffn_in['b2'], 'L1_ffn_tau': _L1_ffn_in['tau'], 'L1_ffn_Wih': _L1_ffn_in['Wih'], 'L1_ffn_Whh': _L1_ffn_in['Whh'], 'L1_ffn_bih': _L1_ffn_in['bih'], 'L1_ffn_bhh': _L1_ffn_in['bhh'], 'L1_ffn_wq': _L1_ffn_in['wq'], 'L1_ffn_bq': _L1_ffn_in['bq'], 'L1_ffn_wk': _L1_ffn_in['wk'], 'L1_ffn_bk': _L1_ffn_in['bk'], 'L1_ffn_wv': _L1_ffn_in['wv'], 'L1_ffn_bv': _L1_ffn_in['bv'], 'L1_ffn_ln_g': _L1_ffn_in['ln_g'], 'L1_ffn_ln_b': _L1_ffn_in['ln_b'], 'L1_ffn_wvp': _L1_ffn_in['wvp'], 'L1_ffn_bvp': _L1_ffn_in['bvp'], 'L1_ffn_wo': _L1_ffn_in['wo'], 'L1_ffn_bo': _L1_ffn_in['bo'], 'L2_attn_qkv': _L2_attn_in['qkv'], 'L2_attn_out_w': _L2_attn_in['out_w'], 'L2_attn_rpe_bias': _L2_attn_in['rpe_bias'], 'L2_ffn_wq': _L2_ffn_in['wq'], 'L2_ffn_wk': _L2_ffn_in['wk'], 'L2_ffn_wv': _L2_ffn_in['wv'], 'L2_ffn_wp': _L2_ffn_in['wp'], 'L2_ffn_wo': _L2_ffn_in['wo'], 'L2_ffn_ln1_g': _L2_ffn_in['ln1_g'], 'L2_ffn_ln1_b': _L2_ffn_in['ln1_b'], 'L2_ffn_ln2_g': _L2_ffn_in['ln2_g'], 'L2_ffn_ln2_b': _L2_ffn_in['ln2_b'], 'L2_ffn_sel_w': _L2_ffn_in['sel_w'], 'L2_ffn_keys': _L2_ffn_in['keys'], 'L2_ffn_values': _L2_ffn_in['values'], 'L3_attn_ln_g': _L3_attn_in['ln_g'], 'L3_attn_ln_b': _L3_attn_in['ln_b'], 'L3_attn_f_in_w': _L3_attn_in['f_in_w'], 'L3_attn_f_conv_w': _L3_attn_in['f_conv_w'], 'L3_attn_f_conv_b': _L3_attn_in['f_conv_b'], 'L3_attn_f_xproj_w': _L3_attn_in['f_xproj_w'], 'L3_attn_f_dt_w': _L3_attn_in['f_dt_w'], 'L3_attn_f_dt_b': _L3_attn_in['f_dt_b'], 'L3_attn_f_Alog': _L3_attn_in['f_Alog'], 'L3_attn_f_D': _L3_attn_in['f_D'], 'L3_attn_f_out_w': _L3_attn_in['f_out_w'], 'L3_attn_b_in_w': _L3_attn_in['b_in_w'], 'L3_attn_b_conv_w': _L3_attn_in['b_conv_w'], 'L3_attn_b_conv_b': _L3_attn_in['b_conv_b'], 'L3_attn_b_xproj_w': _L3_attn_in['b_xproj_w'], 'L3_attn_b_dt_w': _L3_attn_in['b_dt_w'], 'L3_attn_b_dt_b': _L3_attn_in['b_dt_b'], 'L3_attn_b_Alog': _L3_attn_in['b_Alog'], 'L3_attn_b_D': _L3_attn_in['b_D'], 'L3_attn_b_out_w': _L3_attn_in['b_out_w'], 'L3_ffn_router_w': _L3_ffn_in['router_w'], 'L3_ffn_router_b': _L3_ffn_in['router_b'], 'L3_ffn_w_gate': _L3_ffn_in['w_gate'], 'L3_ffn_w_up': _L3_ffn_in['w_up'], 'L3_ffn_w_down': _L3_ffn_in['w_down'], 'L3_ffn_sw_gate': _L3_ffn_in['sw_gate'], 'L3_ffn_sw_up': _L3_ffn_in['sw_up'], 'L3_ffn_sw_down': _L3_ffn_in['sw_down']}
    _x0 = _d['L0_attn_x']
    _d['L0_attn_x'] = jax.random.normal(jax.random.fold_in(jax.random.key(seed), 1), (16, 256, 128), dtype=_x0.dtype)
    del _x0
    return _d

def reference(L0_attn_x, L0_attn_Wq, L0_attn_bq, L0_attn_Wk, L0_attn_bk, L0_attn_Wv, L0_attn_bv, L0_attn_Wo, L0_attn_bo, L0_attn_relpos_table, L0_attn_ln_gamma, L0_attn_ln_beta, L0_attn_Wrk, L0_attn_brk, L0_attn_Wrq, L0_attn_brq, L0_ffn_W_exp, L0_ffn_b_exp, L0_ffn_up_weights, L0_ffn_up_bias, L0_ffn_down_weights, L0_ffn_W_con, L0_ffn_b_con, L0_ffn_down_bias, L1_attn_W_q, L1_attn_W_k, L1_attn_W_v, L1_ffn_slot_init, L1_ffn_w1, L1_ffn_b1, L1_ffn_w2, L1_ffn_b2, L1_ffn_tau, L1_ffn_Wih, L1_ffn_Whh, L1_ffn_bih, L1_ffn_bhh, L1_ffn_wq, L1_ffn_bq, L1_ffn_wk, L1_ffn_bk, L1_ffn_wv, L1_ffn_bv, L1_ffn_ln_g, L1_ffn_ln_b, L1_ffn_wvp, L1_ffn_bvp, L1_ffn_wo, L1_ffn_bo, L2_attn_qkv, L2_attn_out_w, L2_attn_rpe_bias, L2_ffn_wq, L2_ffn_wk, L2_ffn_wv, L2_ffn_wp, L2_ffn_wo, L2_ffn_ln1_g, L2_ffn_ln1_b, L2_ffn_ln2_g, L2_ffn_ln2_b, L2_ffn_sel_w, L2_ffn_keys, L2_ffn_values, L3_attn_ln_g, L3_attn_ln_b, L3_attn_f_in_w, L3_attn_f_conv_w, L3_attn_f_conv_b, L3_attn_f_xproj_w, L3_attn_f_dt_w, L3_attn_f_dt_b, L3_attn_f_Alog, L3_attn_f_D, L3_attn_f_out_w, L3_attn_b_in_w, L3_attn_b_conv_w, L3_attn_b_conv_b, L3_attn_b_xproj_w, L3_attn_b_dt_w, L3_attn_b_dt_b, L3_attn_b_Alog, L3_attn_b_D, L3_attn_b_out_w, L3_ffn_router_w, L3_ffn_router_b, L3_ffn_w_gate, L3_ffn_w_up, L3_ffn_w_down, L3_ffn_sw_gate, L3_ffn_sw_up, L3_ffn_sw_down):

    def _L0_attn_ref(x, Wq, bq, Wk, bk, Wv, bv, Wo, bo, relpos_table, ln_gamma, ln_beta, Wrk, brk, Wrq, brq):
        import jax, jax.numpy as jnp
        import numpy as np
        import math
        NUM_HEADS = 16
        HIDDEN = 128
        HEAD_DIM = HIDDEN // NUM_HEADS
        WIN = 64
        B, S = (2, 256)
        LN_EPS = 1e-05
        Bsz, Slen, H = x.shape
        nh, hd = (NUM_HEADS, HEAD_DIM)
        q = (x @ Wq + bq).reshape(Bsz, Slen, nh, hd)
        k = (x @ Wk + bk).reshape(Bsz, Slen, nh, hd)
        v = (x @ Wv + bv).reshape(Bsz, Slen, nh, hd)
        mu = relpos_table.mean(-1, keepdims=True)
        var = relpos_table.var(-1, keepdims=True)
        e = (relpos_table - mu) * jax.lax.rsqrt(var + LN_EPS) * ln_gamma + ln_beta
        qi = jnp.arange(Slen)
        relpos = jnp.clip(qi[None, :] - qi[:, None], -WIN + 1, 0) + (WIN - 1)
        rk = (e @ Wrk + brk).reshape(WIN, nh, hd)
        rq = (e @ Wrq + brq).reshape(WIN, nh, hd)
        c2c = jnp.einsum('bqhd,bkhd->bhqk', q, k)
        qps = jnp.einsum('bnhd,whd->bhnw', q, rk)
        c2p = qps[:, :, qi[:, None], relpos]
        kps = jnp.einsum('bnhd,whd->bhwn', k, rq)
        p2c = kps[:, :, relpos, qi[None, :]]
        scale_factor = 3.0
        logits = (c2c + c2p + p2c) / math.sqrt(hd * scale_factor)
        causal = qi[None, :] <= qi[:, None]
        logits = jnp.where(causal[None, None], logits, jnp.finfo(logits.dtype).min)
        attn = jax.nn.softmax(logits, axis=-1)
        out = jnp.einsum('bhqk,bkhd->bqhd', attn, v).reshape(Bsz, Slen, H)
        return out @ Wo + bo

    def _L0_ffn_ref(x, W_exp, b_exp, up_weights, up_bias, down_weights, W_con, b_con, down_bias):
        import jax, jax.numpy as jnp
        import numpy as np
        D_MODEL = 128
        EXPANSION = 4
        D_HIDDEN = D_MODEL * EXPANSION
        NUM_STAGES = int(np.log2(D_HIDDEN))

        def butterfly(y, weights, dim):
            lead = y.shape[:-1]
            for stage in range(weights.shape[0]):
                s = 2 ** stage
                nb = dim // (2 * s)
                yr = y.reshape(*lead, nb, 2, s)
                a = yr[..., 0, :]
                b = yr[..., 1, :]
                w = weights[stage].reshape(nb, s, 2, 2)
                na = w[..., 0, 0] * a + w[..., 0, 1] * b
                nb2 = w[..., 1, 0] * a + w[..., 1, 1] * b
                y = jnp.stack([na, nb2], axis=-2).reshape(*lead, dim)
            return y
        h = jnp.einsum('bsd,dh->bsh', x, W_exp) + b_exp
        h = butterfly(h, up_weights, D_HIDDEN)
        h = jax.nn.gelu(h + up_bias, approximate=False)
        h = butterfly(h, down_weights, D_HIDDEN)
        y = jnp.einsum('bsh,hd->bsd', h, W_con) + b_con
        return y + down_bias

    def _L1_attn_ref(x, W_q, W_k, W_v):
        import jax, jax.numpy as jnp
        import numpy as np
        EPS = 1e-12

        def _l2norm(t):
            n = jnp.linalg.norm(t, axis=-1, keepdims=True)
            return t / jnp.maximum(n, EPS)
        Q = _l2norm(jnp.einsum('bnd,ed->bne', x, W_q))
        K = _l2norm(jnp.einsum('bnd,ed->bne', x, W_k))
        V = jnp.einsum('bnd,ed->bne', x, W_v)
        C = x.shape[1]
        global_feat = jnp.sum(K * V, axis=1, keepdims=True) / C
        return Q * global_feat

    def _L1_ffn_ref(x, slot_init, w1, b1, w2, b2, tau, Wih, Whh, bih, bhh, wq, bq, wk, bk, wv, bv, ln_g, ln_b, wvp, bvp, wo, bo):
        import jax, jax.numpy as jnp
        import numpy as np
        B, T, D = (8, 512, 128)
        NUM_SLOTS = 64
        TOP_K = 8
        DQ = D // 4
        DH = D // 2

        def _forward(x, slot_init, w1, b1, w2, b2, tau, Wih, Whh, bih, bhh, wq, bq, wk, bk, wv, bv, ln_g, ln_b, wvp, bvp, wo, bo):
            Bx, Tx, Dx = x.shape
            S = jnp.broadcast_to(slot_init[None], (Bx, NUM_SLOTS, Dx)).astype(x.dtype)
            slot_mean = jnp.broadcast_to(S.mean(axis=1, keepdims=True), (Bx, Tx, Dx))
            ctx = jnp.concatenate([x, slot_mean], axis=-1)
            h = jax.nn.gelu(ctx @ w1 + b1, approximate=False)
            route_logits = (h @ w2 + b2) / (jnp.abs(tau) + 0.1)
            topk_vals, topk_idx = jax.lax.top_k(route_logits, TOP_K)
            topk_w = jax.nn.softmax(topk_vals, axis=-1)
            alpha = (jax.nn.one_hot(topk_idx, NUM_SLOTS, dtype=x.dtype) * topk_w[..., None]).sum(axis=-2)
            slot_input = jnp.einsum('bts,btd->bsd', alpha, x)
            denom = alpha.sum(axis=1) + 1e-08
            si = slot_input / denom[..., None]
            gi = si @ Wih.T + bih
            gh = S @ Whh.T + bhh
            i_r, i_z, i_n = jnp.split(gi, 3, axis=-1)
            h_r, h_z, h_n = jnp.split(gh, 3, axis=-1)
            r = jax.nn.sigmoid(i_r + h_r)
            z = jax.nn.sigmoid(i_z + h_z)
            n = jnp.tanh(i_n + r * h_n)
            S_new = (1.0 - z) * n + z * S
            q = S_new @ wq + bq
            k = S_new @ wk + bk
            v = S_new @ wv + bv
            scale = DQ ** (-0.5)
            attn = jax.nn.softmax(jnp.einsum('bsq,btq->bst', q, k) * scale, axis=-1)
            S_comm = jnp.einsum('bst,btd->bsd', attn, v)
            y = S_new + S_comm
            mu = y.mean(axis=-1, keepdims=True)
            var = y.var(axis=-1, keepdims=True)
            y = (y - mu) * jax.lax.rsqrt(var + 1e-05) * ln_g + ln_b
            slot_values = y @ wvp + bvp
            out = jnp.einsum('bts,bsd->btd', alpha, slot_values)
            return out @ wo + bo
        return _forward(x, slot_init, w1, b1, w2, b2, tau, Wih, Whh, bih, bhh, wq, bq, wk, bk, wv, bv, ln_g, ln_b, wvp, bvp, wo, bo)

    def _L2_attn_ref(x, qkv, out_w, rpe_bias):
        import jax, jax.numpy as jnp
        import numpy as np
        B, S, H, N, D = (2, 256, 128, 16, 64)
        PAD = -30000.0
        q, k, v = jnp.einsum('bsx,xMnd->Mbnsd', x, qkv)
        s = x.shape[1]
        a = jnp.einsum('bnsd,bntd->bnst', q, k) * q.shape[-1] ** (-0.5)
        cum = jnp.cumsum(rpe_bias[:, :s], axis=-1)
        rel = jnp.arange(s)[:, None] - jnp.arange(s)[None, :]
        bias = jnp.where(rel >= 0, cum[:, jnp.clip(rel, 0)], PAD)
        a = jax.nn.softmax(a + bias, axis=-1)
        mix = jnp.einsum('bnst,bntd->bnsd', a, v)
        return jnp.einsum('bnsd,ndx->bsx', mix, out_w)

    def _L2_ffn_ref(src, wq, wk, wv, wp, wo, ln1_g, ln1_b, ln2_g, ln2_b, sel_w, keys, values):
        import jax, jax.numpy as jnp
        import numpy as np
        D = 128
        H = 16
        HD = D // H
        E = 32
        ES = 128
        K = 4
        B, S = (2, 128)
        ROPE_BASE = 10000.0

        def _layernorm(x, g, b):
            m = x.mean(-1, keepdims=True)
            v = ((x - m) ** 2).mean(-1, keepdims=True)
            return (x - m) * jax.lax.rsqrt(v + 1e-05) * g + b

        def _forward(src, wq, wk, wv, wp, wo, ln1_g, ln1_b, ln2_g, ln2_b, sel_w, keys, values):
            Bs, Ss, Ds = src.shape
            scale = 1.0 / jnp.sqrt(jnp.array(HD, dtype=src.dtype))
            x = _layernorm(src, ln1_g, ln1_b)
            q = (x @ wq).reshape(Bs, Ss, H, HD)
            k = (x @ wk).reshape(Bs, Ss, H, HD)
            v = (x @ wv).reshape(Bs, Ss, H, HD)
            pos = jnp.arange(Ss - 1, -Ss, -1, dtype=src.dtype)
            inv_freq = 1.0 / ROPE_BASE ** (jnp.arange(0, Ds, 2, dtype=src.dtype) / Ds)
            ang = pos[:, None] * inv_freq[None, :]
            pe = jnp.concatenate([jnp.sin(ang), jnp.cos(ang)], axis=-1)
            p = (pe @ wp).reshape(2 * Ss - 1, H, HD)
            ac = jnp.einsum('bihd,bjhd->bhij', q, k)
            bd_full = jnp.einsum('bihd,phd->bhip', q, p)
            rel = jnp.arange(Ss)[:, None] - jnp.arange(Ss)[None, :] + (Ss - 1)
            bd = bd_full[:, :, jnp.arange(Ss)[:, None], rel]
            att = jax.nn.softmax((ac + bd) * scale, axis=-1)
            attn_out = jnp.einsum('bhij,bjhd->bihd', att, v).reshape(Bs, Ss, Ds) @ wo
            src = src + attn_out
            x2 = _layernorm(src, ln2_g, ln2_b)
            sel = jax.nn.sigmoid(x2 @ sel_w)
            scores, idx = jax.lax.top_k(sel, K)
            gate = (jax.nn.one_hot(idx, E, dtype=sel.dtype) * scores[..., None]).sum(-2)
            h = jax.nn.relu(jnp.einsum('bsd,edh->bseh', x2, keys))
            moe_out = jnp.einsum('bseh,ehd,bse->bsd', h, values, gate)
            return src + moe_out
        return _forward(src, wq, wk, wv, wp, wo, ln1_g, ln1_b, ln2_g, ln2_b, sel_w, keys, values)

    def _L3_attn_ref(x, ln_g, ln_b, f_in_w, f_conv_w, f_conv_b, f_xproj_w, f_dt_w, f_dt_b, f_Alog, f_D, f_out_w, b_in_w, b_conv_w, b_conv_b, b_xproj_w, b_dt_w, b_dt_b, b_Alog, b_D, b_out_w):
        import jax, jax.numpy as jnp
        import numpy as np

        def _layernorm(x, g, b, eps=1e-05):
            m = x.mean(-1, keepdims=True)
            v = x.var(-1, keepdims=True)
            return (x - m) * jax.lax.rsqrt(v + eps) * g + b

        def _mamba(x, in_w, conv_w, conv_b, xproj_w, dt_w, dt_b, A_log, D, out_w):
            Bsz, L, _ = x.shape
            d_state = A_log.shape[1]
            dt_rank = dt_w.shape[1]
            d_conv = conv_w.shape[1]
            u, z = jnp.split(x @ in_w.T, 2, axis=-1)
            u_pad = jnp.pad(u, ((0, 0), (d_conv - 1, 0), (0, 0)))
            u = sum((u_pad[:, k:k + L, :] * conv_w[:, k] for k in range(d_conv))) + conv_b
            u = jax.nn.silu(u)
            dbc = u @ xproj_w.T
            dt = jax.nn.softplus(dbc[..., :dt_rank] @ dt_w.T + dt_b)
            Bm = dbc[..., dt_rank:dt_rank + d_state]
            Cm = dbc[..., dt_rank + d_state:]
            A = -jnp.exp(A_log)
            dA = jnp.exp(dt[..., None] * A)
            dBu = (dt * u)[..., None] * Bm[:, :, None, :]

            def step(h, inp):
                dA_t, dBu_t, C_t = inp
                h = dA_t * h + dBu_t
                return (h, jnp.einsum('bdn,bn->bd', h, C_t))
            h0 = jnp.zeros((Bsz, u.shape[-1], d_state), x.dtype)
            _, ys = jax.lax.scan(step, h0, (dA.swapaxes(0, 1), dBu.swapaxes(0, 1), Cm.swapaxes(0, 1)))
            y = ys.swapaxes(0, 1) + u * D
            return y * jax.nn.silu(z) @ out_w.T
        res = x
        xn = _layernorm(x, ln_g, ln_b)
        out_f = _mamba(xn, f_in_w, f_conv_w, f_conv_b, f_xproj_w, f_dt_w, f_dt_b, f_Alog, f_D, f_out_w)
        out_b = _mamba(xn[:, ::-1, :], b_in_w, b_conv_w, b_conv_b, b_xproj_w, b_dt_w, b_dt_b, b_Alog, b_D, b_out_w)[:, ::-1, :]
        return res + out_f + out_b

    def _L3_ffn_ref(x, router_w, router_b, w_gate, w_up, w_down, sw_gate, sw_up, sw_down):
        import jax, jax.numpy as jnp
        import numpy as np
        B, S, D = (1, 256, 128)
        F = 176
        E = 16
        K = 2
        CAP_FACTOR = 1.25

        def _mlp(h, wg, wu, wd):
            return jax.nn.silu(h @ wg) * (h @ wu) @ wd
        b, s, d = x.shape
        N = b * s
        NK = N * K
        C = int(np.ceil(CAP_FACTOR * NK / E))
        x_tokens = x.reshape(N, d)
        logits = x_tokens @ router_w + router_b
        probs = jax.nn.softmax(logits, axis=-1)
        vals, idx = jax.lax.top_k(probs, K)
        vals = vals / (jnp.sum(vals, axis=-1, keepdims=True) + 1e-09)
        idx_flat = idx.reshape(NK)
        vals_flat = vals.reshape(NK)
        oh_e = jax.nn.one_hot(idx_flat, E, dtype=x.dtype)
        pos = (jnp.cumsum(oh_e, axis=0) * oh_e).sum(axis=1) - 1
        within = (pos < C).astype(x.dtype)
        pos_c = jnp.clip(pos, 0, C - 1).astype(jnp.int32)
        token_ids = jnp.arange(NK) // K
        x_pair = x_tokens[token_ids] * within[:, None]
        expert_inputs = jnp.zeros((E, C, d), x.dtype).at[idx_flat, pos_c].add(x_pair)
        expert_outputs = jax.vmap(_mlp)(expert_inputs, w_gate, w_up, w_down)
        gathered = expert_outputs[idx_flat, pos_c] * (vals_flat * within)[:, None]
        output_tokens = gathered.reshape(N, K, d).sum(axis=1)
        return x + _mlp(x, sw_gate, sw_up, sw_down) + output_tokens.reshape(b, s, d)
    x = L0_attn_x
    xn = _layernorm(x, axis=-1)
    s = _L0_attn_ref(xn, L0_attn_Wq, L0_attn_bq, L0_attn_Wk, L0_attn_bk, L0_attn_Wv, L0_attn_bv, L0_attn_Wo, L0_attn_bo, L0_attn_relpos_table, L0_attn_ln_gamma, L0_attn_ln_beta, L0_attn_Wrk, L0_attn_brk, L0_attn_Wrq, L0_attn_brq)
    g = _silu(_L0_ffn_ref(xn, L0_ffn_W_exp, L0_ffn_b_exp, L0_ffn_up_weights, L0_ffn_up_bias, L0_ffn_down_weights, L0_ffn_W_con, L0_ffn_b_con, L0_ffn_down_bias))
    x = x + s * g
    xn = _layernorm(x, axis=-1)
    s = _L1_attn_ref(xn, L1_attn_W_q, L1_attn_W_k, L1_attn_W_v)
    g = _silu(_L1_ffn_ref(xn, L1_ffn_slot_init, L1_ffn_w1, L1_ffn_b1, L1_ffn_w2, L1_ffn_b2, L1_ffn_tau, L1_ffn_Wih, L1_ffn_Whh, L1_ffn_bih, L1_ffn_bhh, L1_ffn_wq, L1_ffn_bq, L1_ffn_wk, L1_ffn_bk, L1_ffn_wv, L1_ffn_bv, L1_ffn_ln_g, L1_ffn_ln_b, L1_ffn_wvp, L1_ffn_bvp, L1_ffn_wo, L1_ffn_bo))
    x = x + s * g
    xn = _layernorm(x, axis=-1)
    s = _L2_attn_ref(xn, L2_attn_qkv, L2_attn_out_w, L2_attn_rpe_bias)
    g = _silu(_L2_ffn_ref(xn, L2_ffn_wq, L2_ffn_wk, L2_ffn_wv, L2_ffn_wp, L2_ffn_wo, L2_ffn_ln1_g, L2_ffn_ln1_b, L2_ffn_ln2_g, L2_ffn_ln2_b, L2_ffn_sel_w, L2_ffn_keys, L2_ffn_values))
    x = x + s * g
    xn = _layernorm(x, axis=-1)
    s = _L3_attn_ref(xn, L3_attn_ln_g, L3_attn_ln_b, L3_attn_f_in_w, L3_attn_f_conv_w, L3_attn_f_conv_b, L3_attn_f_xproj_w, L3_attn_f_dt_w, L3_attn_f_dt_b, L3_attn_f_Alog, L3_attn_f_D, L3_attn_f_out_w, L3_attn_b_in_w, L3_attn_b_conv_w, L3_attn_b_conv_b, L3_attn_b_xproj_w, L3_attn_b_dt_w, L3_attn_b_dt_b, L3_attn_b_Alog, L3_attn_b_D, L3_attn_b_out_w)
    g = _silu(_L3_ffn_ref(xn, L3_ffn_router_w, L3_ffn_router_b, L3_ffn_w_gate, L3_ffn_w_up, L3_ffn_w_down, L3_ffn_sw_gate, L3_ffn_sw_up, L3_ffn_sw_down))
    x = x + s * g
    return x

_drawn_inputs = setup_inputs


def setup_inputs(seed=0):
    import zlib

    import numpy as np

    out = dict(_drawn_inputs(seed))
    spreads = {'L0_attn_bq': (0.0, 0.1),
     'L0_attn_bk': (0.0, 0.1),
     'L0_attn_bv': (0.0, 0.1),
     'L0_attn_bo': (0.0, 0.1),
     'L0_attn_ln_gamma': (1.0, 0.2),
     'L0_attn_ln_beta': (0.0, 0.1),
     'L0_attn_brk': (0.0, 0.1),
     'L0_attn_brq': (0.0, 0.1),
     'L0_ffn_b_exp': (0.0, 0.1),
     'L0_ffn_up_bias': (0.0, 0.1),
     'L0_ffn_b_con': (0.0, 0.1),
     'L0_ffn_down_bias': (0.0, 0.1),
     'L1_ffn_b1': (0.0, 0.1),
     'L1_ffn_b2': (0.0, 0.1),
     'L1_ffn_bih': (0.0, 0.1),
     'L1_ffn_bhh': (0.0, 0.1),
     'L1_ffn_bq': (0.0, 0.1),
     'L1_ffn_bk': (0.0, 0.1),
     'L1_ffn_bv': (0.0, 0.1),
     'L1_ffn_ln_g': (1.0, 0.2),
     'L1_ffn_ln_b': (0.0, 0.1),
     'L1_ffn_bvp': (0.0, 0.1),
     'L1_ffn_bo': (0.0, 0.1),
     'L2_ffn_ln1_g': (1.0, 0.2),
     'L2_ffn_ln1_b': (0.0, 0.1),
     'L2_ffn_ln2_g': (1.0, 0.2),
     'L2_ffn_ln2_b': (0.0, 0.1),
     'L3_attn_ln_g': (1.0, 0.2),
     'L3_attn_ln_b': (0.0, 0.1),
     'L3_attn_f_conv_b': (0.0, 0.1),
     'L3_attn_f_D': (1.0, 0.2),
     'L3_attn_b_conv_b': (0.0, 0.1),
     'L3_attn_b_D': (1.0, 0.2),
     'L3_ffn_router_b': (0.0, 0.1)}
    factors = {}
    for name, (base, spread) in spreads.items():
        noise = np.random.default_rng([zlib.crc32(name.encode()), seed]).standard_normal(out[name].shape)
        drawn = base * np.exp(spread * noise) if base else spread * noise
        out[name] = jnp.asarray(drawn.astype(out[name].dtype))
    for name, factor in factors.items():
        out[name] = (out[name] * factor).astype(out[name].dtype)
    return out
```

```python
from contextlib import ExitStack

import numpy as np

import concourse.bass as bass
from concourse import mybir

F32 = mybir.dt.float32
U32 = mybir.dt.uint32
ALU = mybir.AluOpType
ACT = mybir.ActivationFunctionType
AX_X = mybir.AxisListType.X

P = 128
T = 256
NB = 16
H = 16
BANK = 512
LN_EPS = 1e-5
MASKED = -1e30


class Scope:

    def __init__(self, nc, name):
        self.nc, self.name, self.ctx, self.nums = nc, f"{name}_{nc.next_id()}", ExitStack(), []

    def __enter__(self):
        return self

    def __exit__(self, *e):
        self.ctx.__exit__(*e)
        self.nc.reset_free_semaphores(sorted(self.nc.free_semaphores))

    def sb(self, name, shape, dt=F32):
        return self.ctx.enter_context(self.nc.sbuf_tensor(f"{self.name}_{name}", shape, dt))

    def banks(self, name, n=1):
        return self.ctx.enter_context(self.nc.psum_tensor(f"{self.name}_{name}_psum", [P, n, BANK], F32))

    def sems(self, names):
        got = [self.ctx.enter_context(self.nc.semaphore(f"{self.name}_{n}")) for n in names.split()]
        self.nums += [s.num for s in got]
        return got[0] if len(got) == 1 else got

    def barrier(self):
        lo, hi = min(self.nums), max(self.nums)
        assert hi - lo + 1 == len(self.nums), self.nums
        self.nc.all_engine_barrier(sems_to_clear=range(lo, hi + 1))


class Link:

    def __init__(self, engine, sem):
        self.engine, self.sem, self.n = engine, sem, 0

    def __call__(self, ins):
        self.n += 1
        ins.then_inc(self.sem, 1)
        self.engine.wait_ge(self.sem, self.n)


def tokens(b, n=T):
    return bass.ds(b * n, n)


def make_constants(nc, scope):
    c = {
        "mean": scope.sb("mean", [P, P]), "ones": scope.sb("ones", [P, P]), "ident": scope.sb("ident", [P, P]),
        "earlier": scope.sb("earlier", [P, P]), "eps": scope.sb("eps", [P, 1]),
    }
    with Scope(nc, "const") as s:
        filled = s.sems("filled")
        with nc.Block() as block:
            @block.gpsimd
            def _(pool):
                nc.gpsimd.memset(c["mean"][:], 1.0 / P)
                nc.gpsimd.memset(c["ones"][:], 1.0)
                nc.gpsimd.memset(c["eps"][:], LN_EPS)
                nc.gpsimd.memset(c["ident"][:], 0.0)
                nc.gpsimd.memset(c["earlier"][:], 1.0).then_inc(filled, 1)
                pool.wait_ge(filled, 1)
                nc.gpsimd.affine_select(out=c["ident"][:], in_=c["ident"][:], compare_op=ALU.not_equal, fill=1.0,
                                        base=0, pattern=[[-1, P]], channel_multiplier=1)
                nc.gpsimd.affine_select(out=c["earlier"][:], in_=c["earlier"][:], compare_op=ALU.is_gt, fill=0.0,
                                        base=0, pattern=[[1, P]], channel_multiplier=-1).then_inc(filled, 1)
        s.barrier()
    return c


def load(nc, scope, pairs):
    with Scope(nc, scope.name + "_load") as s:
        landed = s.sems("landed")
        with nc.Block() as block:
            @block.sync
            def _(sp):
                for dst, src in pairs:
                    sp.dma_start(dst, src, allow_slow_non_contiguous=True).then_inc(landed, 16)
                sp.wait_ge(landed, 16 * len(pairs))
        s.barrier()


def column(v):
    return v.rearrange("(c p) -> p c", p=min(P, v.shape[0]))


def gate_and_norm(nc, c, x, xn, s=None, g=None, gate=False, norm=True, out=None, affine=None):
    W = BANK
    N = x.shape[1] // W
    NBUF, NPS = 3, 4
    with Scope(nc, "norm") as q:
        if norm:
            sq = q.sb("squares", [P, NBUF, W])
            rs = q.sb("inv_dev", [P, N, W])
            mean = q.banks("mean", NPS)
            var = q.banks("var", NPS)
        gated, mixed, x_new, mean_ready, centered, squared, var_ready, logged, rooted, normed, stored = q.sems(
            "gated mixed x_new mean_ready centered squared var_ready logged rooted normed stored")

        def cols(k):
            return slice(k * W, (k + 1) * W)
        with nc.Block() as block:
            @block.scalar
            def _(act):
                if gate:
                    for k in range(N):
                        nc.scalar.activation(g[:, cols(k)], g[:, cols(k)], ACT.Silu).then_inc(gated, 1)
                if norm:
                    def take_log(k):
                        act.wait_ge(var_ready, k + 1)
                        nc.scalar.activation(rs[:, k, :], var[:, k % NPS, :], ACT.Ln, bias=c["eps"][:]).then_inc(logged, 1)
                    for k in range(N + 1):
                        if k < N:
                            act.wait_ge(centered, k + 1)
                            if k >= NBUF:
                                act.wait_ge(var_ready, k - NBUF + 1)
                            nc.scalar.activation(sq[:, k % NBUF, :], xn[:, cols(k)], ACT.Square).then_inc(squared, 1)
                        if k >= 1:
                            take_log(k - 1)
                    for k in range(N):
                        act.wait_ge(logged, k + 1)
                        nc.scalar.activation(rs[:, k, :], rs[:, k, :], ACT.Exp, scale=-0.5).then_inc(rooted, 1)

            @block.vector
            def _(dve):
                if gate:
                    for k in range(N):
                        dve.wait_ge(gated, k + 1)
                        nc.vector.tensor_tensor(g[:, cols(k)], g[:, cols(k)], s[:, cols(k)], ALU.mult).then_inc(mixed, 1)
                        dve.wait_ge(mixed, k + 1)
                        nc.vector.tensor_tensor(x[:, cols(k)], x[:, cols(k)], g[:, cols(k)], ALU.add).then_inc(x_new, 1)
                if norm:
                    for k in range(N):
                        if gate:
                            dve.wait_ge(x_new, k + 1)
                        dve.wait_ge(mean_ready, k + 1)
                        nc.vector.tensor_tensor(xn[:, cols(k)], x[:, cols(k)], mean[:, k % NPS, :],
                                                ALU.subtract).then_inc(centered, 1)
                    for k in range(N):
                        dve.wait_ge(rooted, k + 1)
                        nc.vector.tensor_tensor(xn[:, cols(k)], xn[:, cols(k)], rs[:, k, :], ALU.mult).then_inc(normed, 1)
                        if affine is not None:
                            dve.wait_ge(normed, k + 1)
                            nc.vector.tensor_scalar(xn[:, cols(k)], xn[:, cols(k)], affine[0], affine[1], ALU.mult,
                                                    ALU.add)

            if norm:
                @block.tensor
                def _(pe):
                    def variance(k):
                        pe.wait_ge(squared, k + 1)
                        if k >= NPS:
                            pe.wait_ge(logged, k - NPS + 1)
                        nc.tensor.matmul(var[:, k % NPS, :], c["mean"][:], sq[:, k % NBUF, :], start=True,
                                         stop=True).then_inc(var_ready, 1)
                    for k in range(N + 1):
                        if k < N:
                            if gate:
                                pe.wait_ge(x_new, k + 1)
                            if k >= NPS:
                                pe.wait_ge(centered, k - NPS + 1)
                            nc.tensor.matmul(mean[:, k % NPS, :], c["mean"][:], x[:, cols(k)], start=True,
                                             stop=True).then_inc(mean_ready, 1)
                        if k >= 1:
                            variance(k - 1)

            if out is not None:
                @block.sync
                def _(sp):
                    for k in range(N):
                        sp.wait_ge(x_new, k + 1)
                        sp.dma_start(out[:, cols(k)], x[:, cols(k)]).then_inc(stored, 16)
                    sp.wait_ge(stored, 16 * N)
        q.barrier()


def load_padded_columns(nc, scope, pairs):
    with Scope(nc, scope.name + "_pad") as s:
        zeroed, landed = s.sems("zeroed landed")
        with nc.Block() as block:
            @block.gpsimd
            def _(pool):
                for i, (dst, _) in enumerate(pairs):
                    nc.gpsimd.memset(dst, 0.0).then_inc(zeroed, 1)

            @block.sync
            def _(sp):
                sp.wait_ge(zeroed, len(pairs))
                for dst, src in pairs:
                    v = src.rearrange("(j g d) -> g d j", j=4, g=4)
                    for g in range(4):
                        sp.dma_start(dst[32 * g:32 * g + 8, :], v[g], allow_slow_non_contiguous=True).then_inc(landed, 16)
                sp.wait_ge(landed, 64 * len(pairs))
        s.barrier()


def pad_heads(nc, dst, src):
    return nc.vector.tensor_copy(dst.rearrange("p j (g e) -> p (j g) e", g=4)[:, :, 0:8],
                                 src.rearrange("p (h d) -> p h d", d=8))


def l0_attention(nc, c, d, xn, s_out):
    WIN, HD = 64, 8
    ROW = 3 * WIN
    SC = 1.0 / float(np.sqrt(HD * 3.0))
    with Scope(nc, "a0") as s:
        names = ["Wq", "Wk", "Wv", "Wo", "Wrk", "Wrq"]
        w = {n: s.sb(n, [P, P]) for n in names}
        wp = {n: s.sb(n + "_padded", [P, 4, P]) for n in ["Wq", "Wk", "Wrk", "Wrq"]}
        vec = s.sb("vectors", [P, 4])
        cols = {n: s.sb(n, [P, 4]) for n in ["bq", "bk", "brk", "brq", "shift_q", "shift_k"]}
        rel = s.sb("relpos", [P, WIN])
        rel2 = s.sb("relpos2", [P, WIN])
        rt = {"k": s.sb("rk", [P, 4, WIN]), "q": s.sb("rq", [P, 4, WIN])}
        rb = {"k": s.sb("rk_blocks", [P, 4, 4, WIN]), "q": s.sb("rq_blocks", [P, 4, 4, WIN])}
        zero = s.sb("zero", [P, 2 * ROW])
        band_rows = nc.dram_tensor("a0_band_rows", (2, H, T, ROW), F32).ap()
        pj = s.banks("project", 4)
        load(nc, s, [(w[n][:], d[n]) for n in names] + [(vec[:, 0:1], column(d["bv"])), (vec[:, 1:2], column(d["bo"])),
             (vec[:, 2:3], column(d["ln_gamma"])), (vec[:, 3:4], column(d["ln_beta"])), (rel[:], d["relpos_tableT"])])
        load_padded_columns(nc, s, [(cols[n][:], d[n]) for n in ["bq", "bk", "brk", "brq"]])
        with Scope(nc, "a0t") as t:
            step, zeroed, table, zeros_out = t.sems("step zeroed table zeros_out")
            mm = t.sems("mm")
            with nc.Block() as block:
                @block.gpsimd
                def _(pool):
                    for n in wp:
                        nc.gpsimd.memset(wp[n][:], 0.0)
                    for n in rb:
                        nc.gpsimd.memset(rb[n][:], 0.0)
                    nc.gpsimd.memset(zero[:], 0.0).then_inc(zeroed, 1)

                @block.sync
                def _(sp):
                    sp.wait_ge(zeroed, 1)
                    for kind in range(2):
                        for h in range(H):
                            sp.dma_start(band_rows[kind, h].rearrange("(p r) e -> p (r e)", p=P),
                                         zero[:]).then_inc(zeros_out, 16)
                    sp.wait_ge(zeros_out, 16 * 2 * H)

                @block.tensor
                def _(pe):
                    nc.tensor.matmul(pj[:, 0, 0:WIN], c["mean"][:], rel[:], start=True, stop=True).then_inc(mm, 1)
                    pe.wait_ge(table, 1)
                    nc.tensor.matmul(pj[:, 1, 0:WIN], c["mean"][:], rel2[:], start=True, stop=True).then_inc(mm, 1)
                    pe.wait_ge(table, 2)
                    for n, (a, wn) in enumerate((("k", "Wrk"), ("q", "Wrq"))):
                        for j in range(4):
                            nc.tensor.matmul(pj[:, 2 + n, j * WIN:(j + 1) * WIN], wp[wn][:, j, :], rel[:],
                                             start=True, stop=True).then_inc(mm, 1)

                @block.scalar
                def _(act):
                    act.wait_ge(mm, 2)
                    nc.scalar.activation(rel2[:], pj[:, 1, 0:WIN], ACT.Sqrt, bias=c["eps"][:]).then_inc(zeroed, 1)

                @block.vector
                def _(dve):
                    link = Link(dve, step)
                    dve.wait_ge(zeroed, 1)
                    for n in wp:
                        pad_heads(nc, wp[n][:], w[n][:])
                    dve.wait_ge(mm, 1)
                    link(nc.vector.tensor_tensor(rel[:], rel[:], pj[:, 0, 0:WIN], ALU.subtract))
                    nc.vector.tensor_tensor(rel2[:], rel[:], rel[:], ALU.mult).then_inc(table, 1)
                    dve.wait_ge(zeroed, 2)
                    link(nc.vector.reciprocal(rel2[:], rel2[:]))
                    link(nc.vector.tensor_tensor(rel[:], rel[:], rel2[:], ALU.mult))
                    nc.vector.tensor_scalar(rel[:], rel[:], vec[:, 2:3], vec[:, 3:4], ALU.mult,
                                            ALU.add).then_inc(table, 1)
                    dve.wait_ge(mm, 10)
                    for n, (a, bias, sum_) in enumerate((("k", "brk", "shift_k"), ("q", "brq", "shift_q"))):
                        tab = pj[:, 2 + n, 0:4 * WIN].rearrange("p (j w) -> p j w", j=4)
                        link(nc.vector.tensor_copy(rt[a][:], tab))
                        link(nc.vector.tensor_tensor(cols[sum_][:], cols[bias][:], rt[a][:, :, 0], ALU.add))
                        for g in range(4):
                            r = slice(32 * g, 32 * g + 32)
                            e = rt[a][r, :, :]
                            if a == "q":
                                e = e[:, :, ::-1]
                            link(nc.vector.tensor_tensor(rb[a][r, :, g, :], e,
                                                         rt[a][r, :, 0:1].broadcast_to([32, 4, WIN]), ALU.subtract))
            t.barrier()

        tile_x = s.sb("x", [P, T])
        qT, kT, qA, kA = (s.sb(n, [P, 4, T]) for n in ["qT", "kT", "qA", "kA"])
        v = s.sb("v", [P, 2, P])
        band = s.sb("band", [P, 4, H * WIN])
        A = [s.sb("A0", [P, H, P]), s.sb("A1", [P, H, T])]
        B = [s.sb("B0", [P, H, ROW]), s.sb("B1", [P, H, P])]
        NL, NP_, NT = 3, 3, 3
        lg = s.sb("logits", [P, NL, T])
        pr = s.sb("probs", [P, NP_, T])
        pt = s.sb("probs_T", [P, NT, T])
        nmax = s.sb("neg_max", [P, 2 * H])
        rsum = s.sb("row_sum", [P, 2 * H])
        rinv = s.sb("row_inv", [P, 2 * H])
        on = s.sb("o_normed", [P, 2, P])
        oT = s.sb("oT", [P, T])
        ob = s.banks("out", 2)
        fin = s.banks("final", 1)
        (copied, q_mm, k_mm, q_ready, k_ready, shifted, v_mm, v_ready, band_mm, band_lo, band_hi, qb_out, kb_out, a_in, b_in, masked, logit_mm, logits,
         probs, tr_mm, tr_sb, pv_mm, inv, normed, oT_mm, oT_sb, wo_mm) = s.sems(
            "copied q_mm k_mm q_ready k_ready shifted v_mm v_ready band_mm band_lo band_hi qb_out kb_out a_in b_in masked logit_mm logits probs tr_mm "
            "tr_sb pv_mm inv normed oT_mm oT_sb wo_mm")
        units = [(h, t) for t in range(2) for h in range(H)]
        NU = len(units)

        with nc.Block() as block:
            @block.gpsimd
            def _(pool):
                nc.gpsimd.memset(A[1][:], 0.0)
        s.barrier()
        with nc.Fori(0, xn.shape[1] // T) as b:
            with nc.Block() as block:
                def evac(eng, u):
                    h, t = units[u]
                    nk = P * (t + 1)
                    eng.wait_ge(tr_mm, u + 1)
                    if u >= NT:
                        eng.wait_ge(pv_mm, u - NT + 1)
                    eng.wait_ge(tr_sb, u)
                    if u % 2:
                        ins = nc.scalar.activation(pt[:, u % NT, 0:nk], pj[:, 2 + u % 2, 0:nk], ACT.Copy)
                    else:
                        ins = nc.vector.tensor_copy(pt[:, u % NT, 0:nk], pj[:, 2 + u % 2, 0:nk])
                    ins.then_inc(tr_sb, 1)

                @block.tensor
                def _(pe):
                    for kind, n in enumerate(["Wq", "Wk"]):
                        for j in range(4):
                            nc.tensor.matmul(pj[:, 2 * kind + j // 2, (j % 2) * T:(j % 2 + 1) * T], wp[n][:, j, :],
                                             xn[:, tokens(b)], start=True, stop=True).then_inc((q_mm, k_mm)[kind], 1)
                    pe.wait_ge(copied, 1)
                    for t in range(2):
                        nc.tensor.matmul(fin[:, 0, t * P:(t + 1) * P], tile_x[:, t * P:(t + 1) * P], w["Wv"][:],
                                         start=True, stop=True).then_inc(v_mm, 1)
                    for n, (kind, t) in enumerate([(0, 0), (0, 1), (1, 0), (1, 1)]):
                        src, tab = (qT, rb["k"]) if kind == 0 else (kT, rb["q"])
                        pe.wait_ge((q_ready, k_ready)[kind], 4)
                        if n == 0:
                            pe.wait_ge(k_ready, 4)
                        if n >= 2:
                            pe.wait_ge(band_lo, n - 1)
                            pe.wait_ge(band_hi, n - 1)
                        for j in range(4):
                            nc.tensor.matmul(pj[:, 2 * (n % 2) + j // 2, (j % 2) * T:(j % 2 + 1) * T],
                                             src[:, j, t * P:(t + 1) * P], tab[:, j].rearrange("p g w -> p (g w)"),
                                             start=True, stop=True).then_inc(band_mm, 1)
                    pe.wait_ge(band_lo, 4)
                    pe.wait_ge(band_hi, 4)

                    def logit(u):
                        h, t = units[u]
                        r, j = slice(32 * (h % 4), 32 * (h % 4) + 32), h // 4
                        nk = P * (t + 1)
                        if u >= 2:
                            pe.wait_ge(logits, u - 1)
                        dst = pj[:, u % 2, :]
                        nc.tensor.matmul(dst[:, 0:nk], qA[r, j, t * P:(t + 1) * P], kA[r, j, 0:nk], start=True,
                                         stop=False, tile_position=(32 * (h % 4), 0))
                        if t == 1:
                            nc.tensor.matmul(dst[0:64, 0:P], B[0][:, h, P:P + 64], c["ident"][:], start=False, stop=False)
                        nc.tensor.matmul(dst[:, t * P:nk], B[t][:, h, 0:P], c["ident"][:], start=False,
                                         stop=True).then_inc(logit_mm, 1)

                    def transpose(u):
                        h, t = units[u]
                        pe.wait_ge(probs, u + 1)
                        if u >= 2:
                            pe.wait_ge(tr_sb, u - 1)
                        for kt in range(t + 1):
                            ins = nc.tensor.transpose(pj[:, 2 + u % 2, kt * P:(kt + 1) * P],
                                                      pr[:, u % NP_, kt * P:(kt + 1) * P], c["ident"][:])
                        ins.then_inc(tr_mm, 1)

                    def weigh(u):
                        h, t = units[u]
                        pe.wait_ge(tr_sb, u + 1)
                        for kt in range(t + 1):
                            ins = nc.tensor.matmul(ob[:, t, 8 * h:8 * h + 8],
                                                   pt[:, u % NT, kt * P:(kt + 1) * P], v[:, kt, 8 * h:8 * h + 8],
                                                   start=kt == 0, stop=kt == t)
                        ins.then_inc(pv_mm, 1)

                    pe.wait_ge(b_in, 32)
                    pe.wait_ge(v_ready, 1)
                    pe.wait_ge(shifted, 8)
                    for u in range(NU + 3):
                        if u < NU:
                            logit(u)
                        if 2 <= u < NU + 2:
                            transpose(u - 2)
                        if 3 <= u:
                            weigh(u - 3)
                    for t in range(2):
                        pe.wait_ge(normed, t + 1)
                        nc.tensor.transpose(fin[:, 0, t * P:(t + 1) * P], on[:, t, :], c["ident"][:]).then_inc(oT_mm, 1)
                    pe.wait_ge(oT_sb, 1)
                    nc.tensor.matmul(fin[:, 0, T:2 * T], w["Wo"][:], oT[:], start=True, stop=True).then_inc(wo_mm, 1)

                @block.scalar
                def _(act):
                    nc.scalar.activation(tile_x[:], xn[:, tokens(b)], ACT.Copy).then_inc(copied, 1)
                    for j in range(4):
                        act.wait_ge(q_mm, 2 * (j // 2) + 2)
                        nc.scalar.activation(qT[:, j, :], pj[:, j // 2, (j % 2) * T:(j % 2 + 1) * T],
                                             ACT.Identity, bias=cols["bq"][:, j:j + 1]).then_inc(q_ready, 1)
                    act.wait_ge(v_mm, 2)
                    nc.scalar.activation(v[:].rearrange("p t e -> p (t e)"), fin[:, 0, 0:T], ACT.Copy).then_inc(v_ready, 1)
                    for n in range(4):
                        act.wait_ge(band_mm, 4 * n + 2)
                        nc.scalar.activation(band[:, n, 0:BANK], pj[:, 2 * (n % 2), :], ACT.Copy).then_inc(band_lo, 1)
                    for u in range(NU):
                        h, t = units[u]
                        nk = P * (t + 1)
                        act.wait_ge(logits, u + 1)
                        if u >= NP_:
                            act.wait_ge(tr_mm, u - NP_ + 1)
                        nc.scalar.activation(pr[:, u % NP_, 0:nk], lg[:, u % NL, 0:nk], ACT.Exp, scale=-1.0,
                                             bias=nmax[:, u:u + 1], accum_out=rsum[:, u:u + 1]).then_inc(probs, 1)
                        if u >= 1 and u % 2 == 0:
                            evac(act, u - 1)
                    evac(act, NU - 1)
                    act.wait_ge(oT_mm, 2)
                    nc.scalar.activation(oT[:], fin[:, 0, 0:T], ACT.Identity, bias=vec[:, 0:1]).then_inc(oT_sb, 1)
                    act.wait_ge(wo_mm, 1)
                    nc.scalar.activation(s_out[:, tokens(b)], fin[:, 0, T:2 * T], ACT.Identity, bias=vec[:, 1:2])

                @block.vector
                def _(dve):
                    for j in range(4):
                        dve.wait_ge(k_mm, 2 * (j // 2) + 2)
                        nc.vector.tensor_scalar(kT[:, j, :], pj[:, 2 + j // 2, (j % 2) * T:(j % 2 + 1) * T],
                                                cols["bk"][:, j:j + 1], None, ALU.add).then_inc(k_ready, 1)
                    for n in range(4):
                        dve.wait_ge(band_mm, 4 * n + 4)
                        nc.vector.tensor_copy(band[:, n, BANK:], pj[:, 2 * (n % 2) + 1, :]).then_inc(band_hi, 1)
                    for u in range(NU + 2):
                        if u < NU:
                            h, t = units[u]
                            nk = P * (t + 1)
                            dve.wait_ge(logit_mm, u + 1)
                            dve.wait_ge(masked, t + 1)
                            if u >= NL:
                                dve.wait_ge(probs, u - NL + 1)
                            nc.vector.tensor_tensor_reduce(out=lg[:, u % NL, 0:nk], in0=pj[:, u % 2, 0:nk],
                                                           in1=A[t][:, h, :], scale=-SC, scalar=3e38, op0=ALU.add,
                                                           op1=ALU.min, accum_out=nmax[:, u:u + 1]).then_inc(logits, 1)
                        if u >= 2 and (u - 2) % 2 == 0:
                            evac(dve, u - 2)
                    for t in range(2):
                        dve.wait_ge(probs, H * (t + 1))
                        nc.vector.reciprocal(rinv[:, H * t:H * (t + 1)], rsum[:, H * t:H * (t + 1)]).then_inc(inv, 1)
                        dve.wait_ge(inv, t + 1)
                        dve.wait_ge(pv_mm, H * (t + 1))
                        nc.vector.tensor_tensor(on[:, t, :].rearrange("p (h e) -> p h e", h=H),
                                                ob[:, t, 0:P].rearrange("p (h e) -> p h e", h=H),
                                                rinv[:, H * t:H * (t + 1)].unsqueeze(2).broadcast_to([P, H, 8]),
                                                ALU.mult).then_inc(normed, 1)

                @block.sync
                def _(sp):
                    for n, (kind, t) in enumerate([(0, 0), (0, 1), (1, 0), (1, 1)]):
                        sp.wait_ge(band_lo, n + 1)
                        sp.wait_ge(band_hi, n + 1)
                        sp.dma_start(band_rows[kind, :, t * P:(t + 1) * P, 0:WIN].rearrange("h p w -> p h w"),
                                     band[:, n, :].rearrange("p (h w) -> p h w", h=H)).then_inc((qb_out, kb_out)[kind], 16)

                    def skewed(kind, tile, first, n):
                        v0 = band_rows[kind]
                        return bass.AP(tensor=v0.tensor, offset=v0.offset + (ROW - 1) * P * tile + first,
                                       ap=[[ROW - 1, P], [T * ROW, H], [1, n]])
                    sp.wait_ge(qb_out, 32)
                    sp.dma_start(A[0][:], skewed(0, 0, WIN - 1, P)).then_inc(a_in, 16)
                    sp.dma_start(A[1][:, :, 64:], skewed(0, 1, 64 + WIN - 1, ROW)).then_inc(a_in, 16)
                    sp.wait_ge(kb_out, 32)
                    sp.dma_start(B[0][:], skewed(1, 0, 0, ROW)).then_inc(b_in, 16)
                    sp.dma_start(B[1][:], skewed(1, 1, P, P)).then_inc(b_in, 16)

                @block.gpsimd
                def _(pool):
                    for j in range(4):
                        for dst, src, n, ready in ((qA, qT, "shift_q", q_ready), (kA, kT, "shift_k", k_ready)):
                            pool.wait_ge(ready, j + 1)
                            nc.gpsimd.tensor_scalar(dst[:, j, :], src[:, j, :], cols[n][:, j:j + 1], None,
                                                    ALU.add).then_inc(shifted, 1)
                    pool.wait_ge(a_in, 32)
                    for t in range(2):
                        part = A[t][:, :, t * P:(t + 1) * P]
                        nc.gpsimd.affine_select(out=part, in_=part, compare_op=ALU.is_ge, fill=MASKED, base=0,
                                                pattern=[[0, H], [-1, P]], channel_multiplier=1).then_inc(masked, 1)
            s.barrier()


def l0_ffn(nc, c, d, xn, g_out):
    F, ST = 512, 9
    NF = F // P
    with Scope(nc, "f0") as s:
        up = s.sb("up", [P, F])
        dn = s.sb("dn", [P, F])
        upb = s.sb("up_bias", [1, F])
        one = s.sb("one", [1, 1])
        wc = s.sb("W_con", [P, NF, P])
        down = s.sb("down", [P, NF, P])
        bias_up = s.sb("bias_up", [P, NF])
        bias_out = s.sb("bias_out", [P, 2])
        bo = s.sb("bo", [P, 1])
        load(nc, s, [(up[:], d["W_exp"]), (upb[:], d["b_exp"].rearrange("(a n) -> a n", a=1)),
                     (wc[:], d["W_con"].rearrange("(c p) n -> p c n", p=P)), (bias_up[:], column(d["up_bias"])),
                     (bias_out[:, 0:1], column(d["b_con"])), (bias_out[:, 1:2], column(d["down_bias"]))])
        with Scope(nc, "f0t") as t:
            ps = t.banks("ps")
            turned, kept = t.sems("turned kept")
            with nc.Block() as block:
                @block.tensor
                def _(pe):
                    for i in range(NF):
                        nc.tensor.transpose(ps[:, 0, i * P:(i + 1) * P], wc[:, i, :], c["ident"][:]).then_inc(turned, 1)

                @block.vector
                def _(dve):
                    nc.vector.memset(one[:], 1.0)
                    nc.vector.tensor_tensor(bo[:], bias_out[:, 0:1], bias_out[:, 1:2], ALU.add)
                    dve.wait_ge(turned, NF)
                    nc.vector.tensor_copy(dn[:], ps[:, 0, :]).then_inc(kept, 1)
            t.barrier()
        with Scope(nc, "f0b") as t:
            wt = t.sb("stage_w", [P, 2, 2, 2 * F])
            tmp = t.sb("tmp", [P, 2, F])
            alt = t.sb("alt", [P, 2, F])
            btmp = t.sb("btmp", [1, F])
            balt = t.sb("balt", [1, F])
            w_in0, w_in1, stage_done, bstage_done, step, bstep = t.sems("w_in0 w_in1 stage_done bstage_done step bstep")
            w_in = [w_in0, w_in1]
            with nc.Block() as block:
                @block.sync
                def _(sp):
                    for i in range(ST):
                        if i >= 2:
                            sp.wait_ge(stage_done, i - 1)
                            sp.wait_ge(bstage_done, i - 1)
                        for k, (name, st) in enumerate((("up_weights", i), ("down_weights", ST - 1 - i))):
                            sp.dma_start(wt[:, i % 2, k, :], d[name][st].rearrange("k r c -> (k r c)").unsqueeze(0)
                                         .broadcast_to([P, 2 * F])).then_inc(w_in[i % 2], 16)

                def stage(eng, link, i, k, src, dst, tm, st, flip):
                    rows = src.shape[0]
                    n, nb = 2 ** st, F // (2 * 2 ** st)
                    y = src.rearrange("p (m r n) -> p m r n", r=2, n=n)
                    o = dst.rearrange("p (m r n) -> p m r n", r=2, n=n)
                    w = wt[0:rows, i % 2, k, :].rearrange("p (m n r c) -> p m n r c", m=nb, n=n, r=2, c=2)
                    m = tm.rearrange("p (m r n) -> p m r n", r=2, n=n)

                    def wgt(r, cc):
                        return w[:, :, :, cc, r] if flip else w[:, :, :, r, cc]
                    for r in range(2):
                        link(eng.tensor_tensor(m[:, :, r, :], wgt(r, 1), y[:, :, 1, :], ALU.mult))
                        link(eng.tensor_tensor(o[:, :, r, :], wgt(r, 0), y[:, :, 0, :], ALU.mult))
                        link(eng.tensor_tensor(o[:, :, r, :], o[:, :, r, :], m[:, :, r, :], ALU.add))

                @block.vector
                def _(dve):
                    link = Link(dve, step)
                    bufs = [[up[:], alt[:, 0, :]], [dn[:], alt[:, 1, :]]]
                    for i in range(ST):
                        dve.wait_ge(w_in[i % 2], 32 * (i // 2 + 1))
                        for k, st in enumerate((i, ST - 1 - i)):
                            stage(nc.vector, link, i, k, bufs[k][i % 2], bufs[k][1 - i % 2], tmp[:, k, :], st, k == 1)
                        nc.vector.engine_nop().then_inc(stage_done, 1)
                    for k in range(2):
                        link(nc.vector.tensor_copy(bufs[k][0], bufs[k][1]))

                @block.gpsimd
                def _(pool):
                    link = Link(pool, bstep)
                    bufs = [upb[:], balt[:]]
                    for i in range(ST):
                        pool.wait_ge(w_in[i % 2], 32 * (i // 2 + 1))
                        stage(nc.gpsimd, link, i, 0, bufs[i % 2], bufs[1 - i % 2], btmp[:], i, False)
                        nc.gpsimd.engine_nop().then_inc(bstage_done, 1)
                    link(nc.gpsimd.tensor_copy(upb[:], balt[:]))
            t.barrier()
        with Scope(nc, "f0c") as t:
            ps = t.banks("ps", 2)
            turned, kept = t.sems("turned kept")
            with nc.Block() as block:
                @block.tensor
                def _(pe):
                    for i in range(NF):
                        nc.tensor.transpose(ps[:, 0, i * P:(i + 1) * P], dn[:, i * P:(i + 1) * P],
                                            c["ident"][:]).then_inc(turned, 1)
                        nc.tensor.matmul(ps[:, 1, i:i + 1], upb[:, i * P:(i + 1) * P], one[:], start=True,
                                         stop=True).then_inc(turned, 1)

                @block.vector
                def _(dve):
                    dve.wait_ge(turned, 2 * NF)
                    nc.vector.tensor_copy(down[:].rearrange("p c n -> p (c n)"), ps[:, 0, :]).then_inc(kept, 1)
                    nc.vector.tensor_tensor(bias_up[:], bias_up[:], ps[:, 1, 0:NF], ALU.add).then_inc(kept, 1)
            t.barrier()

        W = BANK
        hid = s.sb("hidden", [P, 2, NF, W])
        hp = s.banks("hidden_ps", NF)
        yp = s.banks("y", 2)
        up_mm, acted, y_mm, y_out = s.sems("up_mm acted y_mm y_out")
        PER = 2
        with nc.Fori(0, xn.shape[1] // (W * PER) or 1) as i:
            per = min(PER, xn.shape[1] // W)
            with nc.Block() as block:
                def cols(k):
                    return bass.ds((i * PER + k) * W, W)

                @block.tensor
                def _(pe):
                    def raise_(k):
                        for f in range(NF):
                            if k:
                                pe.wait_ge(acted, NF * (k - 1) + f + 1)
                            nc.tensor.matmul(hp[:, f, :], up[:, f * P:(f + 1) * P], xn[:, cols(k)], start=True,
                                             stop=True).then_inc(up_mm, 1)

                    def lower(k):
                        for f in range(NF):
                            pe.wait_ge(acted, NF * k + f + 1)
                            ins = nc.tensor.matmul(yp[:, k % 2, :], down[:, f, :], hid[:, k % 2, f, :], start=f == 0,
                                                   stop=f == NF - 1)
                        ins.then_inc(y_mm, 1)
                    raise_(0)
                    for k in range(per):
                        if k + 1 < per:
                            raise_(k + 1)
                        lower(k)

                @block.scalar
                def _(act):
                    for k in range(per):
                        for f in range(NF):
                            act.wait_ge(up_mm, NF * k + f + 1)
                            nc.scalar.activation(hid[:, k % 2, f, :], hp[:, f, :], ACT.Gelu,
                                                 bias=bias_up[:, f:f + 1]).then_inc(acted, 1)

                @block.vector
                def _(dve):
                    for k in range(per):
                        dve.wait_ge(y_mm, k + 1)
                        nc.vector.tensor_scalar(g_out[:, cols(k)], yp[:, k % 2, :], bo[:], None,
                                                ALU.add).then_inc(y_out, 1)
            s.barrier()


def l1_attention(nc, c, d, xn, s_out):
    with Scope(nc, "a1") as s:
        w = {n: s.sb(n, [P, P]) for n in ["W_q", "W_k", "W_v"]}
        load(nc, s, [(w[n][:], d[n + "T"]) for n in w])
        kq = s.sb("kq", [P, 2 * T])
        sq = s.sb("squares", [P, 2 * T])
        nrm = s.sb("norms", [P, 2 * T])
        inv = s.sb("inv_norms", [P, 2 * T])
        kn = s.sb("k_normed", [P, T])
        qn = s.sb("q_normed", [P, T])
        kv = s.sb("kv", [P, T])
        feat = s.sb("feature", [P, 2])
        ps = s.banks("kq", 1)
        vs = s.banks("v", 1)
        ss = s.banks("sum_squares", 1)
        kq_mm, v_mm, kq_sb, squared, ss_mm, rooted, step, inverted, k_normed, q_normed, summed = s.sems(
            "kq_mm v_mm kq_sb squared ss_mm rooted step inverted k_normed q_normed summed")
        with nc.Fori(0, xn.shape[1] // T) as b:
            with nc.Block() as block:
                @block.tensor
                def _(pe):
                    for n, name in enumerate(["W_k", "W_q"]):
                        nc.tensor.matmul(ps[:, 0, n * T:(n + 1) * T], w[name][:], xn[:, tokens(b)], start=True,
                                         stop=True).then_inc(kq_mm, 1)
                    nc.tensor.matmul(vs[:, 0, 0:T], w["W_v"][:], xn[:, tokens(b)], start=True, stop=True).then_inc(v_mm, 1)
                    pe.wait_ge(squared, 1)
                    nc.tensor.matmul(ss[:, 0, :], c["ones"][:], sq[:], start=True, stop=True).then_inc(ss_mm, 1)

                @block.scalar
                def _(act):
                    act.wait_ge(kq_mm, 2)
                    nc.scalar.activation(kq[:], ps[:, 0, :], ACT.Copy).then_inc(kq_sb, 1)
                    nc.scalar.activation(sq[:], ps[:, 0, :], ACT.Square).then_inc(squared, 1)
                    act.wait_ge(ss_mm, 1)
                    nc.scalar.activation(nrm[:], ss[:, 0, :], ACT.Sqrt).then_inc(rooted, 1)

                @block.vector
                def _(dve):
                    dve.wait_ge(rooted, 1)
                    link = Link(dve, step)
                    link(nc.vector.tensor_scalar(nrm[:], nrm[:], 1e-12, None, ALU.max))
                    nc.vector.reciprocal(inv[:, 0:T], nrm[:, 0:T]).then_inc(inverted, 1)
                    nc.vector.reciprocal(inv[:, T:], nrm[:, T:]).then_inc(inverted, 1)
                    dve.wait_ge(k_normed, 1)
                    dve.wait_ge(v_mm, 1)
                    nc.vector.tensor_tensor_reduce(out=kv[:], in0=vs[:, 0, 0:T], in1=kn[:], scale=1.0, scalar=0.0,
                                                   op0=ALU.mult, op1=ALU.add, accum_out=feat[:, 0:1]).then_inc(summed, 1)
                    dve.wait_ge(summed, 1)
                    dve.wait_ge(q_normed, 1)
                    nc.vector.tensor_scalar(s_out[:, tokens(b)], qn[:], feat[:, 0:1], 1.0 / T, ALU.mult, ALU.mult)

                @block.gpsimd
                def _(pool):
                    pool.wait_ge(kq_sb, 1)
                    pool.wait_ge(inverted, 1)
                    nc.gpsimd.tensor_tensor(kn[:], kq[:, 0:T], inv[:, 0:T], ALU.mult).then_inc(k_normed, 1)
                    pool.wait_ge(inverted, 2)
                    nc.gpsimd.tensor_tensor(qn[:], kq[:, T:], inv[:, T:], ALU.mult).then_inc(q_normed, 1)
            s.barrier()


def l1_ffn(nc, c, d, xn, g_out):
    SL, DQ, K = 64, 32, 2
    with Scope(nc, "f1") as s:
        w1 = s.sb("w1", [P, 2, SL])
        w2 = s.sb("w2", [SL, SL])
        slot = s.sb("slotT", [P, SL])
        wih = s.sb("WihT", [P, 3, P])
        whh = s.sb("WhhT", [P, 3, P])
        bih = s.sb("bih", [P, 3])
        bhh = s.sb("bhh", [P, 3])
        wqk = s.sb("wqk", [P, 2, DQ])
        bqk = s.sb("bqk", [DQ, 2])
        wv, wvp, wo = s.sb("wv", [P, P]), s.sb("wvp", [P, P]), s.sb("wo", [P, P])
        vec = s.sb("vectors", [P, 5])
        b1 = s.sb("b1", [SL, 1])
        b2 = s.sb("b2", [1, SL])
        tau = s.sb("tau", [P, 1])
        ntau = s.sb("neg_tau", [P, 1])
        load(nc, s, [(w1[:], d["w1"].rearrange("(a p) n -> p a n", p=P)), (w2[:], d["w2"]), (slot[:], d["slot_initT"]),
                     (wih[:].rearrange("p a n -> p (a n)"), d["WihT"]), (whh[:].rearrange("p a n -> p (a n)"), d["WhhT"]),
                     (bih[:], column(d["bih"])), (bhh[:], column(d["bhh"])), (wqk[:, 0, :], d["wq"]),
                     (wqk[:, 1, :], d["wk"]), (bqk[:, 0:1], d["bq"].rearrange("(p a) -> p a", a=1)),
                     (bqk[:, 1:2], d["bk"].rearrange("(p a) -> p a", a=1)), (wv[:], d["wv"]), (wvp[:], d["wvp"]),
                     (wo[:], d["wo"]), (b1[:], d["b1"].rearrange("(p a) -> p a", a=1)),
                     (b2[:], d["b2"].rearrange("(a n) -> a n", a=1)),
                     (tau[:], d["tau"].unsqueeze(0).broadcast_to([P, 1]))]
             + [(vec[:, i:i + 1], column(d[n])) for i, n in enumerate(["bv", "ln_g", "ln_b", "bvp", "bo"])])
        smean = s.sb("slot_mean", [P, 1])
        hbias = s.sb("hidden_bias", [SL, 1])
        gh = s.sb("ghT", [P, 3, SL])
        with Scope(nc, "f1t") as t:
            ps = t.banks("ps", 2)
            meaned, mm, step = t.sems("meaned mm step")
            with nc.Block() as block:
                @block.tensor
                def _(pe):
                    for i in range(3):
                        nc.tensor.matmul(ps[:, 0, i * SL:(i + 1) * SL], whh[:, i, :], slot[:], start=True,
                                         stop=True).then_inc(mm, 1)
                    pe.wait_ge(meaned, 1)
                    nc.tensor.matmul(ps[0:SL, 1, 0:1], w1[:, 1, :], smean[:], start=True, stop=True).then_inc(mm, 1)

                @block.vector
                def _(dve):
                    link = Link(dve, step)
                    link(nc.vector.reduce_sum(smean[:], slot[:], axis=AX_X))
                    nc.vector.tensor_scalar(smean[:], smean[:], 1.0 / SL, None, ALU.mult).then_inc(meaned, 1)
                    link(nc.vector.tensor_scalar(ntau[:], tau[:], -1.0, None, ALU.mult))
                    link(nc.vector.tensor_tensor(tau[:], tau[:], ntau[:], ALU.max))
                    link(nc.vector.tensor_scalar(tau[:], tau[:], 0.1, None, ALU.add))
                    link(nc.vector.reciprocal(tau[:], tau[:]))
                    link(nc.vector.tensor_tensor(bhh[:, 0:2], bhh[:, 0:2], bih[:, 0:2], ALU.add))
                    dve.wait_ge(mm, 4)
                    link(nc.vector.tensor_tensor(gh[:], ps[:, 0, 0:3 * SL].rearrange("p (a n) -> p a n", a=3),
                                                 bhh[:].unsqueeze(2).broadcast_to([P, 3, SL]), ALU.add))
                    link(nc.vector.tensor_tensor(hbias[:], ps[0:SL, 1, 0:1], b1[:], ALU.add))
            t.barrier()

        def each(name, shape):
            return [s.sb(f"{name}{k}", shape) for k in range(K)]
        tx, hT, xt, lg, rep, m8 = each("x", [P, T]), each("hidden", [SL, T]), each("x_tok", [P, 2, P]), each(
            "route", [P, 2, SL]), each("replaced", [P, 2, SL]), each("top8", [P, 2, 8])
        ex, al, asum, ainv, alT = each("exps", [P, 2, SL]), each("alpha", [P, 2, SL]), each("alpha_sum", [P, 2]), each(
            "alpha_inv", [P, 2]), each("alphaT", [SL, T])
        nm = each("neg_max", [P, 2])
        den, si, ga, rz, u, nn, zs, sn = each("denom", [P, SL]), each("slot_in", [P, SL]), each("gates_in", [P, 2, SL]), \
            each("gates", [P, 2, SL]), each("r_hn", [P, SL]), each("cell", [P, SL]), each("z_part", [P, SL]), each(
            "slots_new", [P, SL])
        qk, v, amax, ae, asm, ai, aT = each("qk", [DQ, 2, SL]), each("v", [SL, P]), each("att_max", [SL, 1]), each(
            "att_exp", [SL, SL]), each("att_sum", [SL, 1]), each("att_inv", [SL, 1]), each("attT", [SL, SL])
        y, yc, ysq, yrs, sv, oT = each("y", [P, SL]), each("y_centered", [P, SL]), each("y_sq", [P, SL]), each(
            "y_inv_dev", [P, SL]), each("slot_values", [SL, P]), each("outT", [P, T])
        bk = [s.banks(f"k{k}", 4) for k in range(K)]
        A, B, C, D = ([bk[k][:, i, :] for k in range(K)] for i in range(4))
        (copied, h_mm, h_act, xt_mm, xt_sb, lg_mm, step, negated, topped, exped, alphaed, si_mm, si_sb, gi_mm, gates_in,
         gates, u_ready, cell, s_new, qk_mm, v_mm, qk_sb, v_sb, att_mm, att_max, att_exp, att_norm, aT_mm, aT_sb,
         comm_mm, y_ready, mean_mm, centered, squared, var_mm, logged, rooted, y_norm, sv_mm, sv_sb, alT_mm, alT_sb,
         out_mm, out_sb, wo_mm) = s.sems(
            "copied h_mm h_act xt_mm xt_sb lg_mm step negated topped exped alphaed si_mm si_sb gi_mm gates_in "
            "gates u_ready cell s_new qk_mm v_mm qk_sb v_sb att_mm att_max att_exp att_norm aT_mm aT_sb "
            "comm_mm y_ready mean_mm centered squared var_mm logged rooted y_norm sv_mm sv_sb alT_mm alT_sb "
            "out_mm out_sb wo_mm")
        ident = c["ident"]
        with nc.Fori(0, xn.shape[1] // (T * K)) as b:
            with nc.Block() as block:
                def seq(k):
                    return bass.ds((b * K + k) * T, T)

                @block.tensor
                def _(pe):
                    mm = nc.tensor.matmul
                    for k in range(K):
                        mm(A[k][0:SL, 0:T], w1[:, 0, :], xn[:, seq(k)], start=True, stop=True).then_inc(h_mm, 1)
                    for k in range(K):
                        pe.wait_ge(copied, k + 1)
                        for t in range(2):
                            ins = nc.tensor.transpose(B[k][:, t * P:(t + 1) * P], tx[k][:, t * P:(t + 1) * P], ident[:])
                        ins.then_inc(xt_mm, 1)
                    for k in range(K):
                        pe.wait_ge(h_act, k + 1)
                        for t in range(2):
                            o = A[k][:, T + t * SL:T + (t + 1) * SL]
                            mm(o, hT[k][:, t * P:(t + 1) * P], w2[:], start=True, stop=False)
                            ins = mm(o, c["ones"][0:1, :], b2[:], start=False, stop=True)
                        ins.then_inc(lg_mm, 1)
                    for k in range(K):
                        pe.wait_ge(alphaed, 2 * k + 2)
                        pe.wait_ge(xt_sb, k + 1)
                        for t in range(2):
                            mm(C[k][:, 0:SL], xt[k][:, t, :], al[k][:, t, :], start=t == 0, stop=t == 1)
                        for t in range(2):
                            ins = mm(C[k][:, SL:2 * SL], c["ones"][:], al[k][:, t, :], start=t == 0, stop=t == 1)
                        ins.then_inc(si_mm, 1)
                    for k in range(K):
                        for t in range(2):
                            ins = nc.tensor.transpose(B[k][0:SL, t * P:(t + 1) * P], al[k][:, t, :], ident[:])
                        ins.then_inc(alT_mm, 1)
                    for k in range(K):
                        pe.wait_ge(si_sb, k + 1)
                        for i in range(3):
                            ins = mm(C[k][:, (2 + i) * SL:(3 + i) * SL], wih[:, i, :], si[k][:], start=True, stop=True)
                        ins.then_inc(gi_mm, 1)
                    for k in range(K):
                        pe.wait_ge(s_new, k + 1)
                        for i in range(2):
                            ins = mm(A[k][0:DQ, i * SL:(i + 1) * SL], wqk[:, i, :], sn[k][:], start=True, stop=True)
                        ins.then_inc(qk_mm, 1)
                        mm(D[k][0:SL, 0:P], sn[k][:], wv[:], start=True, stop=True).then_inc(v_mm, 1)
                    for k in range(K):
                        pe.wait_ge(qk_sb, k + 1)
                        mm(A[k][0:SL, 0:SL], qk[k][:, 0, :], qk[k][:, 1, :], start=True, stop=True).then_inc(att_mm, 1)
                    for k in range(K):
                        pe.wait_ge(att_norm, k + 1)
                        nc.tensor.transpose(A[k][0:SL, SL:2 * SL], ae[k][:], ident[0:SL, 0:SL]).then_inc(aT_mm, 1)
                    for k in range(K):
                        pe.wait_ge(aT_sb, k + 1)
                        pe.wait_ge(v_sb, k + 1)
                        mm(C[k][:, 0:SL], v[k][:], aT[k][:], start=True, stop=True).then_inc(comm_mm, 1)
                    for k in range(K):
                        pe.wait_ge(y_ready, k + 1)
                        mm(A[k][:, 0:SL], c["mean"][:], y[k][:], start=True, stop=True).then_inc(mean_mm, 1)
                    for k in range(K):
                        pe.wait_ge(squared, k + 1)
                        mm(C[k][:, 0:SL], c["mean"][:], ysq[k][:], start=True, stop=True).then_inc(var_mm, 1)
                    for k in range(K):
                        pe.wait_ge(y_norm, k + 1)
                        mm(A[k][0:SL, 0:P], y[k][:], wvp[:], start=True, stop=True).then_inc(sv_mm, 1)
                    for k in range(K):
                        pe.wait_ge(sv_sb, k + 1)
                        pe.wait_ge(alT_sb, k + 1)
                        mm(C[k][:, 0:T], sv[k][:], alT[k][:], start=True, stop=True).then_inc(out_mm, 1)
                    for k in range(K):
                        pe.wait_ge(out_sb, k + 1)
                        mm(A[k][:, 0:T], wo[:], oT[k][:], start=True, stop=True).then_inc(wo_mm, 1)

                @block.scalar
                def _(act):
                    ac = nc.scalar.activation
                    for k in range(K):
                        ac(tx[k][:], xn[:, seq(k)], ACT.Copy).then_inc(copied, 1)
                    for k in range(K):
                        act.wait_ge(h_mm, k + 1)
                        ac(hT[k][:], A[k][0:SL, 0:T], ACT.Gelu, bias=hbias[:]).then_inc(h_act, 1)
                    for k in range(K):
                        act.wait_ge(negated, k + 1)
                        for t in range(2):
                            ac(ex[k][:, t, :], lg[k][:, t, :], ACT.Exp, bias=nm[k][:, t:t + 1]).then_inc(exped, 1)
                    for k in range(K):
                        act.wait_ge(alT_mm, k + 1)
                        ac(alT[k][:], B[k][0:SL, 0:T], ACT.Copy).then_inc(alT_sb, 1)
                    for k in range(K):
                        act.wait_ge(gates_in, k + 1)
                        ac(rz[k][:], ga[k][:], ACT.Tanh, scale=0.5).then_inc(gates, 1)
                    for k in range(K):
                        act.wait_ge(u_ready, k + 1)
                        ac(nn[k][:], u[k][:], ACT.Tanh, bias=bih[:, 2:3]).then_inc(cell, 1)
                    for k in range(K):
                        act.wait_ge(v_mm, k + 1)
                        ac(v[k][:], D[k][0:SL, 0:P], ACT.Copy).then_inc(v_sb, 1)
                    for k in range(K):
                        act.wait_ge(att_max, k + 1)
                        ac(ae[k][:], A[k][0:SL, 0:SL], ACT.Exp, bias=amax[k][:], accum_out=asm[k][:]).then_inc(att_exp, 1)
                    for k in range(K):
                        act.wait_ge(centered, k + 1)
                        ac(ysq[k][:], yc[k][:], ACT.Square).then_inc(squared, 1)
                    for k in range(K):
                        act.wait_ge(var_mm, k + 1)
                        ac(yrs[k][:], C[k][:, 0:SL], ACT.Ln, bias=c["eps"][:]).then_inc(logged, 1)
                    for k in range(K):
                        act.wait_ge(logged, k + 1)
                        ac(yrs[k][:], yrs[k][:], ACT.Exp, scale=-0.5).then_inc(rooted, 1)
                    for k in range(K):
                        act.wait_ge(out_mm, k + 1)
                        ac(oT[k][:], C[k][:, 0:T], ACT.Identity, bias=vec[:, 3:4]).then_inc(out_sb, 1)

                @block.vector
                def _(dve):
                    link = Link(dve, step)
                    tt, ts = nc.vector.tensor_tensor, nc.vector.tensor_scalar
                    for k in range(K):
                        dve.wait_ge(xt_mm, k + 1)
                        nc.vector.tensor_copy(xt[k][:].rearrange("p t n -> p (t n)"), B[k][:, 0:T]).then_inc(xt_sb, 1)
                    for k in range(K):
                        dve.wait_ge(lg_mm, k + 1)
                        link(ts(lg[k][:].rearrange("p t n -> p (t n)"), A[k][:, T:T + 2 * SL], tau[:], None, ALU.mult))
                        for t in range(2):
                            nc.vector.max(m8[k][:, t, :], lg[k][:, t, :]).then_inc(topped, 1)
                        dve.wait_ge(topped, 2 * k + 2)
                        ts(nm[k][:], m8[k][:, :, 0], -1.0, None, ALU.mult).then_inc(negated, 1)
                        for t in range(2):
                            link(nc.vector.match_replace(rep[k][:, t, :], m8[k][:, t, :], lg[k][:, t, :], MASKED))
                        link(tt(rep[k][:], rep[k][:], lg[k][:], ALU.not_equal))
                    for k in range(K):
                        for t in range(2):
                            dve.wait_ge(exped, 2 * k + t + 1)
                            link(nc.vector.tensor_tensor_reduce(out=al[k][:, t, :], in0=ex[k][:, t, :],
                                                                in1=rep[k][:, t, :], scale=1.0, scalar=0.0, op0=ALU.mult,
                                                                op1=ALU.add, accum_out=asum[k][:, t:t + 1]))
                        link(nc.vector.reciprocal(ainv[k][:], asum[k][:]))
                        for t in range(2):
                            ts(al[k][:, t, :], al[k][:, t, :], ainv[k][:, t:t + 1], None, ALU.mult).then_inc(alphaed, 1)
                    for k in range(K):
                        dve.wait_ge(si_mm, k + 1)
                        link(ts(den[k][:], C[k][:, SL:2 * SL], 1e-8, None, ALU.add))
                        link(nc.vector.reciprocal(den[k][:], den[k][:]))
                        tt(si[k][:], C[k][:, 0:SL], den[k][:], ALU.mult).then_inc(si_sb, 1)
                    for k in range(K):
                        dve.wait_ge(gi_mm, k + 1)
                        tt(ga[k][:], C[k][:, 2 * SL:4 * SL].rearrange("p (a n) -> p a n", a=2), gh[:, 0:2, :],
                           ALU.add).then_inc(gates_in, 1)
                    for k in range(K):
                        dve.wait_ge(gates, k + 1)
                        link(ts(rz[k][:], rz[k][:], 0.5, 0.5, ALU.mult, ALU.add))
                        link(tt(u[k][:], rz[k][:, 0, :], gh[:, 2, :], ALU.mult))
                        tt(u[k][:], u[k][:], C[k][:, 4 * SL:5 * SL], ALU.add).then_inc(u_ready, 1)
                    for k in range(K):
                        dve.wait_ge(cell, k + 1)
                        link(tt(zs[k][:], slot[:], nn[k][:], ALU.subtract))
                        link(tt(zs[k][:], zs[k][:], rz[k][:, 1, :], ALU.mult))
                        tt(sn[k][:], nn[k][:], zs[k][:], ALU.add).then_inc(s_new, 1)
                    for k in range(K):
                        dve.wait_ge(qk_mm, k + 1)
                        link(ts(qk[k][:, 0, :], A[k][0:DQ, 0:SL], bqk[:, 0:1], float(DQ) ** -0.5, ALU.add, ALU.mult))
                        ts(qk[k][:, 1, :], A[k][0:DQ, SL:2 * SL], bqk[:, 1:2], None, ALU.add).then_inc(qk_sb, 1)
                    for k in range(K):
                        dve.wait_ge(att_mm, k + 1)
                        nc.vector.tensor_reduce(out=amax[k][:], in_=A[k][0:SL, 0:SL], axis=AX_X, op=ALU.max,
                                                negate=True).then_inc(att_max, 1)
                    for k in range(K):
                        dve.wait_ge(att_exp, k + 1)
                        link(nc.vector.reciprocal(ai[k][:], asm[k][:]))
                        ts(ae[k][:], ae[k][:], ai[k][:], None, ALU.mult).then_inc(att_norm, 1)
                    for k in range(K):
                        dve.wait_ge(aT_mm, k + 1)
                        nc.vector.tensor_copy(aT[k][:], A[k][0:SL, SL:2 * SL]).then_inc(aT_sb, 1)
                    for k in range(K):
                        dve.wait_ge(comm_mm, k + 1)
                        dve.wait_ge(s_new, k + 1)
                        nc.vector.scalar_tensor_tensor(out=y[k][:], in0=C[k][:, 0:SL], scalar=vec[:, 0:1], in1=sn[k][:],
                                                       op0=ALU.add, op1=ALU.add).then_inc(y_ready, 1)
                    for k in range(K):
                        dve.wait_ge(mean_mm, k + 1)
                        tt(yc[k][:], y[k][:], A[k][:, 0:SL], ALU.subtract).then_inc(centered, 1)
                    for k in range(K):
                        dve.wait_ge(rooted, k + 1)
                        link(tt(y[k][:], yc[k][:], yrs[k][:], ALU.mult))
                        ts(y[k][:], y[k][:], vec[:, 1:2], vec[:, 2:3], ALU.mult, ALU.add).then_inc(y_norm, 1)
                    for k in range(K):
                        dve.wait_ge(sv_mm, k + 1)
                        nc.vector.tensor_copy(sv[k][:], A[k][0:SL, 0:P]).then_inc(sv_sb, 1)
                    for k in range(K):
                        dve.wait_ge(wo_mm, k + 1)
                        ts(g_out[:, seq(k)], A[k][:, 0:T], vec[:, 4:5], None, ALU.add)
            s.barrier()


def l2_attention(nc, c, d, xn, s_out):
    HD = 64
    SC = HD ** -0.5
    PAD = -30000.0
    NP2 = H // 2
    with Scope(nc, "a2") as s:
        wqkv = s.sb("wqkv", [P, 3, H * HD])
        wo = s.sb("wo", [P, NP2, P])
        bias = [s.sb("bias0", [P, H, P]), s.sb("bias1", [P, H, T])]
        rows = nc.dram_tensor("a2_bias_rows", (H, P, T + P), F32).ap()
        load(nc, s, [(wqkv[:].rearrange("p m e -> p (m e)"), d["qkv"].rearrange("p m n e -> p (m n e)")),
                     (wo[:], d["out_w"].rearrange("n e x -> (n e) x").rearrange("(c p) x -> p c x", p=P))])
        with Scope(nc, "a2t") as t:
            rb = t.sb("rpe", [H, T])
            zero = t.sb("zero", [H, T])
            cum = t.sb("cum", [H, T])
            rev = t.sb("reversed", [H, T + P])
            in_, filled, step, ready, out_, spread = t.sems("in filled step ready out spread")
            with nc.Block() as block:
                @block.vector
                def _(dve):
                    link = Link(dve, step)
                    link(nc.vector.memset(zero[:], 0.0))
                    link(nc.vector.memset(rev[:], PAD / SC))
                    dve.wait_ge(in_, 16)
                    link(nc.vector.tensor_tensor_scan(cum[:], rb[:], zero[:], 0.0, ALU.add, ALU.add))
                    nc.vector.tensor_scalar(rev[:, 0:T], cum[:, ::-1], 1.0 / SC, None, ALU.mult).then_inc(ready, 1)

                @block.sync
                def _(sp):
                    sp.dma_start(rb[:], d["rpe_bias"]).then_inc(in_, 16)
                    sp.wait_ge(ready, 1)
                    sp.dma_start(rows, rev[:].unsqueeze(1).broadcast_to([H, P, T + P])).then_inc(out_, 16)
                    sp.wait_ge(out_, 16)
                    for tile in range(2):
                        src = bass.AP(tensor=rows.tensor, offset=rows.offset + T - 1 - P * tile,
                                      ap=[[T + P - 1, P], [P * (T + P), H], [1, P * (tile + 1)]])
                        sp.dma_start(bias[tile][:], src).then_inc(spread, 16)
                    sp.wait_ge(spread, 32)
            t.barrier()

        tile_x = s.sb("x", [P, T])
        qT, kT = s.sb("qT", [P, NP2, T]), s.sb("kT", [P, NP2, T])
        v = s.sb("v", [P, 2, H * HD])
        NL, NQ, NT = 3, 3, 3
        lg, pr, pt = s.sb("logits", [P, NL, T]), s.sb("probs", [P, NQ, T]), s.sb("probs_T", [P, NT, T])
        nmax, rsum, rinv = s.sb("neg_max", [P, 2 * H]), s.sb("row_sum", [P, 2 * H]), s.sb("row_inv", [P, 2 * H])
        on = s.sb("o_normed", [P, 2, H * HD])
        oT = s.sb("oT", [P, NP2, T])
        pj = s.banks("pj", 4)
        ob = s.banks("out", 4)
        (copied, qk_mm, lo_sb, hi_sb, logit_mm, logits, probs, tr_mm, tr_sb, pv_mm, inv, normed, oT_mm, oT_lo, oT_hi,
         wo_mm, step) = s.sems("copied qk_mm lo_sb hi_sb logit_mm logits probs tr_mm tr_sb pv_mm inv normed oT_mm "
                               "oT_lo oT_hi wo_mm step")
        units = [(h, t) for t in range(2) for h in range(H)]
        NU = len(units)
        NPJ = 12
        with nc.Fori(0, xn.shape[1] // T) as b:
            with nc.Block() as block:
                def keep(eng, n):
                    eng.wait_ge(qk_mm, 2 * n + 2)
                    src = pj[:, n % 4, :]
                    if n < 8:
                        dst = (qT, kT)[n // 4][:, 2 * (n % 4):2 * (n % 4) + 2, :].rearrange("p j t -> p (j t)")
                    else:
                        dst = v[:, (n - 8) // 2, (n % 2) * BANK:(n % 2 + 1) * BANK]
                    if n % 2 == 0:
                        nc.scalar.activation(dst, src, ACT.Copy).then_inc(lo_sb, 1)
                    else:
                        nc.vector.tensor_copy(dst, src).then_inc(hi_sb, 1)

                def evac(eng, u):
                    h, t = units[u]
                    nk = P * (t + 1)
                    eng.wait_ge(tr_mm, u + 1)
                    if u >= NT:
                        eng.wait_ge(pv_mm, u - NT + 1)
                    eng.wait_ge(tr_sb, u)
                    if u % 2:
                        ins = nc.scalar.activation(pt[:, u % NT, 0:nk], pj[:, 2 + u % 2, 0:nk], ACT.Copy)
                    else:
                        ins = nc.vector.tensor_copy(pt[:, u % NT, 0:nk], pj[:, 2 + u % 2, 0:nk])
                    ins.then_inc(tr_sb, 1)

                def norm(dve, t):
                    dve.wait_ge(probs, H * (t + 1))
                    nc.vector.reciprocal(rinv[:, H * t:H * (t + 1)], rsum[:, H * t:H * (t + 1)]).then_inc(inv, 1)
                    dve.wait_ge(inv, t + 1)
                    dve.wait_ge(pv_mm, H * (t + 1))
                    for i in range(2):
                        h0 = H * t + 8 * i
                        nc.vector.tensor_tensor(on[:, t, i * BANK:(i + 1) * BANK].rearrange("p (h e) -> p h e", h=8),
                                                ob[:, 2 * t + i, :].rearrange("p (h e) -> p h e", h=8),
                                                rinv[:, h0:h0 + 8].unsqueeze(2).broadcast_to([P, 8, HD]),
                                                ALU.mult).then_inc(normed, 1)

                @block.tensor
                def _(pe):
                    for n in range(NPJ):
                        if n >= 4:
                            pe.wait_ge((lo_sb, hi_sb)[n % 2], (n - 4) // 2 + 1)
                        if n == 8:
                            pe.wait_ge(copied, 1)
                        for i in range(2):
                            o = pj[:, n % 4, i * T:(i + 1) * T]
                            if n < 8:
                                col = (2 * (n % 4) + i) * P
                                nc.tensor.matmul(o, wqkv[:, n // 4, col:col + P], xn[:, tokens(b)], start=True,
                                                 stop=True).then_inc(qk_mm, 1)
                            else:
                                t = (n - 8) // 2
                                nc.tensor.matmul(o, tile_x[:, t * P:(t + 1) * P],
                                                 wqkv[:, 2, (2 * (n % 2) + i) * T:(2 * (n % 2) + i + 1) * T], start=True,
                                                 stop=True).then_inc(qk_mm, 1)
                    pe.wait_ge(lo_sb, 6)
                    pe.wait_ge(hi_sb, 6)

                    def logit(u):
                        h, t = units[u]
                        r, j = slice(HD * (h % 2), HD * (h % 2) + HD), h // 2
                        if u >= 2:
                            pe.wait_ge(logits, u - 1)
                        nc.tensor.matmul(pj[:, u % 2, 0:P * (t + 1)], qT[r, j, t * P:(t + 1) * P], kT[r, j, 0:P * (t + 1)],
                                         start=True, stop=True).then_inc(logit_mm, 1)

                    def transpose(u):
                        h, t = units[u]
                        pe.wait_ge(probs, u + 1)
                        if u >= 2:
                            pe.wait_ge(tr_sb, u - 1)
                        for kt in range(t + 1):
                            ins = nc.tensor.transpose(pj[:, 2 + u % 2, kt * P:(kt + 1) * P],
                                                      pr[:, u % NQ, kt * P:(kt + 1) * P], c["ident"][:])
                        ins.then_inc(tr_mm, 1)

                    def weigh(u):
                        h, t = units[u]
                        pe.wait_ge(tr_sb, u + 1)
                        for kt in range(t + 1):
                            ins = nc.tensor.matmul(ob[:, 2 * t + h // 8, HD * (h % 8):HD * (h % 8) + HD],
                                                   pt[:, u % NT, kt * P:(kt + 1) * P], v[:, kt, HD * h:HD * h + HD],
                                                   start=kt == 0, stop=kt == t)
                        ins.then_inc(pv_mm, 1)

                    for u in range(NU + 3):
                        if u < NU:
                            logit(u)
                        if 2 <= u < NU + 2:
                            transpose(u - 2)
                        if 3 <= u:
                            weigh(u - 3)
                    pe.wait_ge(normed, 4)
                    for m in range(4):
                        for i in range(2):
                            for t in range(2):
                                nc.tensor.transpose(pj[:, m, i * T + t * P:i * T + (t + 1) * P],
                                                    on[:, t, (2 * m + i) * P:(2 * m + i + 1) * P],
                                                    c["ident"][:]).then_inc(oT_mm, 1)
                    for j in range(NP2):
                        pe.wait_ge((oT_lo, oT_hi)[(j // 2) % 2], j // 4 + 1)
                        ins = nc.tensor.matmul(ob[:, 0, 0:T], wo[:, j, :], oT[:, j, :], start=j == 0, stop=j == NP2 - 1)
                    ins.then_inc(wo_mm, 1)

                @block.scalar
                def _(act):
                    nc.scalar.activation(tile_x[:], xn[:, tokens(b)], ACT.Copy).then_inc(copied, 1)
                    for n in range(0, NPJ, 2):
                        keep(act, n)
                    for u in range(NU):
                        h, t = units[u]
                        nk = P * (t + 1)
                        act.wait_ge(logits, u + 1)
                        if u >= NQ:
                            act.wait_ge(tr_mm, u - NQ + 1)
                        nc.scalar.activation(pr[:, u % NQ, 0:nk], lg[:, u % NL, 0:nk], ACT.Exp, scale=-1.0,
                                             bias=nmax[:, u:u + 1], accum_out=rsum[:, u:u + 1]).then_inc(probs, 1)
                        if u >= 1 and u % 2 == 0:
                            evac(act, u - 1)
                    evac(act, NU - 1)
                    for m in (0, 2):
                        act.wait_ge(oT_mm, 4 * m + 4)
                        nc.scalar.activation(oT[:, 2 * m:2 * m + 2, :].rearrange("p j t -> p (j t)"), pj[:, m, :],
                                             ACT.Copy).then_inc(oT_lo, 1)
                    act.wait_ge(wo_mm, 1)
                    nc.scalar.activation(s_out[:, tokens(b)], ob[:, 0, 0:T], ACT.Copy)

                @block.vector
                def _(dve):
                    for n in range(1, NPJ, 2):
                        keep(dve, n)
                    for u in range(NU + 2):
                        if u < NU:
                            h, t = units[u]
                            nk = P * (t + 1)
                            dve.wait_ge(logit_mm, u + 1)
                            if u >= NL:
                                dve.wait_ge(probs, u - NL + 1)
                            nc.vector.tensor_tensor_reduce(out=lg[:, u % NL, 0:nk], in0=pj[:, u % 2, 0:nk],
                                                           in1=bias[t][:, h, :], scale=-SC, scalar=3e38, op0=ALU.add,
                                                           op1=ALU.min, accum_out=nmax[:, u:u + 1]).then_inc(logits, 1)
                        if u >= 2 and u % 2 == 0:
                            evac(dve, u - 2)
                        if u == 3 * H // 2 + 2:
                            norm(dve, 0)
                    norm(dve, 1)
                    for m in (1, 3):
                        dve.wait_ge(oT_mm, 4 * m + 4)
                        nc.vector.tensor_copy(oT[:, 2 * m:2 * m + 2, :].rearrange("p j t -> p (j t)"),
                                              pj[:, m, :]).then_inc(oT_hi, 1)
            s.barrier()


def make_iota(nc, s, n):
    whole = s.sb("iota_int", [P, n], mybir.dt.int32)
    real = s.sb("iota", [P, n])
    with Scope(nc, "iota") as t:
        made, kept = t.sems("made kept")
        with nc.Block() as block:
            @block.gpsimd
            def _(pool):
                nc.gpsimd.iota(whole[:], pattern=[[1, n]], base=0, channel_multiplier=0).then_inc(made, 1)

            @block.vector
            def _(dve):
                dve.wait_ge(made, 1)
                nc.vector.tensor_copy(real[:], whole[:]).then_inc(kept, 1)
        t.barrier()
    return real


def l2_ffn_tables(n):
    half = P // 2
    freq = (1.0 / np.float32(10000.0) ** (np.arange(0, P, 2, dtype=np.float32) / np.float32(P))).astype(np.float32)
    ang = freq.astype(np.float64)[:, None] * np.arange(n)[None, :]
    co, si = np.cos(ang), np.sin(ang)
    both = [np.concatenate(v, 0) for v in ((co, co), (si, si), (si, co), (-co, si))]
    assert both[0].shape == (2 * half, n)
    return np.stack(both, 1).astype(np.float32)


def relative_attention(nc, c, d, src, xa, out):
    with Scope(nc, "r2") as s:
        w = {n: s.sb(n, [P, P]) for n in ["wq", "wk", "wv", "wo"]}
        wp_ = {n: s.sb(n + "_padded", [P, 4, P]) for n in ["wq", "wk"]}
        wpos = s.sb("wpT_padded", [P, 4, P])
        trig = s.sb("trig", [P, 4, T])
        load(nc, s, [(w[n][:], d[n]) for n in w] + [(trig[:], d["trig"])])
        with Scope(nc, "r2t") as t:
            zeroed, landed, padded = t.sems("zeroed landed padded")
            with nc.Block() as block:
                @block.gpsimd
                def _(pool):
                    for n in wp_:
                        nc.gpsimd.memset(wp_[n][:], 0.0)
                    nc.gpsimd.memset(wpos[:], 0.0).then_inc(zeroed, 1)

                @block.vector
                def _(dve):
                    dve.wait_ge(zeroed, 1)
                    for n in wp_:
                        pad_heads(nc, wp_[n][:], w[n][:]).then_inc(padded, 1)

                @block.sync
                def _(sp):
                    sp.wait_ge(zeroed, 1)
                    for g in range(4):
                        sp.dma_start(wpos[32 * g:32 * g + 8, :, :],
                                     d["wpT"].rearrange("(j g d) f -> g d j f", j=4, g=4)[g]).then_inc(landed, 16)
                    sp.wait_ge(landed, 64)
            t.barrier()
        tile_x = s.sb("x", [P, T])
        qT, kT = s.sb("qT", [P, 4, T]), s.sb("kT", [P, 4, T])
        v = s.sb("v", [P, 2, P])
        NQW, NP_, NT = 3, 3, 3
        qw = s.sb("qw", [P, 2, T])
        m1, m2 = s.sb("qw_cos", [P, NQW, T]), s.sb("qw_sin", [P, NQW, T])
        pr, pt = s.sb("probs", [P, NP_, T]), s.sb("probs_T", [P, NT, T])
        nmax, rsum, rinv = s.sb("neg_max", [P, 2 * H]), s.sb("row_sum", [P, 2 * H]), s.sb("row_inv", [P, 2 * H])
        on, oT = s.sb("o_normed", [P, 2, P]), s.sb("oT", [P, T])
        pj = s.banks("pj", 6)
        ob = s.banks("out", 2)
        (copied, q_mm, k_mm, v_mm, q_sb, k_sb, v_sb, qw_mm, qw_sb, cosed, sined, logit_mm, maxed, probs, tr_mm, tr_sb,
         pv_mm, inv, normed, oT_mm, oT_sb, wo_mm) = s.sems(
            "copied q_mm k_mm v_mm q_sb k_sb v_sb qw_mm qw_sb cosed sined logit_mm maxed probs tr_mm tr_sb pv_mm inv "
            "normed oT_mm oT_sb wo_mm")
        units = [(h, t) for h in range(H) for t in range(2)]
        NU = len(units)
        with nc.Fori(0, xa.shape[1] // T) as b:
            with nc.Block() as block:
                def evac(eng, u):
                    eng.wait_ge(tr_mm, u + 1)
                    if u >= NT:
                        eng.wait_ge(pv_mm, u - NT + 1)
                    eng.wait_ge(tr_sb, u)
                    if u % 2:
                        ins = nc.scalar.activation(pt[:, u % NT, :], pj[:, 2 + u % 2, 0:T], ACT.Copy)
                    else:
                        ins = nc.vector.tensor_copy(pt[:, u % NT, :], pj[:, 2 + u % 2, 0:T])
                    ins.then_inc(tr_sb, 1)

                @block.tensor
                def _(pe):
                    for kind, n in enumerate(["wq", "wk"]):
                        for j in range(4):
                            nc.tensor.matmul(pj[:, 2 * kind + j // 2, (j % 2) * T:(j % 2 + 1) * T], wp_[n][:, j, :],
                                             xa[:, tokens(b)], start=True, stop=True).then_inc((q_mm, k_mm)[kind], 1)
                    pe.wait_ge(copied, 1)
                    for t in range(2):
                        nc.tensor.matmul(pj[:, 4, t * P:(t + 1) * P], tile_x[:, t * P:(t + 1) * P], w["wv"][:],
                                         start=True, stop=True).then_inc(v_mm, 1)
                    pe.wait_ge(q_sb, 4)
                    pe.wait_ge(k_sb, 4)
                    pe.wait_ge(v_sb, 1)

                    def position(h):
                        r, j = slice(32 * (h % 4), 32 * (h % 4) + 32), h // 4
                        if h >= 2:
                            pe.wait_ge(qw_sb, h - 1)
                        nc.tensor.matmul(pj[:, 4 + h % 2, 0:T], wpos[r, j, :], qT[r, j, :], start=True, stop=True,
                                         tile_position=(32 * (h % 4), 0)).then_inc(qw_mm, 1)

                    def logit(u):
                        h, t = units[u]
                        r, j = slice(32 * (h % 4), 32 * (h % 4) + 32), h // 4
                        o = pj[:, u % 2, 0:T]
                        if u >= 2:
                            pe.wait_ge(probs, u - 1)
                        nc.tensor.matmul(o, qT[r, j, t * P:(t + 1) * P], kT[r, j, :], start=True, stop=False,
                                         tile_position=(32 * (h % 4), 0))
                        pe.wait_ge(cosed, h + 1)
                        nc.tensor.matmul(o, m1[:, h % NQW, t * P:(t + 1) * P], trig[:, 2, :], start=False, stop=False)
                        pe.wait_ge(sined, h + 1)
                        nc.tensor.matmul(o, m2[:, h % NQW, t * P:(t + 1) * P], trig[:, 3, :], start=False,
                                         stop=True).then_inc(logit_mm, 1)

                    def transpose(u):
                        pe.wait_ge(probs, u + 1)
                        if u >= 2:
                            pe.wait_ge(tr_sb, u - 1)
                        for kt in range(2):
                            ins = nc.tensor.transpose(pj[:, 2 + u % 2, kt * P:(kt + 1) * P],
                                                      pr[:, u % NP_, kt * P:(kt + 1) * P], c["ident"][:])
                        ins.then_inc(tr_mm, 1)

                    def weigh(u):
                        h, t = units[u]
                        pe.wait_ge(tr_sb, u + 1)
                        for kt in range(2):
                            ins = nc.tensor.matmul(ob[:, t, 8 * h:8 * h + 8], pt[:, u % NT, kt * P:(kt + 1) * P],
                                                   v[:, kt, 8 * h:8 * h + 8], start=kt == 0, stop=kt == 1)
                        ins.then_inc(pv_mm, 1)

                    position(0)
                    position(1)
                    for u in range(NU + 3):
                        if u < NU:
                            logit(u)
                            if u % 2 == 0 and u // 2 + 2 < H:
                                position(u // 2 + 2)
                        if 2 <= u < NU + 2:
                            transpose(u - 2)
                        if 3 <= u:
                            weigh(u - 3)
                    for t in range(2):
                        pe.wait_ge(normed, t + 1)
                        nc.tensor.transpose(pj[:, 4, t * P:(t + 1) * P], on[:, t, :], c["ident"][:]).then_inc(oT_mm, 1)
                    pe.wait_ge(oT_sb, 1)
                    nc.tensor.matmul(pj[:, 5, 0:T], w["wo"][:], oT[:], start=True, stop=True).then_inc(wo_mm, 1)

                @block.scalar
                def _(act):
                    nc.scalar.activation(tile_x[:], xa[:, tokens(b)], ACT.Copy).then_inc(copied, 1)
                    for j in range(4):
                        act.wait_ge(q_mm, 2 * (j // 2) + 2)
                        nc.scalar.activation(qT[:, j, :], pj[:, j // 2, (j % 2) * T:(j % 2 + 1) * T], ACT.Copy,
                                             scale=8.0 ** -0.5).then_inc(q_sb, 1)
                    act.wait_ge(v_mm, 2)
                    nc.scalar.activation(v[:].rearrange("p t e -> p (t e)"), pj[:, 4, 0:T], ACT.Copy).then_inc(v_sb, 1)

                    def keep_qw(h):
                        act.wait_ge(qw_mm, h + 1)
                        if h >= 2:
                            act.wait_ge(cosed, h - 1)
                            act.wait_ge(sined, h - 1)
                        nc.scalar.activation(qw[:, h % 2, :], pj[:, 4 + h % 2, 0:T], ACT.Copy).then_inc(qw_sb, 1)
                    keep_qw(0)
                    keep_qw(1)
                    for u in range(NU):
                        act.wait_ge(maxed, u + 1)
                        if u >= NP_:
                            act.wait_ge(tr_mm, u - NP_ + 1)
                        nc.scalar.activation(pr[:, u % NP_, :], pj[:, u % 2, 0:T], ACT.Exp, bias=nmax[:, u:u + 1],
                                             accum_out=rsum[:, u:u + 1]).then_inc(probs, 1)
                        if u % 2 == 0 and u // 2 + 2 < H:
                            keep_qw(u // 2 + 2)
                        if u >= 1 and u % 2 == 0:
                            evac(act, u - 1)
                    evac(act, NU - 1)
                    act.wait_ge(oT_mm, 2)
                    nc.scalar.activation(oT[:], pj[:, 4, 0:T], ACT.Copy).then_inc(oT_sb, 1)

                @block.gpsimd
                def _(pool):
                    for h in range(H):
                        pool.wait_ge(qw_sb, h + 1)
                        if h >= NQW:
                            pool.wait_ge(logit_mm, 2 * (h - NQW) + 2)
                        nc.gpsimd.tensor_tensor(m2[:, h % NQW, :], qw[:, h % 2, :], trig[:, 1, :], ALU.mult).then_inc(sined, 1)

                @block.vector
                def _(dve):
                    for j in range(4):
                        dve.wait_ge(k_mm, 2 * (j // 2) + 2)
                        nc.vector.tensor_copy(kT[:, j, :], pj[:, 2 + j // 2, (j % 2) * T:(j % 2 + 1) * T]).then_inc(k_sb, 1)

                    def times_cos(h):
                        dve.wait_ge(qw_sb, h + 1)
                        if h >= NQW:
                            dve.wait_ge(logit_mm, 2 * (h - NQW) + 2)
                        nc.vector.tensor_tensor(m1[:, h % NQW, :], qw[:, h % 2, :], trig[:, 0, :], ALU.mult).then_inc(cosed, 1)
                    times_cos(0)
                    times_cos(1)
                    for u in range(NU + 2):
                        if u < NU:
                            dve.wait_ge(logit_mm, u + 1)
                            nc.vector.tensor_reduce(out=nmax[:, u:u + 1], in_=pj[:, u % 2, 0:T], axis=AX_X, op=ALU.max,
                                                    negate=True).then_inc(maxed, 1)
                            if u % 2 == 0 and u // 2 + 2 < H:
                                times_cos(u // 2 + 2)
                        if u >= 2 and u % 2 == 0:
                            evac(dve, u - 2)
                    dve.wait_ge(probs, NU)
                    nc.vector.reciprocal(rinv[:], rsum[:]).then_inc(inv, 1)
                    dve.wait_ge(inv, 1)
                    dve.wait_ge(pv_mm, NU)
                    for t in range(2):
                        nc.vector.tensor_tensor(on[:, t, :].rearrange("p (h e) -> p h e", h=H),
                                                ob[:, t, 0:P].rearrange("p (h e) -> p h e", h=H),
                                                rinv[:].rearrange("p (h t) -> p h t", t=2)[:, :, t:t + 1]
                                                .broadcast_to([P, H, 8]), ALU.mult).then_inc(normed, 1)
                    dve.wait_ge(wo_mm, 1)
                    nc.vector.tensor_tensor(out[:, tokens(b)], src[:, tokens(b)], pj[:, 5, 0:T], ALU.add)
            s.barrier()


def top_experts(nc, link, m8, idx, idf, iota, chosen, score, k):
    link(nc.vector.max(m8, score))
    link(nc.vector.max_index(idx, m8, score))
    link(nc.vector.tensor_copy(idf, idx))
    link(nc.vector.tensor_scalar(chosen, iota, idf[:, 0:1], None, ALU.is_equal))
    for i in range(1, k):
        link(nc.vector.scalar_tensor_tensor(out=chosen, in0=iota, scalar=idf[:, i:i + 1], in1=chosen,
                                            op0=ALU.is_equal, op1=ALU.add))


def relu_experts(nc, c, d, src, x2, out):
    E, TOPK = 32, 4
    with Scope(nc, "m2") as s:
        keys, vals = s.sb("keys", [P, E, P]), s.sb("values", [P, E, P])
        selw = s.sb("sel_w", [P, E])
        load(nc, s, [(keys[:], d["keys"].rearrange("e p n -> p e n")), (vals[:], d["values"].rearrange("e p n -> p e n")),
                     (selw[:], d["sel_w"])])
        iota = make_iota(nc, s, E)
        tile_x = s.sb("x", [P, T])
        sel, chosen, gate = s.sb("scores", [P, 2, E]), s.sb("chosen", [P, 2, E]), s.sb("gate", [P, 2, E])
        m8, idx, idf = s.sb("top8", [P, 2, 8]), s.sb("idx", [P, 2, 8], U32), s.sb("idx_f", [P, 2, 8])
        NH = 4
        hs = s.sb("hidden", [P, NH, T])
        acc = s.sb("acc", [P, 2, P])
        hp = s.banks("h", 3)
        op = s.banks("o", 3)
        sp_ = s.banks("scores", 1)
        fin = s.banks("final", 1)
        copied, sel_mm, scored, step, gated, h_mm, h_act, o_mm, added, acc_mm = s.sems(
            "copied sel_mm scored step gated h_mm h_act o_mm added acc_mm")
        with nc.Fori(0, x2.shape[1] // T) as b:
            with nc.Block() as block:
                @block.tensor
                def _(pe):
                    pe.wait_ge(copied, 1)
                    for t in range(2):
                        nc.tensor.matmul(sp_[:, 0, t * E:(t + 1) * E], tile_x[:, t * P:(t + 1) * P], selw[:], start=True,
                                         stop=True).then_inc(sel_mm, 1)
                    for e in range(E + 2):
                        if e < E:
                            if e >= 3:
                                pe.wait_ge(h_act, e - 2)
                            nc.tensor.matmul(hp[:, e % 3, 0:T], keys[:, e, :], tile_x[:], start=True,
                                             stop=True).then_inc(h_mm, 1)
                        if e >= 2:
                            f = e - 2
                            pe.wait_ge(h_act, f + 1)
                            if f >= 3:
                                pe.wait_ge(added, 2 * (f - 2))
                            for t in range(2):
                                ins = nc.tensor.matmul(op[:, f % 3, t * P:(t + 1) * P], hs[:, f % NH, t * P:(t + 1) * P],
                                                       vals[:, f, :], start=True, stop=True)
                            ins.then_inc(o_mm, 1)
                    pe.wait_ge(added, 2 * E)
                    for t in range(2):
                        ins = nc.tensor.transpose(fin[:, 0, t * P:(t + 1) * P], acc[:, t, :], c["ident"][:])
                    ins.then_inc(acc_mm, 1)

                @block.scalar
                def _(act):
                    nc.scalar.activation(tile_x[:], x2[:, tokens(b)], ACT.Copy).then_inc(copied, 1)
                    act.wait_ge(sel_mm, 2)
                    nc.scalar.activation(sel[:].rearrange("p t e -> p (t e)"), sp_[:, 0, 0:2 * E],
                                         ACT.Sigmoid).then_inc(scored, 1)
                    for e in range(E):
                        act.wait_ge(h_mm, e + 1)
                        if e >= NH:
                            act.wait_ge(o_mm, e - NH + 1)
                        nc.scalar.activation(hs[:, e % NH, :], hp[:, e % 3, 0:T], ACT.Relu).then_inc(h_act, 1)

                @block.vector
                def _(dve):
                    link = Link(dve, step)
                    dve.wait_ge(scored, 1)
                    for t in range(2):
                        top_experts(nc, link, m8[:, t, :], idx[:, t, :], idf[:, t, :], iota[:], chosen[:, t, :],
                                    sel[:, t, :], TOPK)
                    link(nc.vector.tensor_tensor(gate[:], chosen[:], sel[:], ALU.mult))
                    for e in range(E):
                        dve.wait_ge(o_mm, e + 1)
                        for t in range(2):
                            o = op[:, e % 3, t * P:(t + 1) * P]
                            if e == 0:
                                ins = nc.vector.tensor_scalar(acc[:, t, :], o, gate[:, t, e:e + 1], None, ALU.mult)
                            else:
                                dve.wait_ge(added, 2 * (e - 1) + t + 1)
                                ins = nc.vector.scalar_tensor_tensor(out=acc[:, t, :], in0=o, scalar=gate[:, t, e:e + 1],
                                                                     in1=acc[:, t, :], op0=ALU.mult, op1=ALU.add)
                            ins.then_inc(added, 1)
                    dve.wait_ge(acc_mm, 1)
                    nc.vector.tensor_tensor(out[:, tokens(b)], src[:, tokens(b)], fin[:, 0, 0:T], ALU.add)
            s.barrier()


def l2_ffn(nc, c, d, xn, g_out):
    with Scope(nc, "f2") as s:
        normed = s.sb("normed", [P, xn.shape[1]])
        vec = s.sb("vectors", [P, 4])
        load(nc, s, [(vec[:, i:i + 1], column(d[n])) for i, n in enumerate(["ln1_g", "ln1_b", "ln2_g", "ln2_b"])])
        gate_and_norm(nc, c, xn, normed, affine=(vec[:, 0:1], vec[:, 1:2]))
        relative_attention(nc, c, d, xn, normed, g_out)
        gate_and_norm(nc, c, g_out, normed, affine=(vec[:, 2:3], vec[:, 3:4]))
        relu_experts(nc, c, d, g_out, normed, g_out)


def l3_attention(nc, c, d, xn, s_out, normed):
    DI, NS, DR, KC = 256, 16, 64, 4
    NC_ = DI // P
    DIRS = ("f", "b")
    with Scope(nc, "a3") as s:
        vec = s.sb("vectors", [P, 2])
        W = [{"in": s.sb(f"{x}_in", [P, 2 * DI]), "conv": s.sb(f"{x}_conv", [P, NC_, KC]), "cb": s.sb(f"{x}_cb", [P, NC_]),
              "xp": s.sb(f"{x}_xproj", [P, NC_, DR + 2 * NS]), "dt": s.sb(f"{x}_dt", [DR, DI]),
              "dtb": s.sb(f"{x}_dtb", [P, NC_]), "A": s.sb(f"{x}_A", [P, NC_, NS]), "D": s.sb(f"{x}_D", [P, NC_]),
              "out": s.sb(f"{x}_out", [P, NC_, P])} for x in DIRS]
        pairs = [(vec[:, 0:1], column(d["ln_g"])), (vec[:, 1:2], column(d["ln_b"]))]
        for x, w in zip(DIRS, W):
            pairs += [(w["in"][:], d[x + "_in_wT"]), (w["conv"][:], d[x + "_conv_w"].rearrange("(c p) k -> p c k", p=P)),
                      (w["cb"][:], column(d[x + "_conv_b"])),
                      (w["xp"][:], d[x + "_xproj_wT"].rearrange("(c p) k -> p c k", p=P)), (w["dt"][:], d[x + "_dt_wT"]),
                      (w["dtb"][:], column(d[x + "_dt_b"])), (w["A"][:], d[x + "_Alog"].rearrange("(c p) k -> p c k", p=P)),
                      (w["D"][:], column(d[x + "_D"])), (w["out"][:], d[x + "_out_wT"].rearrange("(c p) k -> p c k", p=P))]
        load(nc, s, pairs)
        gate_and_norm(nc, c, xn, normed, affine=(vec[:, 0:1], vec[:, 1:2]))

        def two(name, shape):
            return [s.sb(f"{name}{i}", shape) for i in range(2)]
        tx = two("x", [P, T])
        up = two("u_padded", [P, NC_, T + KC - 1])
        u, zs, dt, dtu = two("u", [P, NC_, T]), two("silu_z", [P, NC_, T]), two("dt", [P, NC_, T]), two("dt_u", [P, NC_, T])
        ex = two("exp", [P, NC_, T])
        dbc = two("dbc", [DR + 2 * NS, T])
        dA = two("dA", [P, NS, T])
        h = two("h", [P, NS, T])
        Bs = two("B", [P, 2, T])
        Cs = s.sb("C", [P, NS, T])
        yz = s.sb("y", [P, NC_, T])
        sum_ = s.sb("sum", [P, T])
        pj = s.banks("pj", 2)
        bc = s.banks("bc", 3)
        yp = s.banks("y", 2)
        op = s.banks("out", 1)
        cleared = s.sems("cleared")
        (copied, uz_mm, u_sb, z_sb, tapped, conved, u_act, dbc_mm, dbc_sb, dt_mm, dt_abs, dt_exp, dt_log, dt_max, dt_sb, dtu_sb,
         step, dA_sb, b_mm, b_used, b_sb, c_mm, c_sb, hb0, hb1, scanned, hc_dve, hc_pool, y_mm, y_sb, out_mm, summed) = s.sems(
            "copied uz_mm u_sb z_sb tapped conved u_act dbc_mm dbc_sb dt_mm dt_abs dt_exp dt_log dt_max dt_sb dtu_sb "
            "step dA_sb b_mm b_used b_sb c_mm c_sb hb0 hb1 scanned hc_dve hc_pool y_mm y_sb out_mm summed")
        with nc.Block() as block:
            @block.vector
            def _(dve):
                dve.wait_ge(cleared, 1)
                for w in W:
                    nc.vector.tensor_scalar(w["A"][:], w["A"][:], -1.0, None, ALU.mult)

            @block.scalar
            def _(act):
                for w in W:
                    ins = nc.scalar.activation(w["A"][:], w["A"][:], ACT.Exp)
                ins.then_inc(cleared, 1)

            @block.gpsimd
            def _(pool):
                for i in range(2):
                    nc.gpsimd.memset(up[i][:], 0.0)
                    nc.gpsimd.memset(dA[i][:, :, 0:1], 0.0)
        s.barrier()
        NPAIR = NS // 2
        POOL_PAIRS = (1, 3, 5, 7)
        with nc.Fori(0, xn.shape[1] // T) as b:
            with nc.Block() as block:
                @block.tensor
                def _(pe):
                    mm = nc.tensor.matmul
                    for r in range(2):
                        pe.wait_ge(copied, r + 1)
                        for i in range(2):
                            if r:
                                pe.wait_ge((u_sb, z_sb)[i], 1)
                            for k in range(NC_):
                                ins = mm(pj[:, i, k * T:(k + 1) * T], W[r]["in"][:, (i * NC_ + k) * P:(i * NC_ + k + 1) * P],
                                         tx[r][:], start=True, stop=True)
                            ins.then_inc(uz_mm, 1)
                    for r in range(2):
                        pe.wait_ge(u_act, NC_ * (r + 1))
                        pe.wait_ge(u_sb, 2)
                        if r:
                            pe.wait_ge(dbc_sb, 1)
                        for k in range(NC_):
                            ins = mm(pj[0:DR + 2 * NS, 0, 0:T], W[r]["xp"][:, k, :], u[r][:, k, :], start=k == 0,
                                     stop=k == NC_ - 1)
                        ins.then_inc(dbc_mm, 1)
                        pe.wait_ge(dbc_sb, r + 1)
                        pe.wait_ge(z_sb, 2)
                        if r:
                            pe.wait_ge(dt_abs, 2)
                            pe.wait_ge(dt_max, 2)
                        for k in range(NC_):
                            ins = mm(pj[:, 1, k * T:(k + 1) * T], W[r]["dt"][:, k * P:(k + 1) * P], dbc[r][0:DR, :],
                                     start=True, stop=True)
                        ins.then_inc(dt_mm, 1)
                    n_bc = 0
                    for r in range(2):
                        for i in range(2):
                            for m in range(NPAIR):
                                if n_bc >= 3:
                                    q = n_bc - 3
                                    rq, iq, mq = q // (2 * NPAIR), q // NPAIR % 2, q % NPAIR
                                    if iq == 0:
                                        pe.wait_ge(b_sb, rq * NPAIR + mq + 1)
                                        pe.wait_ge(hb0, rq * NPAIR + mq + 1)
                                    else:
                                        pe.wait_ge(c_sb, rq * NPAIR + mq + 1)
                                for k in range(2):
                                    row = DR + NS * i + 2 * m + k
                                    ins = mm(bc[:, n_bc % 3, k * T:(k + 1) * T],
                                             c["ident"][DR:DR + 2 * NS, row:row + 1].broadcast_to([2 * NS, P]),
                                             dbc[r][DR:DR + 2 * NS, :], start=True, stop=True, tile_position=(DR, 0))
                                ins.then_inc((b_mm, c_mm)[i], 1)
                                n_bc += 1
                        for k in range(NC_):
                            if r:
                                pe.wait_ge(y_sb, k + 1)
                            for n in range(NS):
                                m = n // 2
                                if n % 2 == 0:
                                    if k == 1 and m in POOL_PAIRS:
                                        pe.wait_ge(hc_pool, r * len(POOL_PAIRS) + POOL_PAIRS.index(m) + 1)
                                    else:
                                        own = sum(1 for x in range(m + 1) if x not in POOL_PAIRS)
                                        per = 2 * NPAIR - len(POOL_PAIRS)
                                        pe.wait_ge(hc_dve, r * per + (m + 1 if k == 0 else NPAIR + own))
                                ins = mm(yp[:, k, 0:T], c["ident"][:], h[k][:, n, :], start=n == 0, stop=n == NS - 1)
                            ins.then_inc(y_mm, 1)
                        pe.wait_ge(y_sb, NC_ * (r + 1))
                        if r:
                            pe.wait_ge(summed, 1)
                        for k in range(NC_):
                            ins = mm(op[:, 0, 0:T], W[r]["out"][:, k, :], yz[:, k, :], start=k == 0, stop=k == NC_ - 1)
                        ins.then_inc(out_mm, 1)

                @block.scalar
                def _(act):
                    ac = nc.scalar.activation
                    ac(tx[0][:], normed[:, tokens(b)], ACT.Copy).then_inc(copied, 1)
                    act.wait_ge(copied, 1)
                    ac(tx[1][:], tx[0][:, ::-1], ACT.Copy).then_inc(copied, 1)
                    for r in range(2):
                        act.wait_ge(uz_mm, 2 * r + 1)
                        ac(up[r][:, :, KC - 1:], pj[:, 0, :].rearrange("p (k t) -> p k t", k=NC_), ACT.Copy).then_inc(u_sb, 1)
                        act.wait_ge(uz_mm, 2 * r + 2)
                        ac(zs[r][:].rearrange("p k t -> p (k t)"), pj[:, 1, :], ACT.Silu).then_inc(z_sb, 1)
                    for r in range(2):
                        for k in range(NC_):
                            act.wait_ge(conved, NC_ * r + k + 1)
                            ac(u[r][:, k, :], ex[r][:, k, :], ACT.Silu, bias=W[r]["cb"][:, k:k + 1]).then_inc(u_act, 1)
                    for r in range(2):
                        act.wait_ge(dbc_mm, r + 1)
                        ac(dbc[r][:], pj[0:DR + 2 * NS, 0, 0:T], ACT.Copy).then_inc(dbc_sb, 1)
                        act.wait_ge(dt_mm, r + 1)
                        for k in range(NC_):
                            ac(ex[r][:, k, :], pj[:, 1, k * T:(k + 1) * T], ACT.Abs,
                               bias=W[r]["dtb"][:, k:k + 1]).then_inc(dt_abs, 1)
                        act.wait_ge(dt_abs, NC_ * (r + 1))
                        ac(ex[r][:], ex[r][:], ACT.Exp, scale=-1.0).then_inc(dt_exp, 1)
                        act.wait_ge(dt_exp, r + 1)
                        ac(ex[r][:], ex[r][:], ACT.Ln, bias=c["ones"][:, 0:1]).then_inc(dt_log, 1)
                    for r in range(2):
                        act.wait_ge(dt_sb, r + 1)
                        for k in range(NC_):
                            if r:
                                act.wait_ge(scanned, k + 1)
                            for n in range(NS):
                                ac(dA[k][:, n, 1:], dt[r][:, k, 1:], ACT.Exp,
                                   scale=W[r]["A"][:, k, n:n + 1]).then_inc(dA_sb, 1)
                                if k == 0 and n % 2:
                                    m = n // 2
                                    act.wait_ge(b_mm, r * NPAIR + m + 1)
                                    act.wait_ge(hb0, r * NPAIR + m + 1)
                                    if r * NPAIR + m >= 2:
                                        act.wait_ge(hb1, r * NPAIR + m - 1)
                                    ac(Bs[m % 2][:].rearrange("p k t -> p (k t)"), bc[:, (r * 2 * NPAIR + m) % 3, :],
                                       ACT.Copy).then_inc(b_sb, 1)
                                if k == 1 and n % 2:
                                    m = n // 2
                                    act.wait_ge(c_mm, r * NPAIR + m + 1)
                                    if r:
                                        act.wait_ge(hc_dve, 2 * NPAIR - len(POOL_PAIRS))
                                        act.wait_ge(hc_pool, len(POOL_PAIRS))
                                    ac(Cs[:, 2 * m:2 * m + 2, :].rearrange("p k t -> p (k t)"),
                                       bc[:, (r * 2 * NPAIR + NPAIR + m) % 3, :], ACT.Copy).then_inc(c_sb, 1)

                @block.gpsimd
                def _(pool):
                    for r in range(2):
                        pool.wait_ge(dtu_sb, r + 1)
                        for m in range(NPAIR):
                            pool.wait_ge(b_sb, r * NPAIR + m + 1)
                            if r:
                                pool.wait_ge(y_mm, 2)
                            nc.gpsimd.tensor_tensor(h[1][:, 2 * m:2 * m + 2, :], Bs[m % 2][:],
                                                    dtu[r][:, 1:2, :].broadcast_to([P, 2, T]), ALU.mult).then_inc(hb1, 1)
                        pool.wait_ge(scanned, NC_ * r + 2)
                        for m in POOL_PAIRS:
                            pool.wait_ge(c_sb, r * NPAIR + m + 1)
                            nc.gpsimd.tensor_tensor(h[1][:, 2 * m:2 * m + 2, :], h[1][:, 2 * m:2 * m + 2, :],
                                                    Cs[:, 2 * m:2 * m + 2, :], ALU.mult).then_inc(hc_pool, 1)

                @block.vector
                def _(dve):
                    link = Link(dve, step)
                    for r in range(2):
                        dve.wait_ge(u_sb, r + 1)
                        for k in range(NC_):
                            w = W[r]["conv"]
                            link(nc.vector.tensor_scalar(ex[r][:, k, :], up[r][:, k, 0:T], w[:, k, 0:1], None, ALU.mult))
                            for j in range(1, KC):
                                ins = nc.vector.scalar_tensor_tensor(out=ex[r][:, k, :], in0=up[r][:, k, j:j + T],
                                                                     scalar=w[:, k, j:j + 1], in1=ex[r][:, k, :],
                                                                     op0=ALU.mult, op1=ALU.add)
                                if j < KC - 1:
                                    link(ins)
                            ins.then_inc(conved, 1)
                    for r in range(2):
                        dve.wait_ge(dt_abs, NC_ * (r + 1))
                        for k in range(NC_):
                            nc.vector.tensor_scalar(dt[r][:, k, :], pj[:, 1, k * T:(k + 1) * T], W[r]["dtb"][:, k:k + 1],
                                                    0.0, ALU.add, ALU.max).then_inc(dt_max, 1)
                        dve.wait_ge(dt_max, NC_ * (r + 1))
                        dve.wait_ge(dt_log, r + 1)
                        nc.vector.tensor_tensor(dt[r][:], dt[r][:], ex[r][:], ALU.add).then_inc(dt_sb, 1)
                        dve.wait_ge(dt_sb, r + 1)
                        dve.wait_ge(u_act, NC_ * (r + 1))
                        nc.vector.tensor_tensor(dtu[r][:], dt[r][:], u[r][:], ALU.mult).then_inc(dtu_sb, 1)
                    for r in range(2):
                        dve.wait_ge(dtu_sb, r + 1)
                        for m in range(NPAIR):
                            dve.wait_ge(b_mm, r * NPAIR + m + 1)
                            if r:
                                dve.wait_ge(y_mm, 1)
                            nc.vector.tensor_tensor(h[0][:, 2 * m:2 * m + 2, :],
                                                    bc[:, (r * 2 * NPAIR + m) % 3, :].rearrange("p (k t) -> p k t", k=2),
                                                    dtu[r][:, 0:1, :].broadcast_to([P, 2, T]), ALU.mult).then_inc(hb0, 1)
                        for k in range(NC_):
                            dve.wait_ge((hb0, hb1)[k], (r + 1) * NPAIR)
                            dve.wait_ge(dA_sb, (NC_ * r + k + 1) * NS)
                            flat = h[k][:].rearrange("p n t -> p (n t)")
                            nc.vector.tensor_tensor_scan(flat, dA[k][:].rearrange("p n t -> p (n t)"), flat, 0.0, ALU.mult,
                                                         ALU.add).then_inc(scanned, 1)
                            dve.wait_ge(scanned, NC_ * r + k + 1)
                            for m in range(NPAIR):
                                if k == 1 and m in POOL_PAIRS:
                                    continue
                                dve.wait_ge(c_sb, r * NPAIR + m + 1)
                                nc.vector.tensor_tensor(h[k][:, 2 * m:2 * m + 2, :], h[k][:, 2 * m:2 * m + 2, :],
                                                        Cs[:, 2 * m:2 * m + 2, :], ALU.mult).then_inc(hc_dve, 1)
                        for k in range(NC_):
                            dve.wait_ge(y_mm, NC_ * r + k + 1)
                            if r:
                                dve.wait_ge(out_mm, 1)
                            link(nc.vector.scalar_tensor_tensor(out=yz[:, k, :], in0=u[r][:, k, :],
                                                                scalar=W[r]["D"][:, k:k + 1], in1=yp[:, k, 0:T],
                                                                op0=ALU.mult, op1=ALU.add))
                            nc.vector.tensor_tensor(yz[:, k, :], yz[:, k, :], zs[r][:, k, :], ALU.mult).then_inc(y_sb, 1)
                        dve.wait_ge(out_mm, r + 1)
                        if r == 0:
                            nc.vector.tensor_tensor(sum_[:], xn[:, tokens(b)], op[:, 0, 0:T], ALU.add).then_inc(summed, 1)
                        else:
                            dve.wait_ge(summed, 1)
                            nc.vector.tensor_tensor(s_out[:, tokens(b)], sum_[:], op[:, 0, 0:T][:, ::-1], ALU.add)
            s.barrier()


def l3_ffn(nc, c, d, xn, g_out):
    E, F, TOPK = 16, 176, 2
    CAP = int(np.ceil(1.25 * xn.shape[1] * TOPK / E))
    FH = F // 2
    NE = E + 1
    with Scope(nc, "f3") as s:
        wg, wu = s.sb("w_gate", [P, NE, F]), s.sb("w_up", [P, NE, F])
        wd = s.sb("w_down", [FH, NE, 2, P])
        rw, rb = s.sb("router_w", [P, E]), s.sb("router_b", [1, E])
        load(nc, s, [(wg[:, 0:E, :], d["w_gate"].rearrange("e p f -> p e f")), (wg[:, E, :], d["sw_gate"]),
                     (wu[:, 0:E, :], d["w_up"].rearrange("e p f -> p e f")), (wu[:, E, :], d["sw_up"]),
                     (wd[:, 0:E].rearrange("p e a n -> p (e a) n"),
                      d["w_down"].rearrange("e (a p) n -> p (e a) n", p=FH)),
                     (wd[:, E], d["sw_down"].rearrange("(a p) n -> p a n", p=FH)),
                     (rw[:], d["router_w"]), (rb[:], d["router_b"].rearrange("(a n) -> a n", a=1))])
        iota = make_iota(nc, s, E)
        tile_x = s.sb("x", [P, T])
        nmax, psum_, pinv = s.sb("neg_max", [P, 2]), s.sb("prob_sum", [P, 2]), s.sb("prob_inv", [P, 2])
        probs, chosen = s.sb("probs", [P, 2, E]), s.sb("chosen", [P, 2, E])
        m8, idx, idf = s.sb("top8", [P, 2, 8]), s.sb("idx", [P, 2, 8], U32), s.sb("idx_f", [P, 2, 8])
        gate = s.sb("gate", [P, 2, NE])
        seen = s.sb("seen", [P, E])
        NHB = 3
        sg = s.sb("silu", [FH, NHB, 2, T])
        hm = s.sb("hidden", [FH, NHB, 2, T])
        acc = s.sb("acc", [P, 2, P])
        gp, upp, op = s.banks("gate", 2), s.banks("up", 2), s.banks("o", 2)
        lp, cp = s.banks("logits", 1), s.banks("count", 1)
        copied, log_mm, maxed, exped, step, picked, cnt_mm, g_mm, u_mm, silued, hidden, o_mm, added, acc_mm = s.sems(
            "copied log_mm maxed exped step picked cnt_mm g_mm u_mm silued hidden o_mm added acc_mm")
        with nc.Block() as block:
            @block.vector
            def _(dve):
                nc.vector.memset(seen[:], 0.0)
                nc.vector.memset(gate[:], 1.0)
        s.barrier()
        with nc.Fori(0, xn.shape[1] // T) as b:
            with nc.Block() as block:
                order = [E] + list(range(E))

                @block.tensor
                def _(pe):
                    mm = nc.tensor.matmul
                    pe.wait_ge(copied, 1)
                    for t in range(2):
                        o = lp[:, 0, t * E:(t + 1) * E]
                        mm(o, tile_x[:, t * P:(t + 1) * P], rw[:], start=True, stop=False)
                        ins = mm(o, c["ones"][0:1, :], rb[:], start=False, stop=True)
                    ins.then_inc(log_mm, 1)

                    def raise_(i):
                        e = order[i]
                        for w, ps, done, used in ((wg, gp, g_mm, silued), (wu, upp, u_mm, hidden)):
                            if i >= 2:
                                pe.wait_ge(used, i - 1)
                            for a in range(2):
                                ins = mm(ps[0:FH, i % 2, a * T:(a + 1) * T], w[:, e, a * FH:(a + 1) * FH], tile_x[:],
                                         start=True, stop=True)
                            ins.then_inc(done, 1)

                    def lower(i):
                        e = order[i]
                        pe.wait_ge(hidden, i + 1)
                        if i >= 2:
                            pe.wait_ge(added, 2 * (i - 1))
                        for t in range(2):
                            for a in range(2):
                                ins = mm(op[:, i % 2, t * P:(t + 1) * P], hm[:, i % NHB, a, t * P:(t + 1) * P],
                                         wd[:, e, a, :], start=a == 0, stop=a == 1)
                        ins.then_inc(o_mm, 1)

                    for i in range(NE + 1):
                        if i < NE:
                            raise_(i)
                        if i == 1:
                            pe.wait_ge(picked, 2)
                            mm(cp[:, 0, 0:E], c["earlier"][:], chosen[:, 0, :], start=True, stop=False)
                            mm(cp[:, 0, 0:E], c["mean"][:], seen[:], start=False, stop=True)
                            mm(cp[:, 0, E:2 * E], c["earlier"][:], chosen[:, 1, :], start=True, stop=False)
                            mm(cp[:, 0, E:2 * E], c["mean"][:], seen[:], start=False, stop=False)
                            mm(cp[:, 0, E:2 * E], c["ones"][:], chosen[:, 0, :], start=False, stop=True)
                            for t in range(2):
                                ins = mm(cp[:, 0, 2 * E:3 * E], c["ones"][:], chosen[:, t, :], start=t == 0, stop=t == 1)
                            ins.then_inc(cnt_mm, 1)
                        if i >= 1:
                            lower(i - 1)
                    pe.wait_ge(added, 2 * NE)
                    for t in range(2):
                        ins = nc.tensor.transpose(op[:, 0, t * P:(t + 1) * P], acc[:, t, :], c["ident"][:])
                    ins.then_inc(acc_mm, 1)

                @block.scalar
                def _(act):
                    nc.scalar.activation(tile_x[:], xn[:, tokens(b)], ACT.Copy).then_inc(copied, 1)
                    for t in range(2):
                        act.wait_ge(maxed, 1)
                        nc.scalar.activation(probs[:, t, :], lp[:, 0, t * E:(t + 1) * E], ACT.Exp, bias=nmax[:, t:t + 1],
                                             accum_out=psum_[:, t:t + 1]).then_inc(exped, 1)
                    for i in range(NE):
                        act.wait_ge(g_mm, i + 1)
                        if i >= NHB:
                            act.wait_ge(hidden, i - NHB + 1)
                        nc.scalar.activation(sg[:, i % NHB].rearrange("p a t -> p (a t)"), gp[0:FH, i % 2, :],
                                             ACT.Silu).then_inc(silued, 1)

                @block.vector
                def _(dve):
                    link = Link(dve, step)
                    tt, ts = nc.vector.tensor_tensor, nc.vector.tensor_scalar
                    dve.wait_ge(log_mm, 1)
                    nc.vector.tensor_reduce(out=nmax[:], in_=lp[:, 0, 0:2 * E].rearrange("p (t e) -> p t e", t=2),
                                            axis=AX_X, op=ALU.max, negate=True).then_inc(maxed, 1)
                    dve.wait_ge(exped, 2)
                    link(nc.vector.reciprocal(pinv[:], psum_[:]))
                    for t in range(2):
                        link(ts(probs[:, t, :], probs[:, t, :], pinv[:, t:t + 1], None, ALU.mult))
                        top_experts(nc, link, m8[:, t, :], idx[:, t, :], idf[:, t, :], iota[:], chosen[:, t, :],
                                    probs[:, t, :], TOPK)
                        link(nc.vector.tensor_tensor_reduce(out=gate[:, t, 0:E], in0=chosen[:, t, :], in1=probs[:, t, :],
                                                            scale=1.0, scalar=0.0, op0=ALU.mult, op1=ALU.add,
                                                            accum_out=pinv[:, t:t + 1]))
                        link(ts(pinv[:, t:t + 1], pinv[:, t:t + 1], 1e-9, None, ALU.add))
                        link(nc.vector.reciprocal(pinv[:, t:t + 1], pinv[:, t:t + 1]))
                        ts(gate[:, t, 0:E], gate[:, t, 0:E], pinv[:, t:t + 1], None, ALU.mult).then_inc(picked, 1)

                    def combine(i):
                        e = order[i]
                        dve.wait_ge(o_mm, i + 1)
                        for t in range(2):
                            o = op[:, i % 2, t * P:(t + 1) * P]
                            if i == 0:
                                ins = nc.vector.tensor_copy(acc[:, t, :], o)
                            else:
                                dve.wait_ge(added, 2 * (i - 1) + t + 1)
                                ins = nc.vector.scalar_tensor_tensor(out=acc[:, t, :], in0=o, scalar=gate[:, t, e:e + 1],
                                                                     in1=acc[:, t, :], op0=ALU.mult, op1=ALU.add)
                            ins.then_inc(added, 1)

                    for i in range(NE + 1):
                        if i < NE:
                            dve.wait_ge(silued, i + 1)
                            dve.wait_ge(u_mm, i + 1)
                            if i >= NHB:
                                dve.wait_ge(o_mm, i - NHB + 1)
                            tt(hm[:, i % NHB].rearrange("p a t -> p (a t)"), sg[:, i % NHB].rearrange("p a t -> p (a t)"),
                               upp[0:FH, i % 2, :], ALU.mult).then_inc(hidden, 1)
                        if i == 1:
                            dve.wait_ge(cnt_mm, 1)
                            link(nc.vector.scalar_tensor_tensor(
                                out=gate[:, :, 0:E], in0=cp[:, 0, 0:2 * E].rearrange("p (t e) -> p t e", t=2),
                                scalar=float(CAP), in1=gate[:, :, 0:E], op0=ALU.is_lt, op1=ALU.mult))
                            link(tt(seen[:], seen[:], cp[:, 0, 2 * E:3 * E], ALU.add))
                        if i >= 1:
                            combine(i - 1)
                    dve.wait_ge(acc_mm, 1)
                    tt(g_out[:, tokens(b)], xn[:, tokens(b)], op[:, 0, 0:T], ALU.add)
            s.barrier()


TRANSPOSED = {
    "L0_attn_relpos_table", "L1_attn_W_q", "L1_attn_W_k", "L1_attn_W_v", "L1_ffn_slot_init", "L1_ffn_Wih", "L1_ffn_Whh",
    "L2_ffn_wp", "L3_attn_f_in_w", "L3_attn_f_xproj_w", "L3_attn_f_dt_w", "L3_attn_f_out_w", "L3_attn_b_in_w",
    "L3_attn_b_xproj_w", "L3_attn_b_dt_w", "L3_attn_b_out_w",
}


def build(nc, d, out):
    def part(prefix):
        return {k[len(prefix) + 1:]: v for k, v in d.items() if k.startswith(prefix + "_")}
    n = out.shape[1]
    with Scope(nc, "main") as m:
        x, xn, s, g = (m.sb(name, [P, n]) for name in ("x", "xn", "s", "g"))
        c = make_constants(nc, m)
        load(nc, m, [(x[:], d["x"])])
        gate_and_norm(nc, c, x, xn)
        l0_attention(nc, c, part("L0_attn"), xn, s)
        l0_ffn(nc, c, part("L0_ffn"), xn, g)
        gate_and_norm(nc, c, x, xn, s, g, gate=True)
        l1_attention(nc, c, part("L1_attn"), xn, s)
        l1_ffn(nc, c, part("L1_ffn"), xn, g)
        gate_and_norm(nc, c, x, xn, s, g, gate=True)
        l2_attention(nc, c, part("L2_attn"), xn, s)
        l2_ffn(nc, c, part("L2_ffn"), xn, g)
        gate_and_norm(nc, c, x, xn, s, g, gate=True)
        l3_attention(nc, c, part("L3_attn"), xn, s, g)
        l3_ffn(nc, c, part("L3_ffn"), xn, g)
        gate_and_norm(nc, c, x, xn, s, g, gate=True, norm=False, out=out)


def kernel(**inputs):
    import concourse.bacc as bacc
    from concourse.bass_utils import run_bass_kernel_spmd as run

    nc = bacc.Bacc("TRN2", target_bir_lowering=False, num_devices=1)
    x = np.asarray(inputs["L0_attn_x"])
    nb, t, f = x.shape
    arrays = {"x": np.ascontiguousarray(x.reshape(nb * t, f).T), "L2_ffn_trig": l2_ffn_tables(t)}
    for name, a in inputs.items():
        if name == "L0_attn_x":
            continue
        a = np.asarray(a)
        arrays[name + "T" if name in TRANSPOSED else name] = np.ascontiguousarray(a.T if name in TRANSPOSED else a)
    d = {k: nc.dram_tensor(k, a.shape, mybir.dt.from_np(a.dtype), kind="ExternalInput").ap() for k, a in arrays.items()}
    out = nc.dram_tensor("out", (f, nb * t), F32, kind="ExternalOutput").ap()
    build(nc, d, out)
    r = run(nc, [arrays], core_ids=[0])
    return np.ascontiguousarray(r.results[0]["out"].T).reshape(nb, t, f)
```

```python
from contextlib import ExitStack

import numpy as np

import concourse.bass as bass
from concourse import mybir

F32 = mybir.dt.float32
U32 = mybir.dt.uint32
BF16 = mybir.dt.bfloat16
ALU = mybir.AluOpType
ACT = mybir.ActivationFunctionType
AX_X = mybir.AxisListType.X

P = 128
T = 256
NB = 16
H = 16
BANK = 512
LN_EPS = 1e-5
MASKED = -1e30


class Scope:

    def __init__(self, nc, name):
        self.nc, self.name, self.ctx, self.nums = nc, f"{name}_{nc.next_id()}", ExitStack(), []

    def __enter__(self):
        return self

    def __exit__(self, *e):
        self.ctx.__exit__(*e)
        self.nc.reset_free_semaphores(sorted(self.nc.free_semaphores))

    def sb(self, name, shape, dt=F32):
        return self.ctx.enter_context(self.nc.sbuf_tensor(f"{self.name}_{name}", shape, dt))

    def banks(self, name, n=1):
        return self.ctx.enter_context(self.nc.psum_tensor(f"{self.name}_{name}_psum", [P, n, BANK], F32))

    def sems(self, names):
        got = [self.ctx.enter_context(self.nc.semaphore(f"{self.name}_{n}")) for n in names.split()]
        self.nums += [s.num for s in got]
        return got[0] if len(got) == 1 else got

    def barrier(self):
        lo, hi = min(self.nums), max(self.nums)
        assert hi - lo + 1 == len(self.nums), self.nums
        self.nc.all_engine_barrier(sems_to_clear=range(lo, hi + 1))


class Link:

    def __init__(self, engine, sem):
        self.engine, self.sem, self.n = engine, sem, 0

    def __call__(self, ins):
        self.n += 1
        ins.then_inc(self.sem, 1)
        self.engine.wait_ge(self.sem, self.n)


def tokens(b, n=T):
    return bass.ds(b * n, n)


def make_constants(nc, scope):
    c = {
        "mean": scope.sb("mean", [P, P]), "ones": scope.sb("ones", [P, P]), "ident": scope.sb("ident", [P, P]),
        "earlier": scope.sb("earlier", [P, P]), "eps": scope.sb("eps", [P, 1]),
    }
    with Scope(nc, "const") as s:
        filled = s.sems("filled")
        with nc.Block() as block:
            @block.gpsimd
            def _(pool):
                nc.gpsimd.memset(c["mean"][:], 1.0 / P)
                nc.gpsimd.memset(c["ones"][:], 1.0)
                nc.gpsimd.memset(c["eps"][:], LN_EPS)
                nc.gpsimd.memset(c["ident"][:], 0.0)
                nc.gpsimd.memset(c["earlier"][:], 1.0).then_inc(filled, 1)
                pool.wait_ge(filled, 1)
                nc.gpsimd.affine_select(out=c["ident"][:], in_=c["ident"][:], compare_op=ALU.not_equal, fill=1.0,
                                        base=0, pattern=[[-1, P]], channel_multiplier=1)
                nc.gpsimd.affine_select(out=c["earlier"][:], in_=c["earlier"][:], compare_op=ALU.is_gt, fill=0.0,
                                        base=0, pattern=[[1, P]], channel_multiplier=-1).then_inc(filled, 1)
        s.barrier()
    return c


def load(nc, scope, pairs):
    with Scope(nc, scope.name + "_load") as s:
        landed = s.sems("landed")
        with nc.Block() as block:
            @block.sync
            def _(sp):
                for dst, src in pairs:
                    sp.dma_start(dst, src, allow_slow_non_contiguous=True).then_inc(landed, 16)
                sp.wait_ge(landed, 16 * len(pairs))
        s.barrier()


def column(v):
    return v.rearrange("(c p) -> p c", p=min(P, v.shape[0]))


def gate_and_norm(nc, c, x, xn, s=None, g=None, gate=False, norm=True, out=None, affine=None):
    W = BANK
    N = x.shape[1] // W
    NBUF, NPS = 3, 4
    with Scope(nc, "norm") as q:
        if norm:
            sq = q.sb("squares", [P, NBUF, W])
            rs = q.sb("inv_dev", [P, N, W])
            mean = q.banks("mean", NPS)
            var = q.banks("var", NPS)
        gated, mixed, x_new, mean_ready, centered, squared, var_ready, logged, rooted, normed, stored = q.sems(
            "gated mixed x_new mean_ready centered squared var_ready logged rooted normed stored")

        def cols(k):
            return slice(k * W, (k + 1) * W)
        with nc.Block() as block:
            @block.scalar
            def _(act):
                if gate:
                    for k in range(N):
                        nc.scalar.activation(g[:, cols(k)], g[:, cols(k)], ACT.Silu).then_inc(gated, 1)
                if norm:
                    def take_log(k):
                        act.wait_ge(var_ready, k + 1)
                        nc.scalar.activation(rs[:, k, :], var[:, k % NPS, :], ACT.Ln, bias=c["eps"][:]).then_inc(logged, 1)
                    for k in range(N + 1):
                        if k < N:
                            act.wait_ge(centered, k + 1)
                            if k >= NBUF:
                                act.wait_ge(var_ready, k - NBUF + 1)
                            nc.scalar.activation(sq[:, k % NBUF, :], xn[:, cols(k)], ACT.Square).then_inc(squared, 1)
                        if k >= 1:
                            take_log(k - 1)
                    for k in range(N):
                        act.wait_ge(logged, k + 1)
                        nc.scalar.activation(rs[:, k, :], rs[:, k, :], ACT.Exp, scale=-0.5).then_inc(rooted, 1)

            @block.vector
            def _(dve):
                if gate:
                    for k in range(N):
                        dve.wait_ge(gated, k + 1)
                        nc.vector.tensor_tensor(g[:, cols(k)], g[:, cols(k)], s[:, cols(k)], ALU.mult).then_inc(mixed, 1)
                        dve.wait_ge(mixed, k + 1)
                        nc.vector.tensor_tensor(x[:, cols(k)], x[:, cols(k)], g[:, cols(k)], ALU.add).then_inc(x_new, 1)
                if norm:
                    for k in range(N):
                        if gate:
                            dve.wait_ge(x_new, k + 1)
                        dve.wait_ge(mean_ready, k + 1)
                        nc.vector.tensor_tensor(xn[:, cols(k)], x[:, cols(k)], mean[:, k % NPS, :],
                                                ALU.subtract).then_inc(centered, 1)
                    for k in range(N):
                        dve.wait_ge(rooted, k + 1)
                        nc.vector.tensor_tensor(xn[:, cols(k)], xn[:, cols(k)], rs[:, k, :], ALU.mult).then_inc(normed, 1)
                        if affine is not None:
                            dve.wait_ge(normed, k + 1)
                            nc.vector.tensor_scalar(xn[:, cols(k)], xn[:, cols(k)], affine[0], affine[1], ALU.mult,
                                                    ALU.add)

            if norm:
                @block.tensor
                def _(pe):
                    def variance(k):
                        pe.wait_ge(squared, k + 1)
                        if k >= NPS:
                            pe.wait_ge(logged, k - NPS + 1)
                        nc.tensor.matmul(var[:, k % NPS, :], c["mean"][:], sq[:, k % NBUF, :], start=True,
                                         stop=True).then_inc(var_ready, 1)
                    for k in range(N + 1):
                        if k < N:
                            if gate:
                                pe.wait_ge(x_new, k + 1)
                            if k >= NPS:
                                pe.wait_ge(centered, k - NPS + 1)
                            nc.tensor.matmul(mean[:, k % NPS, :], c["mean"][:], x[:, cols(k)], start=True,
                                             stop=True).then_inc(mean_ready, 1)
                        if k >= 1:
                            variance(k - 1)

            if out is not None:
                @block.sync
                def _(sp):
                    for k in range(N):
                        sp.wait_ge(x_new, k + 1)
                        sp.dma_start(out[:, cols(k)], x[:, cols(k)]).then_inc(stored, 16)
                    sp.wait_ge(stored, 16 * N)
        q.barrier()


def load_padded_columns(nc, scope, pairs):
    with Scope(nc, scope.name + "_pad") as s:
        zeroed, landed = s.sems("zeroed landed")
        with nc.Block() as block:
            @block.gpsimd
            def _(pool):
                for i, (dst, _) in enumerate(pairs):
                    nc.gpsimd.memset(dst, 0.0).then_inc(zeroed, 1)

            @block.sync
            def _(sp):
                sp.wait_ge(zeroed, len(pairs))
                for dst, src in pairs:
                    v = src.rearrange("(j g d) -> g d j", j=4, g=4)
                    for g in range(4):
                        sp.dma_start(dst[32 * g:32 * g + 8, :], v[g], allow_slow_non_contiguous=True).then_inc(landed, 16)
                sp.wait_ge(landed, 64 * len(pairs))
        s.barrier()


def pad_heads(nc, dst, src):
    return nc.vector.tensor_copy(dst.rearrange("p j (g e) -> p (j g) e", g=4)[:, :, 0:8],
                                 src.rearrange("p (h d) -> p h d", d=8))


def l0_attention(nc, c, d, xn, s_out):
    WIN, HD = 64, 8
    ROW = 3 * WIN
    SC = 1.0 / float(np.sqrt(HD * 3.0))
    with Scope(nc, "a0") as s:
        names = ["Wq", "Wk", "Wv", "Wo", "Wrk", "Wrq"]
        w = {n: s.sb(n, [P, P]) for n in names}
        wp = {n: s.sb(n + "_padded", [P, 4, P]) for n in ["Wq", "Wk", "Wrk", "Wrq"]}
        vec = s.sb("vectors", [P, 4])
        cols = {n: s.sb(n, [P, 4]) for n in ["bq", "bk", "brk", "brq", "shift_q", "shift_k"]}
        rel = s.sb("relpos", [P, WIN])
        rel2 = s.sb("relpos2", [P, WIN])
        rt = {"k": s.sb("rk", [P, 4, WIN]), "q": s.sb("rq", [P, 4, WIN])}
        rb = {"k": s.sb("rk_blocks", [P, 4, 4, WIN]), "q": s.sb("rq_blocks", [P, 4, 4, WIN])}
        zero = s.sb("zero", [P, 2 * ROW])
        band_rows = nc.dram_tensor("a0_band_rows", (2, H, T, ROW), F32).ap()
        pj = s.banks("project", 4)
        load(nc, s, [(w[n][:], d[n]) for n in names] + [(vec[:, 0:1], column(d["bv"])), (vec[:, 1:2], column(d["bo"])),
             (vec[:, 2:3], column(d["ln_gamma"])), (vec[:, 3:4], column(d["ln_beta"])), (rel[:], d["relpos_tableT"])])
        load_padded_columns(nc, s, [(cols[n][:], d[n]) for n in ["bq", "bk", "brk", "brq"]])
        with Scope(nc, "a0t") as t:
            step, zeroed, table, zeros_out = t.sems("step zeroed table zeros_out")
            mm = t.sems("mm")
            with nc.Block() as block:
                @block.gpsimd
                def _(pool):
                    for n in wp:
                        nc.gpsimd.memset(wp[n][:], 0.0)
                    for n in rb:
                        nc.gpsimd.memset(rb[n][:], 0.0)
                    nc.gpsimd.memset(zero[:], 0.0).then_inc(zeroed, 1)

                @block.sync
                def _(sp):
                    sp.wait_ge(zeroed, 1)
                    for kind in range(2):
                        for h in range(H):
                            sp.dma_start(band_rows[kind, h].rearrange("(p r) e -> p (r e)", p=P),
                                         zero[:]).then_inc(zeros_out, 16)
                    sp.wait_ge(zeros_out, 16 * 2 * H)

                @block.tensor
                def _(pe):
                    nc.tensor.matmul(pj[:, 0, 0:WIN], c["mean"][:], rel[:], start=True, stop=True).then_inc(mm, 1)
                    pe.wait_ge(table, 1)
                    nc.tensor.matmul(pj[:, 1, 0:WIN], c["mean"][:], rel2[:], start=True, stop=True).then_inc(mm, 1)
                    pe.wait_ge(table, 2)
                    for n, (a, wn) in enumerate((("k", "Wrk"), ("q", "Wrq"))):
                        for j in range(4):
                            nc.tensor.matmul(pj[:, 2 + n, j * WIN:(j + 1) * WIN], wp[wn][:, j, :], rel[:],
                                             start=True, stop=True).then_inc(mm, 1)

                @block.scalar
                def _(act):
                    act.wait_ge(mm, 2)
                    nc.scalar.activation(rel2[:], pj[:, 1, 0:WIN], ACT.Sqrt, bias=c["eps"][:]).then_inc(zeroed, 1)

                @block.vector
                def _(dve):
                    link = Link(dve, step)
                    dve.wait_ge(zeroed, 1)
                    for n in wp:
                        pad_heads(nc, wp[n][:], w[n][:])
                    dve.wait_ge(mm, 1)
                    link(nc.vector.tensor_tensor(rel[:], rel[:], pj[:, 0, 0:WIN], ALU.subtract))
                    nc.vector.tensor_tensor(rel2[:], rel[:], rel[:], ALU.mult).then_inc(table, 1)
                    dve.wait_ge(zeroed, 2)
                    link(nc.vector.reciprocal(rel2[:], rel2[:]))
                    link(nc.vector.tensor_tensor(rel[:], rel[:], rel2[:], ALU.mult))
                    nc.vector.tensor_scalar(rel[:], rel[:], vec[:, 2:3], vec[:, 3:4], ALU.mult,
                                            ALU.add).then_inc(table, 1)
                    dve.wait_ge(mm, 10)
                    for n, (a, bias, sum_) in enumerate((("k", "brk", "shift_k"), ("q", "brq", "shift_q"))):
                        tab = pj[:, 2 + n, 0:4 * WIN].rearrange("p (j w) -> p j w", j=4)
                        link(nc.vector.tensor_copy(rt[a][:], tab))
                        link(nc.vector.tensor_tensor(cols[sum_][:], cols[bias][:], rt[a][:, :, 0], ALU.add))
                        for g in range(4):
                            r = slice(32 * g, 32 * g + 32)
                            e = rt[a][r, :, :]
                            if a == "q":
                                e = e[:, :, ::-1]
                            link(nc.vector.tensor_tensor(rb[a][r, :, g, :], e,
                                                         rt[a][r, :, 0:1].broadcast_to([32, 4, WIN]), ALU.subtract))
            t.barrier()

        R, QUART = 2, H // 4
        tile_x = s.sb("x", [P, T])
        qT, kT = s.sb("qT", [P, 4, T]), s.sb("kT", [P, 4, T])
        qA, kA = ([s.sb(f"{n}{r}", [P, 4, T]) for r in range(R)] for n in ("qA", "kA"))
        v = [s.sb(f"v{r}", [P, 2, P]) for r in range(R)]
        band = s.sb("band", [P, 4, H * WIN])
        A = [s.sb("A0", [P, H, P]), s.sb("A1", [P, H, T])]
        B = [s.sb("B0", [P, H, ROW]), s.sb("B1", [P, H, P])]
        NL, NP_, NT = 3, 3, 3
        lg = s.sb("logits", [P, NL, T])
        pr = s.sb("probs", [P, NP_, T])
        pt = s.sb("probs_T", [P, NT, T])
        nmax = s.sb("neg_max", [P, R * 2 * H])
        rsum = s.sb("row_sum", [P, R * 2 * H])
        rinv = s.sb("row_inv", [P, R * 2 * H])
        on = s.sb("o_normed", [P, 2, P])
        oT = s.sb("oT", [P, T])
        ob = s.banks("out", 2)
        fin = s.banks("final", 1)
        (copied, q_mm, k_mm, q_ready, k_ready, shifted, v_mm, v_ready, band_mm, band_lo, band_hi, qb_out, kb_out,
         first_in, next_A0_in, masked, logit_mm, logits, probs, tr_mm, tr_sb, pv_mm, inv, normed, oT_mm, oT_sb, wo_mm,
         taken, *next_in) = s.sems(
            "copied q_mm k_mm q_ready k_ready shifted v_mm v_ready band_mm band_lo band_hi qb_out kb_out first_in "
            "next_A0_in masked logit_mm logits probs tr_mm tr_sb pv_mm inv normed oT_mm oT_sb wo_mm taken "
            "next_in0 next_in1 next_in2 next_in3")
        units = [(r, h, t) for r in range(R) for t in range(2) for h in range(H)]
        PERSEQ = 2 * H
        NU = len(units)

        with nc.Block() as block:
            @block.gpsimd
            def _(pool):
                nc.gpsimd.memset(A[1][:], 0.0)
        s.barrier()
        with nc.Fori(0, xn.shape[1] // (R * T)) as b:
            with nc.Block() as block:
                def seq(r):
                    return bass.ds((b * R + r) * T, T)

                def evac(eng, u):
                    _, h, t = units[u]
                    nk = P * (t + 1)
                    eng.wait_ge(tr_mm, u + 1)
                    if u >= NT:
                        eng.wait_ge(pv_mm, u - NT + 1)
                    if u:
                        eng.wait_ge(tr_sb, u)
                    if u % 2:
                        ins = nc.scalar.activation(pt[:, u % NT, 0:nk], pj[:, 2 + u % 2, 0:nk], ACT.Copy)
                    else:
                        ins = nc.vector.tensor_copy(pt[:, u % NT, 0:nk], pj[:, 2 + u % 2, 0:nk])
                    ins.then_inc(tr_sb, 1)

                @block.tensor
                def _(pe):
                    for r in range(R):
                        for kind, n in enumerate(["Wq", "Wk"]):
                            if r:
                                pe.wait_ge(band_lo, 4 * r - 1 + kind)
                                pe.wait_ge(band_hi, 4 * r - 1 + kind)
                            for j in range(4):
                                nc.tensor.matmul(pj[:, 2 * kind + j // 2, (j % 2) * T:(j % 2 + 1) * T], wp[n][:, j, :],
                                                 xn[:, seq(r)], start=True, stop=True).then_inc((q_mm, k_mm)[kind], 1)
                        pe.wait_ge(copied, r + 1)
                        if r:
                            pe.wait_ge(v_ready, r)
                        for t in range(2):
                            nc.tensor.matmul(fin[:, 0, t * P:(t + 1) * P], tile_x[:, t * P:(t + 1) * P], w["Wv"][:],
                                             start=True, stop=True).then_inc(v_mm, 1)
                        for n, (kind, t) in enumerate([(0, 0), (0, 1), (1, 0), (1, 1)]):
                            src, tab = (qT, rb["k"]) if kind == 0 else (kT, rb["q"])
                            pe.wait_ge((q_ready, k_ready)[kind], 4 * (r + 1))
                            if n == 0:
                                pe.wait_ge(k_ready, 4 * (r + 1))
                            if n >= 2:
                                pe.wait_ge(band_lo, 4 * r + n - 1)
                                pe.wait_ge(band_hi, 4 * r + n - 1)
                            for j in range(4):
                                nc.tensor.matmul(pj[:, 2 * (n % 2) + j // 2, (j % 2) * T:(j % 2 + 1) * T],
                                                 src[:, j, t * P:(t + 1) * P], tab[:, j].rearrange("p g w -> p (g w)"),
                                                 start=True, stop=True).then_inc(band_mm, 1)
                    pe.wait_ge(band_lo, 4 * R)
                    pe.wait_ge(band_hi, 4 * R)

                    def logit(u):
                        s_, h, t = units[u]
                        r, j = slice(32 * (h % 4), 32 * (h % 4) + 32), h // 4
                        nk = P * (t + 1)
                        if u >= 2:
                            pe.wait_ge(logits, u - 1)
                        if s_:
                            pe.wait_ge(next_in[h // QUART], 48)
                        dst = pj[:, u % 2, :]
                        nc.tensor.matmul(dst[:, 0:nk], qA[s_][r, j, t * P:(t + 1) * P], kA[s_][r, j, 0:nk], start=True,
                                         stop=False, tile_position=(32 * (h % 4), 0))
                        if t == 1:
                            nc.tensor.matmul(dst[0:64, 0:P], B[0][:, h, P:P + 64], c["ident"][:], start=False, stop=False)
                        nc.tensor.matmul(dst[:, t * P:nk], B[t][:, h, 0:P], c["ident"][:], start=False,
                                         stop=True).then_inc(logit_mm, 1)

                    def transpose(u):
                        _, h, t = units[u]
                        pe.wait_ge(probs, u + 1)
                        if u >= 2:
                            pe.wait_ge(tr_sb, u - 1)
                        for kt in range(t + 1):
                            ins = nc.tensor.transpose(pj[:, 2 + u % 2, kt * P:(kt + 1) * P],
                                                      pr[:, u % NP_, kt * P:(kt + 1) * P], c["ident"][:])
                        ins.then_inc(tr_mm, 1)

                    def weigh(u):
                        s_, h, t = units[u]
                        pe.wait_ge(tr_sb, u + 1)
                        if s_ and h == 0:
                            pe.wait_ge(normed, 2 * (s_ - 1) + t + 1)
                        for kt in range(t + 1):
                            ins = nc.tensor.matmul(ob[:, t, 8 * h:8 * h + 8],
                                                   pt[:, u % NT, kt * P:(kt + 1) * P], v[s_][:, kt, 8 * h:8 * h + 8],
                                                   start=kt == 0, stop=kt == t)
                        ins.then_inc(pv_mm, 1)

                    def turn_out(r):
                        if r:
                            pe.wait_ge(taken, r)
                        for t in range(2):
                            pe.wait_ge(normed, 2 * r + t + 1)
                            nc.tensor.transpose(fin[:, 0, t * P:(t + 1) * P], on[:, t, :], c["ident"][:]).then_inc(oT_mm, 1)

                    def project_out(r):
                        pe.wait_ge(oT_sb, r + 1)
                        nc.tensor.matmul(fin[:, 0, T:2 * T], w["Wo"][:], oT[:], start=True, stop=True).then_inc(wo_mm, 1)

                    pe.wait_ge(first_in, 64)
                    pe.wait_ge(v_ready, R)
                    pe.wait_ge(shifted, 8 * R)
                    for u in range(NU + 3):
                        if u < NU:
                            logit(u)
                        if 2 <= u < NU + 2:
                            transpose(u - 2)
                        if 3 <= u:
                            weigh(u - 3)
                        if u == PERSEQ + 7:
                            turn_out(0)
                        if u == PERSEQ + 10:
                            project_out(0)
                    turn_out(1)
                    project_out(1)

                @block.scalar
                def _(act):
                    def take_oT(r):
                        act.wait_ge(oT_mm, 2 * r + 2)
                        nc.scalar.activation(oT[:], fin[:, 0, 0:T], ACT.Identity, bias=vec[:, 0:1]).then_inc(oT_sb, 1)

                    def take_out(r):
                        act.wait_ge(wo_mm, r + 1)
                        nc.scalar.activation(s_out[:, seq(r)], fin[:, 0, T:2 * T], ACT.Identity,
                                             bias=vec[:, 1:2]).then_inc(taken, 1)

                    for r in range(R):
                        if r:
                            act.wait_ge(v_mm, 2 * r)
                        nc.scalar.activation(tile_x[:], xn[:, seq(r)], ACT.Copy).then_inc(copied, 1)
                        if r:
                            act.wait_ge(shifted, 8 * r)
                            act.wait_ge(band_mm, 16 * r - 8)
                        for j in range(4):
                            act.wait_ge(q_mm, 4 * r + 2 * (j // 2) + 2)
                            nc.scalar.activation(qT[:, j, :], pj[:, j // 2, (j % 2) * T:(j % 2 + 1) * T],
                                                 ACT.Identity, bias=cols["bq"][:, j:j + 1]).then_inc(q_ready, 1)
                        act.wait_ge(v_mm, 2 * r + 2)
                        nc.scalar.activation(v[r][:].rearrange("p t e -> p (t e)"), fin[:, 0, 0:T],
                                             ACT.Copy).then_inc(v_ready, 1)
                        for n in range(4):
                            act.wait_ge(band_mm, 16 * r + 4 * n + 2)
                            if r:
                                act.wait_ge((qb_out, kb_out)[n // 2], 32 * r)
                            nc.scalar.activation(band[:, n, 0:BANK], pj[:, 2 * (n % 2), :], ACT.Copy).then_inc(band_lo, 1)
                    for u in range(NU):
                        _, h, t = units[u]
                        nk = P * (t + 1)
                        act.wait_ge(logits, u + 1)
                        if u >= NP_:
                            act.wait_ge(tr_mm, u - NP_ + 1)
                        nc.scalar.activation(pr[:, u % NP_, 0:nk], lg[:, u % NL, 0:nk], ACT.Exp, scale=-1.0,
                                             bias=nmax[:, u:u + 1], accum_out=rsum[:, u:u + 1]).then_inc(probs, 1)
                        if u >= 1 and u % 2 == 0:
                            evac(act, u - 1)
                        if u == PERSEQ + 8:
                            take_oT(0)
                        if u == PERSEQ + 11:
                            take_out(0)
                    evac(act, NU - 1)
                    take_oT(1)
                    take_out(1)

                @block.vector
                def _(dve):
                    for r in range(R):
                        if r:
                            dve.wait_ge(shifted, 8 * r)
                            dve.wait_ge(band_mm, 16 * r)
                        for j in range(4):
                            dve.wait_ge(k_mm, 4 * r + 2 * (j // 2) + 2)
                            nc.vector.tensor_scalar(kT[:, j, :], pj[:, 2 + j // 2, (j % 2) * T:(j % 2 + 1) * T],
                                                    cols["bk"][:, j:j + 1], None, ALU.add).then_inc(k_ready, 1)
                        for n in range(4):
                            dve.wait_ge(band_mm, 16 * r + 4 * n + 4)
                            if r:
                                dve.wait_ge((qb_out, kb_out)[n // 2], 32 * r)
                            nc.vector.tensor_copy(band[:, n, BANK:], pj[:, 2 * (n % 2) + 1, :]).then_inc(band_hi, 1)

                    def normalize_out(r, t):
                        first = PERSEQ * r + H * t
                        dve.wait_ge(probs, first + H)
                        nc.vector.reciprocal(rinv[:, first:first + H], rsum[:, first:first + H]).then_inc(inv, 1)
                        dve.wait_ge(inv, 2 * r + t + 1)
                        dve.wait_ge(pv_mm, first + H)
                        if r:
                            dve.wait_ge(oT_mm, 2 * r)
                        nc.vector.tensor_tensor(on[:, t, :].rearrange("p (h e) -> p h e", h=H),
                                                ob[:, t, 0:P].rearrange("p (h e) -> p h e", h=H),
                                                rinv[:, first:first + H].unsqueeze(2).broadcast_to([P, H, 8]),
                                                ALU.mult).then_inc(normed, 1)

                    for u in range(NU + 2):
                        if u < NU:
                            r, h, t = units[u]
                            nk = P * (t + 1)
                            dve.wait_ge(logit_mm, u + 1)
                            dve.wait_ge(masked, 2 * r + t + 1)
                            if u >= NL:
                                dve.wait_ge(probs, u - NL + 1)
                            nc.vector.tensor_tensor_reduce(out=lg[:, u % NL, 0:nk], in0=pj[:, u % 2, 0:nk],
                                                           in1=A[t][:, h, :], scale=-SC, scalar=3e38, op0=ALU.add,
                                                           op1=ALU.min, accum_out=nmax[:, u:u + 1]).then_inc(logits, 1)
                        if u >= 2 and (u - 2) % 2 == 0:
                            evac(dve, u - 2)
                        if u >= H + 2 and (u - 2) % H == 1 and u < NU:
                            done = (u - 3) // H - 1
                            normalize_out(done // 2, done % 2)
                    normalize_out(1, 1)

                @block.sync
                def _(sp):
                    def skewed(kind, tile, first, n, h0=0, nh=H):
                        v0 = band_rows[kind]
                        return bass.AP(tensor=v0.tensor, offset=v0.offset + T * ROW * h0 + (ROW - 1) * P * tile + first,
                                       ap=[[ROW - 1, P], [T * ROW, nh], [1, n]])

                    for r in range(R):
                        if r:
                            sp.wait_ge(first_in, 64)
                        for n, (kind, t) in enumerate([(0, 0), (0, 1), (1, 0), (1, 1)]):
                            sp.wait_ge(band_lo, 4 * r + n + 1)
                            sp.wait_ge(band_hi, 4 * r + n + 1)
                            sp.dma_start(band_rows[kind, :, t * P:(t + 1) * P, 0:WIN].rearrange("h p w -> p h w"),
                                         band[:, n, :].rearrange("p (h w) -> p h w", h=H)).then_inc((qb_out, kb_out)[kind], 16)
                        if r == 0:
                            sp.wait_ge(qb_out, 32)
                            sp.dma_start(A[0][:], skewed(0, 0, WIN - 1, P)).then_inc(first_in, 16)
                            sp.dma_start(A[1][:, :, 64:], skewed(0, 1, 64 + WIN - 1, ROW)).then_inc(first_in, 16)
                            sp.wait_ge(kb_out, 32)
                            sp.dma_start(B[0][:], skewed(1, 0, 0, ROW)).then_inc(first_in, 16)
                            sp.dma_start(B[1][:], skewed(1, 1, P, P)).then_inc(first_in, 16)
                    sp.wait_ge(qb_out, 64)
                    sp.wait_ge(kb_out, 64)
                    sp.wait_ge(logits, H)
                    sp.dma_start(A[0][:], skewed(0, 0, WIN - 1, P)).then_inc(next_A0_in, 16)
                    for g in range(4):
                        h0, h1 = QUART * g, QUART * (g + 1)
                        sp.wait_ge(logits, H + h1)
                        sp.wait_ge(logit_mm, H + h1)
                        for dst, src in ((A[1][:, h0:h1, 64:], skewed(0, 1, 64 + WIN - 1, ROW, h0, QUART)),
                                         (B[0][:, h0:h1, :], skewed(1, 0, 0, ROW, h0, QUART)),
                                         (B[1][:, h0:h1, :], skewed(1, 1, P, P, h0, QUART))):
                            sp.dma_start(dst, src).then_inc(next_in[g], 16)

                @block.gpsimd
                def _(pool):
                    def mask(t):
                        part = A[t][:, :, t * P:(t + 1) * P]
                        nc.gpsimd.affine_select(out=part, in_=part, compare_op=ALU.is_ge, fill=MASKED, base=0,
                                                pattern=[[0, H], [-1, P]], channel_multiplier=1).then_inc(masked, 1)

                    for r in range(R):
                        for j in range(4):
                            for dst, src, n, ready in ((qA, qT, "shift_q", q_ready), (kA, kT, "shift_k", k_ready)):
                                pool.wait_ge(ready, 4 * r + j + 1)
                                nc.gpsimd.tensor_scalar(dst[r][:, j, :], src[:, j, :], cols[n][:, j:j + 1], None,
                                                        ALU.add).then_inc(shifted, 1)
                    pool.wait_ge(first_in, 64)
                    mask(0)
                    mask(1)
                    pool.wait_ge(next_A0_in, 16)
                    mask(0)
                    for g in range(4):
                        pool.wait_ge(next_in[g], 48)
                    mask(1)
            s.barrier()


def l0_ffn(nc, c, d, xn, g_out):
    F, ST = 512, 9
    NF = F // P
    with Scope(nc, "f0") as s:
        up = s.sb("up", [P, F])
        dn = s.sb("dn", [P, F])
        upb = s.sb("up_bias", [1, F])
        one = s.sb("one", [1, 1])
        wc = s.sb("W_con", [P, NF, P])
        down = s.sb("down", [P, NF, P])
        bias_up = s.sb("bias_up", [P, NF])
        bias_out = s.sb("bias_out", [P, 2])
        bo = s.sb("bo", [P, 1])
        load(nc, s, [(up[:], d["W_exp"]), (upb[:], d["b_exp"].rearrange("(a n) -> a n", a=1)),
                     (wc[:], d["W_con"].rearrange("(c p) n -> p c n", p=P)), (bias_up[:], column(d["up_bias"])),
                     (bias_out[:, 0:1], column(d["b_con"])), (bias_out[:, 1:2], column(d["down_bias"]))])
        with Scope(nc, "f0t") as t:
            ps = t.banks("ps")
            turned, kept = t.sems("turned kept")
            with nc.Block() as block:
                @block.tensor
                def _(pe):
                    for i in range(NF):
                        nc.tensor.transpose(ps[:, 0, i * P:(i + 1) * P], wc[:, i, :], c["ident"][:]).then_inc(turned, 1)

                @block.vector
                def _(dve):
                    nc.vector.memset(one[:], 1.0)
                    nc.vector.tensor_tensor(bo[:], bias_out[:, 0:1], bias_out[:, 1:2], ALU.add)
                    dve.wait_ge(turned, NF)
                    nc.vector.tensor_copy(dn[:], ps[:, 0, :]).then_inc(kept, 1)
            t.barrier()
        with Scope(nc, "f0b") as t:
            wt = t.sb("stage_w", [P, 2, 2, 2 * F])
            tmp = t.sb("tmp", [P, 2, F])
            alt = t.sb("alt", [P, 2, F])
            btmp = t.sb("btmp", [1, F])
            balt = t.sb("balt", [1, F])
            w_in0, w_in1, stage_done, bstage_done, step, bstep = t.sems("w_in0 w_in1 stage_done bstage_done step bstep")
            w_in = [w_in0, w_in1]
            with nc.Block() as block:
                @block.sync
                def _(sp):
                    for i in range(ST):
                        if i >= 2:
                            sp.wait_ge(stage_done, i - 1)
                            sp.wait_ge(bstage_done, i - 1)
                        for k, (name, st) in enumerate((("up_weights", i), ("down_weights", ST - 1 - i))):
                            sp.dma_start(wt[:, i % 2, k, :], d[name][st].rearrange("k r c -> (k r c)").unsqueeze(0)
                                         .broadcast_to([P, 2 * F])).then_inc(w_in[i % 2], 16)

                def stage(eng, link, i, k, src, dst, tm, st, flip):
                    rows = src.shape[0]
                    n, nb = 2 ** st, F // (2 * 2 ** st)
                    y = src.rearrange("p (m r n) -> p m r n", r=2, n=n)
                    o = dst.rearrange("p (m r n) -> p m r n", r=2, n=n)
                    w = wt[0:rows, i % 2, k, :].rearrange("p (m n r c) -> p m n r c", m=nb, n=n, r=2, c=2)
                    m = tm.rearrange("p (m r n) -> p m r n", r=2, n=n)

                    def wgt(r, cc):
                        return w[:, :, :, cc, r] if flip else w[:, :, :, r, cc]
                    for r in range(2):
                        link(eng.tensor_tensor(m[:, :, r, :], wgt(r, 1), y[:, :, 1, :], ALU.mult))
                        link(eng.tensor_tensor(o[:, :, r, :], wgt(r, 0), y[:, :, 0, :], ALU.mult))
                        link(eng.tensor_tensor(o[:, :, r, :], o[:, :, r, :], m[:, :, r, :], ALU.add))

                @block.vector
                def _(dve):
                    link = Link(dve, step)
                    bufs = [[up[:], alt[:, 0, :]], [dn[:], alt[:, 1, :]]]
                    for i in range(ST):
                        dve.wait_ge(w_in[i % 2], 32 * (i // 2 + 1))
                        for k, st in enumerate((i, ST - 1 - i)):
                            stage(nc.vector, link, i, k, bufs[k][i % 2], bufs[k][1 - i % 2], tmp[:, k, :], st, k == 1)
                        nc.vector.engine_nop().then_inc(stage_done, 1)
                    for k in range(2):
                        link(nc.vector.tensor_copy(bufs[k][0], bufs[k][1]))

                @block.gpsimd
                def _(pool):
                    link = Link(pool, bstep)
                    bufs = [upb[:], balt[:]]
                    for i in range(ST):
                        pool.wait_ge(w_in[i % 2], 32 * (i // 2 + 1))
                        stage(nc.gpsimd, link, i, 0, bufs[i % 2], bufs[1 - i % 2], btmp[:], i, False)
                        nc.gpsimd.engine_nop().then_inc(bstage_done, 1)
                    link(nc.gpsimd.tensor_copy(upb[:], balt[:]))
            t.barrier()
        with Scope(nc, "f0c") as t:
            ps = t.banks("ps", 2)
            turned, kept = t.sems("turned kept")
            with nc.Block() as block:
                @block.tensor
                def _(pe):
                    for i in range(NF):
                        nc.tensor.transpose(ps[:, 0, i * P:(i + 1) * P], dn[:, i * P:(i + 1) * P],
                                            c["ident"][:]).then_inc(turned, 1)
                        nc.tensor.matmul(ps[:, 1, i:i + 1], upb[:, i * P:(i + 1) * P], one[:], start=True,
                                         stop=True).then_inc(turned, 1)

                @block.vector
                def _(dve):
                    dve.wait_ge(turned, 2 * NF)
                    nc.vector.tensor_copy(down[:].rearrange("p c n -> p (c n)"), ps[:, 0, :]).then_inc(kept, 1)
                    nc.vector.tensor_tensor(bias_up[:], bias_up[:], ps[:, 1, 0:NF], ALU.add).then_inc(kept, 1)
            t.barrier()

        W = BANK
        hid = s.sb("hidden", [P, 2, NF, W])
        hp = s.banks("hidden_ps", NF)
        yp = s.banks("y", 2)
        up_mm, acted, y_mm, y_out = s.sems("up_mm acted y_mm y_out")
        PER = 2
        with nc.Fori(0, xn.shape[1] // (W * PER) or 1) as i:
            per = min(PER, xn.shape[1] // W)
            with nc.Block() as block:
                def cols(k):
                    return bass.ds((i * PER + k) * W, W)

                @block.tensor
                def _(pe):
                    def raise_(k):
                        for f in range(NF):
                            if k:
                                pe.wait_ge(acted, NF * (k - 1) + f + 1)
                            nc.tensor.matmul(hp[:, f, :], up[:, f * P:(f + 1) * P], xn[:, cols(k)], start=True,
                                             stop=True).then_inc(up_mm, 1)

                    def lower(k):
                        for f in range(NF):
                            pe.wait_ge(acted, NF * k + f + 1)
                            ins = nc.tensor.matmul(yp[:, k % 2, :], down[:, f, :], hid[:, k % 2, f, :], start=f == 0,
                                                   stop=f == NF - 1)
                        ins.then_inc(y_mm, 1)
                    raise_(0)
                    for k in range(per):
                        if k + 1 < per:
                            raise_(k + 1)
                        lower(k)

                @block.scalar
                def _(act):
                    for k in range(per):
                        for f in range(NF):
                            act.wait_ge(up_mm, NF * k + f + 1)
                            nc.scalar.activation(hid[:, k % 2, f, :], hp[:, f, :], ACT.Gelu,
                                                 bias=bias_up[:, f:f + 1]).then_inc(acted, 1)

                @block.vector
                def _(dve):
                    for k in range(per):
                        dve.wait_ge(y_mm, k + 1)
                        nc.vector.tensor_scalar(g_out[:, cols(k)], yp[:, k % 2, :], bo[:], None,
                                                ALU.add).then_inc(y_out, 1)
            s.barrier()


def l1_attention(nc, c, d, xn, s_out):
    with Scope(nc, "a1") as s:
        w = {n: s.sb(n, [P, P]) for n in ["W_q", "W_k", "W_v"]}
        load(nc, s, [(w[n][:], d[n + "T"]) for n in w])
        kq = s.sb("kq", [P, 2 * T])
        sq = s.sb("squares", [P, 2 * T])
        nrm = s.sb("norms", [P, 2 * T])
        inv = s.sb("inv_norms", [P, 2 * T])
        kn = s.sb("k_normed", [P, T])
        qn = s.sb("q_normed", [P, T])
        kv = s.sb("kv", [P, T])
        feat = s.sb("feature", [P, 2])
        ps = s.banks("kq", 1)
        vs = s.banks("v", 1)
        ss = s.banks("sum_squares", 1)
        kq_mm, v_mm, kq_sb, squared, ss_mm, rooted, step, inverted, k_normed, q_normed, summed = s.sems(
            "kq_mm v_mm kq_sb squared ss_mm rooted step inverted k_normed q_normed summed")
        with nc.Fori(0, xn.shape[1] // T) as b:
            with nc.Block() as block:
                @block.tensor
                def _(pe):
                    for n, name in enumerate(["W_k", "W_q"]):
                        nc.tensor.matmul(ps[:, 0, n * T:(n + 1) * T], w[name][:], xn[:, tokens(b)], start=True,
                                         stop=True).then_inc(kq_mm, 1)
                    nc.tensor.matmul(vs[:, 0, 0:T], w["W_v"][:], xn[:, tokens(b)], start=True, stop=True).then_inc(v_mm, 1)
                    pe.wait_ge(squared, 1)
                    nc.tensor.matmul(ss[:, 0, :], c["ones"][:], sq[:], start=True, stop=True).then_inc(ss_mm, 1)

                @block.scalar
                def _(act):
                    act.wait_ge(kq_mm, 2)
                    nc.scalar.activation(kq[:], ps[:, 0, :], ACT.Copy).then_inc(kq_sb, 1)
                    nc.scalar.activation(sq[:], ps[:, 0, :], ACT.Square).then_inc(squared, 1)
                    act.wait_ge(ss_mm, 1)
                    nc.scalar.activation(nrm[:], ss[:, 0, :], ACT.Sqrt).then_inc(rooted, 1)

                @block.vector
                def _(dve):
                    dve.wait_ge(rooted, 1)
                    link = Link(dve, step)
                    link(nc.vector.tensor_scalar(nrm[:], nrm[:], 1e-12, None, ALU.max))
                    nc.vector.reciprocal(inv[:, 0:T], nrm[:, 0:T]).then_inc(inverted, 1)
                    nc.vector.reciprocal(inv[:, T:], nrm[:, T:]).then_inc(inverted, 1)
                    dve.wait_ge(k_normed, 1)
                    dve.wait_ge(v_mm, 1)
                    nc.vector.tensor_tensor_reduce(out=kv[:], in0=vs[:, 0, 0:T], in1=kn[:], scale=1.0, scalar=0.0,
                                                   op0=ALU.mult, op1=ALU.add, accum_out=feat[:, 0:1]).then_inc(summed, 1)
                    dve.wait_ge(summed, 1)
                    dve.wait_ge(q_normed, 1)
                    nc.vector.tensor_scalar(s_out[:, tokens(b)], qn[:], feat[:, 0:1], 1.0 / T, ALU.mult, ALU.mult)

                @block.gpsimd
                def _(pool):
                    pool.wait_ge(kq_sb, 1)
                    pool.wait_ge(inverted, 1)
                    nc.gpsimd.tensor_tensor(kn[:], kq[:, 0:T], inv[:, 0:T], ALU.mult).then_inc(k_normed, 1)
                    pool.wait_ge(inverted, 2)
                    nc.gpsimd.tensor_tensor(qn[:], kq[:, T:], inv[:, T:], ALU.mult).then_inc(q_normed, 1)
            s.barrier()


def l1_ffn(nc, c, d, xn, g_out):
    SL, DQ, K = 64, 32, 2
    with Scope(nc, "f1") as s:
        w1 = s.sb("w1", [P, 2, SL])
        w2 = s.sb("w2", [SL, SL])
        slot = s.sb("slotT", [P, SL])
        wih = s.sb("WihT", [P, 3, P])
        whh = s.sb("WhhT", [P, 3, P])
        bih = s.sb("bih", [P, 3])
        bhh = s.sb("bhh", [P, 3])
        wqk = s.sb("wqk", [P, 2, DQ])
        bqk = s.sb("bqk", [DQ, 2])
        wv, wvp, wo = s.sb("wv", [P, P]), s.sb("wvp", [P, P]), s.sb("wo", [P, P])
        vec = s.sb("vectors", [P, 5])
        b1 = s.sb("b1", [SL, 1])
        b2 = s.sb("b2", [1, SL])
        tau = s.sb("tau", [P, 1])
        ntau = s.sb("neg_tau", [P, 1])
        load(nc, s, [(w1[:], d["w1"].rearrange("(a p) n -> p a n", p=P)), (w2[:], d["w2"]), (slot[:], d["slot_initT"]),
                     (wih[:].rearrange("p a n -> p (a n)"), d["WihT"]), (whh[:].rearrange("p a n -> p (a n)"), d["WhhT"]),
                     (bih[:], column(d["bih"])), (bhh[:], column(d["bhh"])), (wqk[:, 0, :], d["wq"]),
                     (wqk[:, 1, :], d["wk"]), (bqk[:, 0:1], d["bq"].rearrange("(p a) -> p a", a=1)),
                     (bqk[:, 1:2], d["bk"].rearrange("(p a) -> p a", a=1)), (wv[:], d["wv"]), (wvp[:], d["wvp"]),
                     (wo[:], d["wo"]), (b1[:], d["b1"].rearrange("(p a) -> p a", a=1)),
                     (b2[:], d["b2"].rearrange("(a n) -> a n", a=1)),
                     (tau[:], d["tau"].unsqueeze(0).broadcast_to([P, 1]))]
             + [(vec[:, i:i + 1], column(d[n])) for i, n in enumerate(["bv", "ln_g", "ln_b", "bvp", "bo"])])
        smean = s.sb("slot_mean", [P, 1])
        hbias = s.sb("hidden_bias", [SL, 1])
        gh = s.sb("ghT", [P, 3, SL])
        with Scope(nc, "f1t") as t:
            ps = t.banks("ps", 2)
            meaned, mm, step = t.sems("meaned mm step")
            with nc.Block() as block:
                @block.tensor
                def _(pe):
                    for i in range(3):
                        nc.tensor.matmul(ps[:, 0, i * SL:(i + 1) * SL], whh[:, i, :], slot[:], start=True,
                                         stop=True).then_inc(mm, 1)
                    pe.wait_ge(meaned, 1)
                    nc.tensor.matmul(ps[0:SL, 1, 0:1], w1[:, 1, :], smean[:], start=True, stop=True).then_inc(mm, 1)

                @block.vector
                def _(dve):
                    link = Link(dve, step)
                    link(nc.vector.reduce_sum(smean[:], slot[:], axis=AX_X))
                    nc.vector.tensor_scalar(smean[:], smean[:], 1.0 / SL, None, ALU.mult).then_inc(meaned, 1)
                    link(nc.vector.tensor_scalar(ntau[:], tau[:], -1.0, None, ALU.mult))
                    link(nc.vector.tensor_tensor(tau[:], tau[:], ntau[:], ALU.max))
                    link(nc.vector.tensor_scalar(tau[:], tau[:], 0.1, None, ALU.add))
                    link(nc.vector.reciprocal(tau[:], tau[:]))
                    link(nc.vector.tensor_tensor(bhh[:, 0:2], bhh[:, 0:2], bih[:, 0:2], ALU.add))
                    dve.wait_ge(mm, 4)
                    link(nc.vector.tensor_tensor(gh[:], ps[:, 0, 0:3 * SL].rearrange("p (a n) -> p a n", a=3),
                                                 bhh[:].unsqueeze(2).broadcast_to([P, 3, SL]), ALU.add))
                    link(nc.vector.tensor_tensor(hbias[:], ps[0:SL, 1, 0:1], b1[:], ALU.add))
            t.barrier()

        def each(name, shape):
            return [s.sb(f"{name}{k}", shape) for k in range(K)]
        tx, hT, xt, lg, rep, m8 = each("x", [P, T]), each("hidden", [SL, T]), each("x_tok", [P, 2, P]), each(
            "route", [P, 2, SL]), each("replaced", [P, 2, SL]), each("top8", [P, 2, 8])
        ex, al, asum, ainv, alT = each("exps", [P, 2, SL]), each("alpha", [P, 2, SL]), each("alpha_sum", [P, 2]), each(
            "alpha_inv", [P, 2]), each("alphaT", [SL, T])
        nm = each("neg_max", [P, 2])
        den, si, ga, rz, u, nn, zs, sn = each("denom", [P, SL]), each("slot_in", [P, SL]), each("gates_in", [P, 2, SL]), \
            each("gates", [P, 2, SL]), each("r_hn", [P, SL]), each("cell", [P, SL]), each("z_part", [P, SL]), each(
            "slots_new", [P, SL])
        qk, v, amax, ae, asm, ai, aT = each("qk", [DQ, 2, SL]), each("v", [SL, P]), each("att_max", [SL, 1]), each(
            "att_exp", [SL, SL]), each("att_sum", [SL, 1]), each("att_inv", [SL, 1]), each("attT", [SL, SL])
        y, yc, ysq, yrs, sv, oT = each("y", [P, SL]), each("y_centered", [P, SL]), each("y_sq", [P, SL]), each(
            "y_inv_dev", [P, SL]), each("slot_values", [SL, P]), each("outT", [P, T])
        bk = [s.banks(f"k{k}", 4) for k in range(K)]
        A, B, C, D = ([bk[k][:, i, :] for k in range(K)] for i in range(4))
        (copied, h_mm, h_act, xt_mm, xt_sb, lg_mm, step, negated, topped, exped, alphaed, si_mm, si_sb, gi_mm, gates_in,
         gates, u_ready, cell, s_new, qk_mm, v_mm, qk_sb, v_sb, att_mm, att_max, att_exp, att_norm, aT_mm, aT_sb,
         comm_mm, y_ready, mean_mm, centered, squared, var_mm, logged, rooted, y_norm, sv_mm, sv_sb, alT_mm, alT_sb,
         out_mm, out_sb, wo_mm) = s.sems(
            "copied h_mm h_act xt_mm xt_sb lg_mm step negated topped exped alphaed si_mm si_sb gi_mm gates_in "
            "gates u_ready cell s_new qk_mm v_mm qk_sb v_sb att_mm att_max att_exp att_norm aT_mm aT_sb "
            "comm_mm y_ready mean_mm centered squared var_mm logged rooted y_norm sv_mm sv_sb alT_mm alT_sb "
            "out_mm out_sb wo_mm")
        ident = c["ident"]
        with nc.Fori(0, xn.shape[1] // (T * K)) as b:
            with nc.Block() as block:
                def seq(k):
                    return bass.ds((b * K + k) * T, T)

                @block.tensor
                def _(pe):
                    mm = nc.tensor.matmul
                    for k in range(K):
                        mm(A[k][0:SL, 0:T], w1[:, 0, :], xn[:, seq(k)], start=True, stop=True).then_inc(h_mm, 1)
                    for k in range(K):
                        pe.wait_ge(copied, k + 1)
                        for t in range(2):
                            ins = nc.tensor.transpose(B[k][:, t * P:(t + 1) * P], tx[k][:, t * P:(t + 1) * P], ident[:])
                        ins.then_inc(xt_mm, 1)
                    for k in range(K):
                        pe.wait_ge(h_act, k + 1)
                        for t in range(2):
                            o = A[k][:, T + t * SL:T + (t + 1) * SL]
                            mm(o, hT[k][:, t * P:(t + 1) * P], w2[:], start=True, stop=False)
                            ins = mm(o, c["ones"][0:1, :], b2[:], start=False, stop=True)
                        ins.then_inc(lg_mm, 1)
                    for k in range(K):
                        pe.wait_ge(alphaed, 2 * k + 2)
                        pe.wait_ge(xt_sb, k + 1)
                        for t in range(2):
                            mm(C[k][:, 0:SL], xt[k][:, t, :], al[k][:, t, :], start=t == 0, stop=t == 1)
                        for t in range(2):
                            ins = mm(C[k][:, SL:2 * SL], c["ones"][:], al[k][:, t, :], start=t == 0, stop=t == 1)
                        ins.then_inc(si_mm, 1)
                    for k in range(K):
                        for t in range(2):
                            ins = nc.tensor.transpose(B[k][0:SL, t * P:(t + 1) * P], al[k][:, t, :], ident[:])
                        ins.then_inc(alT_mm, 1)
                    for k in range(K):
                        pe.wait_ge(si_sb, k + 1)
                        for i in range(3):
                            ins = mm(C[k][:, (2 + i) * SL:(3 + i) * SL], wih[:, i, :], si[k][:], start=True, stop=True)
                        ins.then_inc(gi_mm, 1)
                    for k in range(K):
                        pe.wait_ge(s_new, k + 1)
                        for i in range(2):
                            ins = mm(A[k][0:DQ, i * SL:(i + 1) * SL], wqk[:, i, :], sn[k][:], start=True, stop=True)
                        ins.then_inc(qk_mm, 1)
                        mm(D[k][0:SL, 0:P], sn[k][:], wv[:], start=True, stop=True).then_inc(v_mm, 1)
                    for k in range(K):
                        pe.wait_ge(qk_sb, k + 1)
                        mm(A[k][0:SL, 0:SL], qk[k][:, 0, :], qk[k][:, 1, :], start=True, stop=True).then_inc(att_mm, 1)
                    for k in range(K):
                        pe.wait_ge(att_norm, k + 1)
                        nc.tensor.transpose(A[k][0:SL, SL:2 * SL], ae[k][:], ident[0:SL, 0:SL]).then_inc(aT_mm, 1)
                    for k in range(K):
                        pe.wait_ge(aT_sb, k + 1)
                        pe.wait_ge(v_sb, k + 1)
                        mm(C[k][:, 0:SL], v[k][:], aT[k][:], start=True, stop=True).then_inc(comm_mm, 1)
                    for k in range(K):
                        pe.wait_ge(y_ready, k + 1)
                        mm(A[k][:, 0:SL], c["mean"][:], y[k][:], start=True, stop=True).then_inc(mean_mm, 1)
                    for k in range(K):
                        pe.wait_ge(squared, k + 1)
                        mm(C[k][:, 0:SL], c["mean"][:], ysq[k][:], start=True, stop=True).then_inc(var_mm, 1)
                    for k in range(K):
                        pe.wait_ge(y_norm, k + 1)
                        mm(A[k][0:SL, 0:P], y[k][:], wvp[:], start=True, stop=True).then_inc(sv_mm, 1)
                    for k in range(K):
                        pe.wait_ge(sv_sb, k + 1)
                        pe.wait_ge(alT_sb, k + 1)
                        mm(C[k][:, 0:T], sv[k][:], alT[k][:], start=True, stop=True).then_inc(out_mm, 1)
                    for k in range(K):
                        pe.wait_ge(out_sb, k + 1)
                        mm(A[k][:, 0:T], wo[:], oT[k][:], start=True, stop=True).then_inc(wo_mm, 1)

                @block.scalar
                def _(act):
                    ac = nc.scalar.activation
                    for k in range(K):
                        ac(tx[k][:], xn[:, seq(k)], ACT.Copy).then_inc(copied, 1)
                    for k in range(K):
                        act.wait_ge(h_mm, k + 1)
                        ac(hT[k][:], A[k][0:SL, 0:T], ACT.Gelu, bias=hbias[:]).then_inc(h_act, 1)
                    for k in range(K):
                        act.wait_ge(negated, k + 1)
                        for t in range(2):
                            ac(ex[k][:, t, :], lg[k][:, t, :], ACT.Exp, bias=nm[k][:, t:t + 1]).then_inc(exped, 1)
                    for k in range(K):
                        act.wait_ge(alT_mm, k + 1)
                        ac(alT[k][:], B[k][0:SL, 0:T], ACT.Copy).then_inc(alT_sb, 1)
                    for k in range(K):
                        act.wait_ge(gates_in, k + 1)
                        ac(rz[k][:], ga[k][:], ACT.Tanh, scale=0.5).then_inc(gates, 1)
                    for k in range(K):
                        act.wait_ge(u_ready, k + 1)
                        ac(nn[k][:], u[k][:], ACT.Tanh, bias=bih[:, 2:3]).then_inc(cell, 1)
                    for k in range(K):
                        act.wait_ge(v_mm, k + 1)
                        ac(v[k][:], D[k][0:SL, 0:P], ACT.Copy).then_inc(v_sb, 1)
                    for k in range(K):
                        act.wait_ge(att_max, k + 1)
                        ac(ae[k][:], A[k][0:SL, 0:SL], ACT.Exp, bias=amax[k][:], accum_out=asm[k][:]).then_inc(att_exp, 1)
                    for k in range(K):
                        act.wait_ge(centered, k + 1)
                        ac(ysq[k][:], yc[k][:], ACT.Square).then_inc(squared, 1)
                    for k in range(K):
                        act.wait_ge(var_mm, k + 1)
                        ac(yrs[k][:], C[k][:, 0:SL], ACT.Ln, bias=c["eps"][:]).then_inc(logged, 1)
                    for k in range(K):
                        act.wait_ge(logged, k + 1)
                        ac(yrs[k][:], yrs[k][:], ACT.Exp, scale=-0.5).then_inc(rooted, 1)
                    for k in range(K):
                        act.wait_ge(out_mm, k + 1)
                        ac(oT[k][:], C[k][:, 0:T], ACT.Identity, bias=vec[:, 3:4]).then_inc(out_sb, 1)

                @block.vector
                def _(dve):
                    link = Link(dve, step)
                    tt, ts = nc.vector.tensor_tensor, nc.vector.tensor_scalar
                    for k in range(K):
                        dve.wait_ge(xt_mm, k + 1)
                        nc.vector.tensor_copy(xt[k][:].rearrange("p t n -> p (t n)"), B[k][:, 0:T]).then_inc(xt_sb, 1)
                    for k in range(K):
                        dve.wait_ge(lg_mm, k + 1)
                        link(ts(lg[k][:].rearrange("p t n -> p (t n)"), A[k][:, T:T + 2 * SL], tau[:], None, ALU.mult))
                        for t in range(2):
                            nc.vector.max(m8[k][:, t, :], lg[k][:, t, :]).then_inc(topped, 1)
                        dve.wait_ge(topped, 2 * k + 2)
                        ts(nm[k][:], m8[k][:, :, 0], -1.0, None, ALU.mult).then_inc(negated, 1)
                        for t in range(2):
                            link(nc.vector.match_replace(rep[k][:, t, :], m8[k][:, t, :], lg[k][:, t, :], MASKED))
                        link(tt(rep[k][:], rep[k][:], lg[k][:], ALU.not_equal))
                    for k in range(K):
                        for t in range(2):
                            dve.wait_ge(exped, 2 * k + t + 1)
                            link(nc.vector.tensor_tensor_reduce(out=al[k][:, t, :], in0=ex[k][:, t, :],
                                                                in1=rep[k][:, t, :], scale=1.0, scalar=0.0, op0=ALU.mult,
                                                                op1=ALU.add, accum_out=asum[k][:, t:t + 1]))
                        link(nc.vector.reciprocal(ainv[k][:], asum[k][:]))
                        for t in range(2):
                            ts(al[k][:, t, :], al[k][:, t, :], ainv[k][:, t:t + 1], None, ALU.mult).then_inc(alphaed, 1)
                    for k in range(K):
                        dve.wait_ge(si_mm, k + 1)
                        link(ts(den[k][:], C[k][:, SL:2 * SL], 1e-8, None, ALU.add))
                        link(nc.vector.reciprocal(den[k][:], den[k][:]))
                        tt(si[k][:], C[k][:, 0:SL], den[k][:], ALU.mult).then_inc(si_sb, 1)
                    for k in range(K):
                        dve.wait_ge(gi_mm, k + 1)
                        tt(ga[k][:], C[k][:, 2 * SL:4 * SL].rearrange("p (a n) -> p a n", a=2), gh[:, 0:2, :],
                           ALU.add).then_inc(gates_in, 1)
                    for k in range(K):
                        dve.wait_ge(gates, k + 1)
                        link(ts(rz[k][:], rz[k][:], 0.5, 0.5, ALU.mult, ALU.add))
                        link(tt(u[k][:], rz[k][:, 0, :], gh[:, 2, :], ALU.mult))
                        tt(u[k][:], u[k][:], C[k][:, 4 * SL:5 * SL], ALU.add).then_inc(u_ready, 1)
                    for k in range(K):
                        dve.wait_ge(cell, k + 1)
                        link(tt(zs[k][:], slot[:], nn[k][:], ALU.subtract))
                        link(tt(zs[k][:], zs[k][:], rz[k][:, 1, :], ALU.mult))
                        tt(sn[k][:], nn[k][:], zs[k][:], ALU.add).then_inc(s_new, 1)
                    for k in range(K):
                        dve.wait_ge(qk_mm, k + 1)
                        link(ts(qk[k][:, 0, :], A[k][0:DQ, 0:SL], bqk[:, 0:1], float(DQ) ** -0.5, ALU.add, ALU.mult))
                        ts(qk[k][:, 1, :], A[k][0:DQ, SL:2 * SL], bqk[:, 1:2], None, ALU.add).then_inc(qk_sb, 1)
                    for k in range(K):
                        dve.wait_ge(att_mm, k + 1)
                        nc.vector.tensor_reduce(out=amax[k][:], in_=A[k][0:SL, 0:SL], axis=AX_X, op=ALU.max,
                                                negate=True).then_inc(att_max, 1)
                    for k in range(K):
                        dve.wait_ge(att_exp, k + 1)
                        link(nc.vector.reciprocal(ai[k][:], asm[k][:]))
                        ts(ae[k][:], ae[k][:], ai[k][:], None, ALU.mult).then_inc(att_norm, 1)
                    for k in range(K):
                        dve.wait_ge(aT_mm, k + 1)
                        nc.vector.tensor_copy(aT[k][:], A[k][0:SL, SL:2 * SL]).then_inc(aT_sb, 1)
                    for k in range(K):
                        dve.wait_ge(comm_mm, k + 1)
                        dve.wait_ge(s_new, k + 1)
                        nc.vector.scalar_tensor_tensor(out=y[k][:], in0=C[k][:, 0:SL], scalar=vec[:, 0:1], in1=sn[k][:],
                                                       op0=ALU.add, op1=ALU.add).then_inc(y_ready, 1)
                    for k in range(K):
                        dve.wait_ge(mean_mm, k + 1)
                        tt(yc[k][:], y[k][:], A[k][:, 0:SL], ALU.subtract).then_inc(centered, 1)
                    for k in range(K):
                        dve.wait_ge(rooted, k + 1)
                        link(tt(y[k][:], yc[k][:], yrs[k][:], ALU.mult))
                        ts(y[k][:], y[k][:], vec[:, 1:2], vec[:, 2:3], ALU.mult, ALU.add).then_inc(y_norm, 1)
                    for k in range(K):
                        dve.wait_ge(sv_mm, k + 1)
                        nc.vector.tensor_copy(sv[k][:], A[k][0:SL, 0:P]).then_inc(sv_sb, 1)
                    for k in range(K):
                        dve.wait_ge(wo_mm, k + 1)
                        ts(g_out[:, seq(k)], A[k][:, 0:T], vec[:, 4:5], None, ALU.add)
            s.barrier()


def l2_attention(nc, c, d, xn, s_out):
    HD = 64
    SC = HD ** -0.5
    PAD = -30000.0
    NP2 = H // 2
    with Scope(nc, "a2") as s:
        wqkv = s.sb("wqkv", [P, 3, H * HD])
        wo = s.sb("wo", [P, NP2, P])
        bias = [s.sb("bias0", [P, H, P]), s.sb("bias1", [P, H, T])]
        rows = nc.dram_tensor("a2_bias_rows", (H, P, T + P), F32).ap()
        load(nc, s, [(wqkv[:].rearrange("p m e -> p (m e)"), d["qkv"].rearrange("p m n e -> p (m n e)")),
                     (wo[:], d["out_w"].rearrange("n e x -> (n e) x").rearrange("(c p) x -> p c x", p=P))])
        with Scope(nc, "a2t") as t:
            rb = t.sb("rpe", [H, T])
            zero = t.sb("zero", [H, T])
            cum = t.sb("cum", [H, T])
            rev = t.sb("reversed", [H, T + P])
            in_, filled, step, ready, out_, spread = t.sems("in filled step ready out spread")
            with nc.Block() as block:
                @block.vector
                def _(dve):
                    link = Link(dve, step)
                    link(nc.vector.memset(zero[:], 0.0))
                    link(nc.vector.memset(rev[:], PAD / SC))
                    dve.wait_ge(in_, 16)
                    link(nc.vector.tensor_tensor_scan(cum[:], rb[:], zero[:], 0.0, ALU.add, ALU.add))
                    nc.vector.tensor_scalar(rev[:, 0:T], cum[:, ::-1], 1.0 / SC, None, ALU.mult).then_inc(ready, 1)

                @block.sync
                def _(sp):
                    sp.dma_start(rb[:], d["rpe_bias"]).then_inc(in_, 16)
                    sp.wait_ge(ready, 1)
                    sp.dma_start(rows, rev[:].unsqueeze(1).broadcast_to([H, P, T + P])).then_inc(out_, 16)
                    sp.wait_ge(out_, 16)
                    for tile in range(2):
                        src = bass.AP(tensor=rows.tensor, offset=rows.offset + T - 1 - P * tile,
                                      ap=[[T + P - 1, P], [P * (T + P), H], [1, P * (tile + 1)]])
                        sp.dma_start(bias[tile][:], src).then_inc(spread, 16)
                    sp.wait_ge(spread, 32)
            t.barrier()

        tile_x = s.sb("x", [P, T])
        qT, kT = s.sb("qT", [P, NP2, T]), s.sb("kT", [P, NP2, T])
        v = s.sb("v", [P, 2, H * HD])
        NL, NQ, NT = 3, 3, 3
        lg, pr, pt = s.sb("logits", [P, NL, T]), s.sb("probs", [P, NQ, T]), s.sb("probs_T", [P, NT, T])
        nmax, rsum, rinv = s.sb("neg_max", [P, 2 * H]), s.sb("row_sum", [P, 2 * H]), s.sb("row_inv", [P, 2 * H])
        on = s.sb("o_normed", [P, 2, H * HD])
        oT = s.sb("oT", [P, NP2, T])
        pj = s.banks("pj", 4)
        ob = s.banks("out", 4)
        (copied, qk_mm, lo_sb, hi_sb, logit_mm, logits, probs, tr_mm, tr_sb, pv_mm, inv, normed, oT_mm, oT_lo, oT_hi,
         wo_mm, step) = s.sems("copied qk_mm lo_sb hi_sb logit_mm logits probs tr_mm tr_sb pv_mm inv normed oT_mm "
                               "oT_lo oT_hi wo_mm step")
        units = [(h, t) for t in range(2) for h in range(H)]
        NU = len(units)
        NPJ = 12
        with nc.Fori(0, xn.shape[1] // T) as b:
            with nc.Block() as block:
                def keep(eng, n):
                    eng.wait_ge(qk_mm, 2 * n + 2)
                    src = pj[:, n % 4, :]
                    if n < 8:
                        dst = (qT, kT)[n // 4][:, 2 * (n % 4):2 * (n % 4) + 2, :].rearrange("p j t -> p (j t)")
                    else:
                        dst = v[:, (n - 8) // 2, (n % 2) * BANK:(n % 2 + 1) * BANK]
                    if n % 2 == 0:
                        nc.scalar.activation(dst, src, ACT.Copy).then_inc(lo_sb, 1)
                    else:
                        nc.vector.tensor_copy(dst, src).then_inc(hi_sb, 1)

                def evac(eng, u):
                    h, t = units[u]
                    nk = P * (t + 1)
                    eng.wait_ge(tr_mm, u + 1)
                    if u >= NT:
                        eng.wait_ge(pv_mm, u - NT + 1)
                    eng.wait_ge(tr_sb, u)
                    if u % 2:
                        ins = nc.scalar.activation(pt[:, u % NT, 0:nk], pj[:, 2 + u % 2, 0:nk], ACT.Copy)
                    else:
                        ins = nc.vector.tensor_copy(pt[:, u % NT, 0:nk], pj[:, 2 + u % 2, 0:nk])
                    ins.then_inc(tr_sb, 1)

                def norm(dve, t):
                    dve.wait_ge(probs, H * (t + 1))
                    nc.vector.reciprocal(rinv[:, H * t:H * (t + 1)], rsum[:, H * t:H * (t + 1)]).then_inc(inv, 1)
                    dve.wait_ge(inv, t + 1)
                    dve.wait_ge(pv_mm, H * (t + 1))
                    for i in range(2):
                        h0 = H * t + 8 * i
                        nc.vector.tensor_tensor(on[:, t, i * BANK:(i + 1) * BANK].rearrange("p (h e) -> p h e", h=8),
                                                ob[:, 2 * t + i, :].rearrange("p (h e) -> p h e", h=8),
                                                rinv[:, h0:h0 + 8].unsqueeze(2).broadcast_to([P, 8, HD]),
                                                ALU.mult).then_inc(normed, 1)

                @block.tensor
                def _(pe):
                    for n in range(NPJ):
                        if n >= 4:
                            pe.wait_ge((lo_sb, hi_sb)[n % 2], (n - 4) // 2 + 1)
                        if n == 8:
                            pe.wait_ge(copied, 1)
                        for i in range(2):
                            o = pj[:, n % 4, i * T:(i + 1) * T]
                            if n < 8:
                                col = (2 * (n % 4) + i) * P
                                nc.tensor.matmul(o, wqkv[:, n // 4, col:col + P], xn[:, tokens(b)], start=True,
                                                 stop=True).then_inc(qk_mm, 1)
                            else:
                                t = (n - 8) // 2
                                nc.tensor.matmul(o, tile_x[:, t * P:(t + 1) * P],
                                                 wqkv[:, 2, (2 * (n % 2) + i) * T:(2 * (n % 2) + i + 1) * T], start=True,
                                                 stop=True).then_inc(qk_mm, 1)
                    pe.wait_ge(lo_sb, 6)
                    pe.wait_ge(hi_sb, 6)

                    def logit(u):
                        h, t = units[u]
                        r, j = slice(HD * (h % 2), HD * (h % 2) + HD), h // 2
                        if u >= 2:
                            pe.wait_ge(logits, u - 1)
                        nc.tensor.matmul(pj[:, u % 2, 0:P * (t + 1)], qT[r, j, t * P:(t + 1) * P], kT[r, j, 0:P * (t + 1)],
                                         start=True, stop=True).then_inc(logit_mm, 1)

                    def transpose(u):
                        h, t = units[u]
                        pe.wait_ge(probs, u + 1)
                        if u >= 2:
                            pe.wait_ge(tr_sb, u - 1)
                        for kt in range(t + 1):
                            ins = nc.tensor.transpose(pj[:, 2 + u % 2, kt * P:(kt + 1) * P],
                                                      pr[:, u % NQ, kt * P:(kt + 1) * P], c["ident"][:])
                        ins.then_inc(tr_mm, 1)

                    def weigh(u):
                        h, t = units[u]
                        pe.wait_ge(tr_sb, u + 1)
                        for kt in range(t + 1):
                            ins = nc.tensor.matmul(ob[:, 2 * t + h // 8, HD * (h % 8):HD * (h % 8) + HD],
                                                   pt[:, u % NT, kt * P:(kt + 1) * P], v[:, kt, HD * h:HD * h + HD],
                                                   start=kt == 0, stop=kt == t)
                        ins.then_inc(pv_mm, 1)

                    for u in range(NU + 3):
                        if u < NU:
                            logit(u)
                        if 2 <= u < NU + 2:
                            transpose(u - 2)
                        if 3 <= u:
                            weigh(u - 3)
                    pe.wait_ge(normed, 4)
                    for m in range(4):
                        for i in range(2):
                            for t in range(2):
                                nc.tensor.transpose(pj[:, m, i * T + t * P:i * T + (t + 1) * P],
                                                    on[:, t, (2 * m + i) * P:(2 * m + i + 1) * P],
                                                    c["ident"][:]).then_inc(oT_mm, 1)
                    for j in range(NP2):
                        pe.wait_ge((oT_lo, oT_hi)[(j // 2) % 2], j // 4 + 1)
                        ins = nc.tensor.matmul(ob[:, 0, 0:T], wo[:, j, :], oT[:, j, :], start=j == 0, stop=j == NP2 - 1)
                    ins.then_inc(wo_mm, 1)

                @block.scalar
                def _(act):
                    nc.scalar.activation(tile_x[:], xn[:, tokens(b)], ACT.Copy).then_inc(copied, 1)
                    for n in range(0, NPJ, 2):
                        keep(act, n)
                    for u in range(NU):
                        h, t = units[u]
                        nk = P * (t + 1)
                        act.wait_ge(logits, u + 1)
                        if u >= NQ:
                            act.wait_ge(tr_mm, u - NQ + 1)
                        nc.scalar.activation(pr[:, u % NQ, 0:nk], lg[:, u % NL, 0:nk], ACT.Exp, scale=-1.0,
                                             bias=nmax[:, u:u + 1], accum_out=rsum[:, u:u + 1]).then_inc(probs, 1)
                        if u >= 1 and u % 2 == 0:
                            evac(act, u - 1)
                    evac(act, NU - 1)
                    for m in (0, 2):
                        act.wait_ge(oT_mm, 4 * m + 4)
                        nc.scalar.activation(oT[:, 2 * m:2 * m + 2, :].rearrange("p j t -> p (j t)"), pj[:, m, :],
                                             ACT.Copy).then_inc(oT_lo, 1)
                    act.wait_ge(wo_mm, 1)
                    nc.scalar.activation(s_out[:, tokens(b)], ob[:, 0, 0:T], ACT.Copy)

                @block.vector
                def _(dve):
                    for n in range(1, NPJ, 2):
                        keep(dve, n)
                    for u in range(NU + 2):
                        if u < NU:
                            h, t = units[u]
                            nk = P * (t + 1)
                            dve.wait_ge(logit_mm, u + 1)
                            if u >= NL:
                                dve.wait_ge(probs, u - NL + 1)
                            nc.vector.tensor_tensor_reduce(out=lg[:, u % NL, 0:nk], in0=pj[:, u % 2, 0:nk],
                                                           in1=bias[t][:, h, :], scale=-SC, scalar=3e38, op0=ALU.add,
                                                           op1=ALU.min, accum_out=nmax[:, u:u + 1]).then_inc(logits, 1)
                        if u >= 2 and u % 2 == 0:
                            evac(dve, u - 2)
                        if u == 3 * H // 2 + 2:
                            norm(dve, 0)
                    norm(dve, 1)
                    for m in (1, 3):
                        dve.wait_ge(oT_mm, 4 * m + 4)
                        nc.vector.tensor_copy(oT[:, 2 * m:2 * m + 2, :].rearrange("p j t -> p (j t)"),
                                              pj[:, m, :]).then_inc(oT_hi, 1)
            s.barrier()


def make_iota(nc, s, n):
    whole = s.sb("iota_int", [P, n], mybir.dt.int32)
    real = s.sb("iota", [P, n])
    with Scope(nc, "iota") as t:
        made, kept = t.sems("made kept")
        with nc.Block() as block:
            @block.gpsimd
            def _(pool):
                nc.gpsimd.iota(whole[:], pattern=[[1, n]], base=0, channel_multiplier=0).then_inc(made, 1)

            @block.vector
            def _(dve):
                dve.wait_ge(made, 1)
                nc.vector.tensor_copy(real[:], whole[:]).then_inc(kept, 1)
        t.barrier()
    return real


def l2_ffn_tables(n):
    half = P // 2
    freq = (1.0 / np.float32(10000.0) ** (np.arange(0, P, 2, dtype=np.float32) / np.float32(P))).astype(np.float32)
    ang = freq.astype(np.float64)[:, None] * np.arange(n)[None, :]
    co, si = np.cos(ang), np.sin(ang)
    both = [np.concatenate(v, 0) for v in ((co, co), (si, si), (si, co), (-co, si))]
    assert both[0].shape == (2 * half, n)
    return np.stack(both, 1).astype(np.float32)


def relative_attention(nc, c, d, src, xa, out):
    with Scope(nc, "r2") as s:
        w = {n: s.sb(n, [P, P]) for n in ["wq", "wk", "wv", "wo"]}
        wp_ = {n: s.sb(n + "_padded", [P, 4, P]) for n in ["wq", "wk"]}
        wpos = s.sb("wpT_padded", [P, 4, P])
        trig = s.sb("trig", [P, 4, T])
        load(nc, s, [(w[n][:], d[n]) for n in w] + [(trig[:], d["trig"])])
        with Scope(nc, "r2t") as t:
            zeroed, landed, padded = t.sems("zeroed landed padded")
            with nc.Block() as block:
                @block.gpsimd
                def _(pool):
                    for n in wp_:
                        nc.gpsimd.memset(wp_[n][:], 0.0)
                    nc.gpsimd.memset(wpos[:], 0.0).then_inc(zeroed, 1)

                @block.vector
                def _(dve):
                    dve.wait_ge(zeroed, 1)
                    for n in wp_:
                        pad_heads(nc, wp_[n][:], w[n][:]).then_inc(padded, 1)

                @block.sync
                def _(sp):
                    sp.wait_ge(zeroed, 1)
                    for g in range(4):
                        sp.dma_start(wpos[32 * g:32 * g + 8, :, :],
                                     d["wpT"].rearrange("(j g d) f -> g d j f", j=4, g=4)[g]).then_inc(landed, 16)
                    sp.wait_ge(landed, 64)
            t.barrier()
        tile_x = s.sb("x", [P, T])
        qT, kT = s.sb("qT", [P, 4, T]), s.sb("kT", [P, 4, T])
        v = s.sb("v", [P, 2, P])
        NQW, NP_, NT = 3, 3, 3
        qw = s.sb("qw", [P, 2, T])
        m1, m2 = s.sb("qw_cos", [P, NQW, T]), s.sb("qw_sin", [P, NQW, T])
        pr, pt = s.sb("probs", [P, NP_, T]), s.sb("probs_T", [P, NT, T])
        nmax, rsum, rinv = s.sb("neg_max", [P, 2 * H]), s.sb("row_sum", [P, 2 * H]), s.sb("row_inv", [P, 2 * H])
        on, oT = s.sb("o_normed", [P, 2, P]), s.sb("oT", [P, T])
        pj = s.banks("pj", 6)
        ob = s.banks("out", 2)
        (copied, q_mm, k_mm, v_mm, q_sb, k_sb, v_sb, qw_mm, qw_sb, cosed, sined, logit_mm, maxed, probs, tr_mm, tr_sb,
         pv_mm, inv, normed, oT_mm, oT_sb, wo_mm) = s.sems(
            "copied q_mm k_mm v_mm q_sb k_sb v_sb qw_mm qw_sb cosed sined logit_mm maxed probs tr_mm tr_sb pv_mm inv "
            "normed oT_mm oT_sb wo_mm")
        units = [(h, t) for h in range(H) for t in range(2)]
        NU = len(units)
        with nc.Fori(0, xa.shape[1] // T) as b:
            with nc.Block() as block:
                def evac(eng, u):
                    eng.wait_ge(tr_mm, u + 1)
                    if u >= NT:
                        eng.wait_ge(pv_mm, u - NT + 1)
                    eng.wait_ge(tr_sb, u)
                    if u % 2:
                        ins = nc.scalar.activation(pt[:, u % NT, :], pj[:, 2 + u % 2, 0:T], ACT.Copy)
                    else:
                        ins = nc.vector.tensor_copy(pt[:, u % NT, :], pj[:, 2 + u % 2, 0:T])
                    ins.then_inc(tr_sb, 1)

                @block.tensor
                def _(pe):
                    for kind, n in enumerate(["wq", "wk"]):
                        for j in range(4):
                            nc.tensor.matmul(pj[:, 2 * kind + j // 2, (j % 2) * T:(j % 2 + 1) * T], wp_[n][:, j, :],
                                             xa[:, tokens(b)], start=True, stop=True).then_inc((q_mm, k_mm)[kind], 1)
                    pe.wait_ge(copied, 1)
                    for t in range(2):
                        nc.tensor.matmul(pj[:, 4, t * P:(t + 1) * P], tile_x[:, t * P:(t + 1) * P], w["wv"][:],
                                         start=True, stop=True).then_inc(v_mm, 1)
                    pe.wait_ge(q_sb, 4)
                    pe.wait_ge(k_sb, 4)
                    pe.wait_ge(v_sb, 1)

                    def position(h):
                        r, j = slice(32 * (h % 4), 32 * (h % 4) + 32), h // 4
                        if h >= 2:
                            pe.wait_ge(qw_sb, h - 1)
                        nc.tensor.matmul(pj[:, 4 + h % 2, 0:T], wpos[r, j, :], qT[r, j, :], start=True, stop=True,
                                         tile_position=(32 * (h % 4), 0)).then_inc(qw_mm, 1)

                    def logit(u):
                        h, t = units[u]
                        r, j = slice(32 * (h % 4), 32 * (h % 4) + 32), h // 4
                        o = pj[:, u % 2, 0:T]
                        if u >= 2:
                            pe.wait_ge(probs, u - 1)
                        nc.tensor.matmul(o, qT[r, j, t * P:(t + 1) * P], kT[r, j, :], start=True, stop=False,
                                         tile_position=(32 * (h % 4), 0))
                        pe.wait_ge(cosed, h + 1)
                        nc.tensor.matmul(o, m1[:, h % NQW, t * P:(t + 1) * P], trig[:, 2, :], start=False, stop=False)
                        pe.wait_ge(sined, h + 1)
                        nc.tensor.matmul(o, m2[:, h % NQW, t * P:(t + 1) * P], trig[:, 3, :], start=False,
                                         stop=True).then_inc(logit_mm, 1)

                    def transpose(u):
                        pe.wait_ge(probs, u + 1)
                        if u >= 2:
                            pe.wait_ge(tr_sb, u - 1)
                        for kt in range(2):
                            ins = nc.tensor.transpose(pj[:, 2 + u % 2, kt * P:(kt + 1) * P],
                                                      pr[:, u % NP_, kt * P:(kt + 1) * P], c["ident"][:])
                        ins.then_inc(tr_mm, 1)

                    def weigh(u):
                        h, t = units[u]
                        pe.wait_ge(tr_sb, u + 1)
                        for kt in range(2):
                            ins = nc.tensor.matmul(ob[:, t, 8 * h:8 * h + 8], pt[:, u % NT, kt * P:(kt + 1) * P],
                                                   v[:, kt, 8 * h:8 * h + 8], start=kt == 0, stop=kt == 1)
                        ins.then_inc(pv_mm, 1)

                    position(0)
                    position(1)
                    for u in range(NU + 3):
                        if u < NU:
                            logit(u)
                            if u % 2 == 0 and u // 2 + 2 < H:
                                position(u // 2 + 2)
                        if 2 <= u < NU + 2:
                            transpose(u - 2)
                        if 3 <= u:
                            weigh(u - 3)
                    for t in range(2):
                        pe.wait_ge(normed, t + 1)
                        nc.tensor.transpose(pj[:, 4, t * P:(t + 1) * P], on[:, t, :], c["ident"][:]).then_inc(oT_mm, 1)
                    pe.wait_ge(oT_sb, 1)
                    nc.tensor.matmul(pj[:, 5, 0:T], w["wo"][:], oT[:], start=True, stop=True).then_inc(wo_mm, 1)

                @block.scalar
                def _(act):
                    nc.scalar.activation(tile_x[:], xa[:, tokens(b)], ACT.Copy).then_inc(copied, 1)
                    for j in range(4):
                        act.wait_ge(q_mm, 2 * (j // 2) + 2)
                        nc.scalar.activation(qT[:, j, :], pj[:, j // 2, (j % 2) * T:(j % 2 + 1) * T], ACT.Copy,
                                             scale=8.0 ** -0.5).then_inc(q_sb, 1)
                    act.wait_ge(v_mm, 2)
                    nc.scalar.activation(v[:].rearrange("p t e -> p (t e)"), pj[:, 4, 0:T], ACT.Copy).then_inc(v_sb, 1)

                    def keep_qw(h):
                        act.wait_ge(qw_mm, h + 1)
                        if h >= 2:
                            act.wait_ge(cosed, h - 1)
                            act.wait_ge(sined, h - 1)
                        nc.scalar.activation(qw[:, h % 2, :], pj[:, 4 + h % 2, 0:T], ACT.Copy).then_inc(qw_sb, 1)
                    keep_qw(0)
                    keep_qw(1)
                    for u in range(NU):
                        act.wait_ge(maxed, u + 1)
                        if u >= NP_:
                            act.wait_ge(tr_mm, u - NP_ + 1)
                        nc.scalar.activation(pr[:, u % NP_, :], pj[:, u % 2, 0:T], ACT.Exp, bias=nmax[:, u:u + 1],
                                             accum_out=rsum[:, u:u + 1]).then_inc(probs, 1)
                        if u % 2 == 0 and u // 2 + 2 < H:
                            keep_qw(u // 2 + 2)
                        if u >= 1 and u % 2 == 0:
                            evac(act, u - 1)
                    evac(act, NU - 1)
                    act.wait_ge(oT_mm, 2)
                    nc.scalar.activation(oT[:], pj[:, 4, 0:T], ACT.Copy).then_inc(oT_sb, 1)

                @block.gpsimd
                def _(pool):
                    for h in range(H):
                        pool.wait_ge(qw_sb, h + 1)
                        if h >= NQW:
                            pool.wait_ge(logit_mm, 2 * (h - NQW) + 2)
                        nc.gpsimd.tensor_tensor(m2[:, h % NQW, :], qw[:, h % 2, :], trig[:, 1, :], ALU.mult).then_inc(sined, 1)

                @block.vector
                def _(dve):
                    for j in range(4):
                        dve.wait_ge(k_mm, 2 * (j // 2) + 2)
                        nc.vector.tensor_copy(kT[:, j, :], pj[:, 2 + j // 2, (j % 2) * T:(j % 2 + 1) * T]).then_inc(k_sb, 1)

                    def times_cos(h):
                        dve.wait_ge(qw_sb, h + 1)
                        if h >= NQW:
                            dve.wait_ge(logit_mm, 2 * (h - NQW) + 2)
                        nc.vector.tensor_tensor(m1[:, h % NQW, :], qw[:, h % 2, :], trig[:, 0, :], ALU.mult).then_inc(cosed, 1)
                    times_cos(0)
                    times_cos(1)
                    for u in range(NU + 2):
                        if u < NU:
                            dve.wait_ge(logit_mm, u + 1)
                            nc.vector.tensor_reduce(out=nmax[:, u:u + 1], in_=pj[:, u % 2, 0:T], axis=AX_X, op=ALU.max,
                                                    negate=True).then_inc(maxed, 1)
                            if u % 2 == 0 and u // 2 + 2 < H:
                                times_cos(u // 2 + 2)
                        if u >= 2 and u % 2 == 0:
                            evac(dve, u - 2)
                    dve.wait_ge(probs, NU)
                    nc.vector.reciprocal(rinv[:], rsum[:]).then_inc(inv, 1)
                    dve.wait_ge(inv, 1)
                    dve.wait_ge(pv_mm, NU)
                    for t in range(2):
                        nc.vector.tensor_tensor(on[:, t, :].rearrange("p (h e) -> p h e", h=H),
                                                ob[:, t, 0:P].rearrange("p (h e) -> p h e", h=H),
                                                rinv[:].rearrange("p (h t) -> p h t", t=2)[:, :, t:t + 1]
                                                .broadcast_to([P, H, 8]), ALU.mult).then_inc(normed, 1)
                    dve.wait_ge(wo_mm, 1)
                    nc.vector.tensor_tensor(out[:, tokens(b)], src[:, tokens(b)], pj[:, 5, 0:T], ALU.add)
            s.barrier()


def top_experts(nc, link, m8, idx, idf, iota, chosen, score, k):
    link(nc.vector.max(m8, score))
    link(nc.vector.max_index(idx, m8, score))
    link(nc.vector.tensor_copy(idf, idx))
    link(nc.vector.tensor_scalar(chosen, iota, idf[:, 0:1], None, ALU.is_equal))
    for i in range(1, k):
        link(nc.vector.scalar_tensor_tensor(out=chosen, in0=iota, scalar=idf[:, i:i + 1], in1=chosen,
                                            op0=ALU.is_equal, op1=ALU.add))


def relu_experts(nc, c, d, src, x2, out):
    E, TOPK = 32, 4
    with Scope(nc, "m2") as s:
        keys, vals = s.sb("keys", [P, E, P]), s.sb("values", [P, E, P])
        selw = s.sb("sel_w", [P, E])
        load(nc, s, [(keys[:], d["keys"].rearrange("e p n -> p e n")), (vals[:], d["values"].rearrange("e p n -> p e n")),
                     (selw[:], d["sel_w"])])
        iota = make_iota(nc, s, E)
        tile_x = s.sb("x", [P, T])
        sel, chosen, gate = s.sb("scores", [P, 2, E]), s.sb("chosen", [P, 2, E]), s.sb("gate", [P, 2, E])
        m8, idx, idf = s.sb("top8", [P, 2, 8]), s.sb("idx", [P, 2, 8], U32), s.sb("idx_f", [P, 2, 8])
        NH = 4
        hs = s.sb("hidden", [P, NH, T])
        acc = s.sb("acc", [P, 2, P])
        hp = s.banks("h", 3)
        op = s.banks("o", 3)
        sp_ = s.banks("scores", 1)
        fin = s.banks("final", 1)
        copied, sel_mm, scored, step, gated, h_mm, h_act, o_mm, added, acc_mm = s.sems(
            "copied sel_mm scored step gated h_mm h_act o_mm added acc_mm")
        with nc.Fori(0, x2.shape[1] // T) as b:
            with nc.Block() as block:
                @block.tensor
                def _(pe):
                    pe.wait_ge(copied, 1)
                    for t in range(2):
                        nc.tensor.matmul(sp_[:, 0, t * E:(t + 1) * E], tile_x[:, t * P:(t + 1) * P], selw[:], start=True,
                                         stop=True).then_inc(sel_mm, 1)
                    for e in range(E + 2):
                        if e < E:
                            if e >= 3:
                                pe.wait_ge(h_act, e - 2)
                            nc.tensor.matmul(hp[:, e % 3, 0:T], keys[:, e, :], tile_x[:], start=True,
                                             stop=True).then_inc(h_mm, 1)
                        if e >= 2:
                            f = e - 2
                            pe.wait_ge(h_act, f + 1)
                            if f >= 3:
                                pe.wait_ge(added, 2 * (f - 2))
                            for t in range(2):
                                ins = nc.tensor.matmul(op[:, f % 3, t * P:(t + 1) * P], hs[:, f % NH, t * P:(t + 1) * P],
                                                       vals[:, f, :], start=True, stop=True)
                            ins.then_inc(o_mm, 1)
                    pe.wait_ge(added, 2 * E)
                    for t in range(2):
                        ins = nc.tensor.transpose(fin[:, 0, t * P:(t + 1) * P], acc[:, t, :], c["ident"][:])
                    ins.then_inc(acc_mm, 1)

                @block.scalar
                def _(act):
                    nc.scalar.activation(tile_x[:], x2[:, tokens(b)], ACT.Copy).then_inc(copied, 1)
                    act.wait_ge(sel_mm, 2)
                    nc.scalar.activation(sel[:].rearrange("p t e -> p (t e)"), sp_[:, 0, 0:2 * E],
                                         ACT.Sigmoid).then_inc(scored, 1)
                    for e in range(E):
                        act.wait_ge(h_mm, e + 1)
                        if e >= NH:
                            act.wait_ge(o_mm, e - NH + 1)
                        nc.scalar.activation(hs[:, e % NH, :], hp[:, e % 3, 0:T], ACT.Relu).then_inc(h_act, 1)

                @block.vector
                def _(dve):
                    link = Link(dve, step)
                    dve.wait_ge(scored, 1)
                    for t in range(2):
                        top_experts(nc, link, m8[:, t, :], idx[:, t, :], idf[:, t, :], iota[:], chosen[:, t, :],
                                    sel[:, t, :], TOPK)
                    link(nc.vector.tensor_tensor(gate[:], chosen[:], sel[:], ALU.mult))
                    for e in range(E):
                        dve.wait_ge(o_mm, e + 1)
                        for t in range(2):
                            o = op[:, e % 3, t * P:(t + 1) * P]
                            if e == 0:
                                ins = nc.vector.tensor_scalar(acc[:, t, :], o, gate[:, t, e:e + 1], None, ALU.mult)
                            else:
                                dve.wait_ge(added, 2 * (e - 1) + t + 1)
                                ins = nc.vector.scalar_tensor_tensor(out=acc[:, t, :], in0=o, scalar=gate[:, t, e:e + 1],
                                                                     in1=acc[:, t, :], op0=ALU.mult, op1=ALU.add)
                            ins.then_inc(added, 1)
                    dve.wait_ge(acc_mm, 1)
                    nc.vector.tensor_tensor(out[:, tokens(b)], src[:, tokens(b)], fin[:, 0, 0:T], ALU.add)
            s.barrier()


def l2_ffn(nc, c, d, xn, g_out):
    with Scope(nc, "f2") as s:
        normed = s.sb("normed", [P, xn.shape[1]])
        vec = s.sb("vectors", [P, 4])
        load(nc, s, [(vec[:, i:i + 1], column(d[n])) for i, n in enumerate(["ln1_g", "ln1_b", "ln2_g", "ln2_b"])])
        gate_and_norm(nc, c, xn, normed, affine=(vec[:, 0:1], vec[:, 1:2]))
        relative_attention(nc, c, d, xn, normed, g_out)
        gate_and_norm(nc, c, g_out, normed, affine=(vec[:, 2:3], vec[:, 3:4]))
        relu_experts(nc, c, d, g_out, normed, g_out)


def l3_attention(nc, c, d, xn, s_out, normed):
    DI, NS, DR, KC = 256, 16, 64, 4
    NC_ = DI // P
    DIRS = ("f", "b")
    with Scope(nc, "a3") as s:
        vec = s.sb("vectors", [P, 2])
        W = [{"in": s.sb(f"{x}_in", [P, 2 * DI]), "conv": s.sb(f"{x}_conv", [P, NC_, KC]), "cb": s.sb(f"{x}_cb", [P, NC_]),
              "xp": s.sb(f"{x}_xproj", [P, NC_, DR + 2 * NS]), "dt": s.sb(f"{x}_dt", [DR, DI]),
              "dtb": s.sb(f"{x}_dtb", [P, NC_]), "A": s.sb(f"{x}_A", [P, NC_, NS]), "D": s.sb(f"{x}_D", [P, NC_]),
              "out": s.sb(f"{x}_out", [P, NC_, P])} for x in DIRS]
        pairs = [(vec[:, 0:1], column(d["ln_g"])), (vec[:, 1:2], column(d["ln_b"]))]
        for x, w in zip(DIRS, W):
            pairs += [(w["in"][:], d[x + "_in_wT"]), (w["conv"][:], d[x + "_conv_w"].rearrange("(c p) k -> p c k", p=P)),
                      (w["cb"][:], column(d[x + "_conv_b"])),
                      (w["xp"][:], d[x + "_xproj_wT"].rearrange("(c p) k -> p c k", p=P)), (w["dt"][:], d[x + "_dt_wT"]),
                      (w["dtb"][:], column(d[x + "_dt_b"])), (w["A"][:], d[x + "_Alog"].rearrange("(c p) k -> p c k", p=P)),
                      (w["D"][:], column(d[x + "_D"])), (w["out"][:], d[x + "_out_wT"].rearrange("(c p) k -> p c k", p=P))]
        load(nc, s, pairs)
        gate_and_norm(nc, c, xn, normed, affine=(vec[:, 0:1], vec[:, 1:2]))

        def two(name, shape, dt=F32):
            return [s.sb(f"{name}{i}", shape, dt) for i in range(2)]
        BC = 2 * NS
        tx = two("x", [P, T])
        up = two("u_padded", [P, NC_, T + KC - 1])
        u, zs, dt, dtu = two("u", [P, NC_, T]), two("silu_z", [P, NC_, T]), two("dt", [P, NC_, T]), two("dt_u", [P, NC_, T])
        ex = two("exp", [P, NC_, T])
        dbc = two("dbc", [DR + BC, T])
        rest = s.sb("bc_rest", [DR + BC, T])
        piece = s.sb("bc_piece", [DR + BC, 2, T], BF16)
        parts = two("bc_parts", [3 * BC, T], BF16)
        pick_int = s.sb("pick_f32", [3 * BC, BC])
        pick = s.sb("pick", [3 * BC, BC], BF16)
        dA = two("dA", [P, NS, T])
        h = two("h", [P, NS, T])
        Bs = two("B", [P, 2, T])
        Cs = s.sb("C", [P, NS, T])
        yz = s.sb("y", [P, NC_, T])
        sum_ = s.sb("sum", [P, T])
        pj = s.banks("pj", 2)
        bc = s.banks("bc", 3)
        yp = s.banks("y", 2)
        op = s.banks("out", 1)
        (copied, uz_mm, u_sb, z_sb, conved, u_act, dbc_mm, dbc_sb, split, dt_mm, dt_abs, dt_exp, dt_log, dt_max, dt_sb,
         dtu_sb, step, dA_sb, b_mm, b_sb, c_mm, c_sb, hb0, hb1, scanned, hc_dve, hc_pool, y0_mm, y1_mm, y_sb, out_mm,
         summed, cleared) = s.sems(
            "copied uz_mm u_sb z_sb conved u_act dbc_mm dbc_sb split dt_mm dt_abs dt_exp dt_log dt_max dt_sb "
            "dtu_sb step dA_sb b_mm b_sb c_mm c_sb hb0 hb1 scanned hc_dve hc_pool y0_mm y1_mm y_sb out_mm "
            "summed cleared")
        with nc.Block() as block:
            @block.vector
            def _(dve):
                dve.wait_ge(cleared, 1)
                for w in W:
                    nc.vector.tensor_scalar(w["A"][:], w["A"][:], -1.0, None, ALU.mult)
                dve.wait_ge(step, 4)
                nc.vector.tensor_copy(pick[:], pick_int[:])

            @block.scalar
            def _(act):
                for w in W:
                    ins = nc.scalar.activation(w["A"][:], w["A"][:], ACT.Exp)
                ins.then_inc(cleared, 1)

            @block.gpsimd
            def _(pool):
                nc.gpsimd.memset(pick_int[:], 0.0).then_inc(step, 1)
                for part in range(3):
                    pool.wait_ge(step, part + 1)
                    nc.gpsimd.affine_select(out=pick_int[:], in_=pick_int[:], compare_op=ALU.not_equal, fill=1.0,
                                            base=-BC * part, pattern=[[-1, BC]], channel_multiplier=1).then_inc(step, 1)
                for i in range(2):
                    nc.gpsimd.memset(up[i][:], 0.0)
                    nc.gpsimd.memset(dA[i][:, :, 0:1], 0.0)
        s.barrier()
        NPAIR = NS // 2
        POOL_PAIRS = (1, 3, 5, 7)
        NPP = len(POOL_PAIRS)
        PER = 2 * NPAIR - NPP
        R = 4

        with nc.Fori(0, xn.shape[1] // (2 * T)) as b:
            with nc.Block() as block:
                def seq(r):
                    return bass.ds((b * 2 + r // 2) * T, T)

                def bank_of(r, i, m):
                    return ((2 * r + i) * NPAIR + m) % 3

                @block.tensor
                def _(pe):
                    mm = nc.tensor.matmul

                    def in_proj(n):
                        w = W[n % 2]
                        pe.wait_ge(copied, n + 1)
                        for i in range(2):
                            if i == 0 and n:
                                pe.wait_ge(dbc_sb, n)
                            if i == 1 and n:
                                pe.wait_ge(dt_max, NC_ * n)
                            for k in range(NC_):
                                ins = mm(pj[:, i, k * T:(k + 1) * T], w["in"][:, (i * NC_ + k) * P:(i * NC_ + k + 1) * P],
                                         tx[n % 2][:], start=True, stop=True)
                            ins.then_inc(uz_mm, 1)

                    def x_proj(n):
                        pe.wait_ge(u_act, NC_ * (n + 1))
                        pe.wait_ge(u_sb, n + 1)
                        for k in range(NC_):
                            ins = mm(pj[0:DR + BC, 0, 0:T], W[n % 2]["xp"][:, k, :], u[n % 2][:, k, :], start=k == 0,
                                     stop=k == NC_ - 1)
                        ins.then_inc(dbc_mm, 1)

                    def dt_proj(n):
                        pe.wait_ge(dbc_sb, n + 1)
                        pe.wait_ge(z_sb, n + 1)
                        for k in range(NC_):
                            ins = mm(pj[:, 1, k * T:(k + 1) * T], W[n % 2]["dt"][:, k * P:(k + 1) * P],
                                     dbc[n % 2][0:DR, :], start=True, stop=True)
                        ins.then_inc(dt_mm, 1)

                    def spread(r, i, m):
                        q = (2 * r + i) * NPAIR + m - 3
                        if q >= 0:
                            rq, iq, mq = q // (2 * NPAIR), q // NPAIR % 2, q % NPAIR
                            pe.wait_ge((b_sb, c_sb)[iq], rq * NPAIR + mq + 1)
                            if iq == 0:
                                pe.wait_ge(hb0, rq * NPAIR + mq + 1)
                        for k in range(2):
                            row = NS * i + 2 * m + k
                            ins = mm(bc[:, bank_of(r, i, m), k * T:(k + 1) * T],
                                     pick[:, row:row + 1].broadcast_to([3 * BC, P]), parts[r % 2][:], start=True, stop=True)
                        ins.then_inc((b_mm, c_mm)[i], 1)

                    def sum_states(r, k, m):
                        if k == 1 and m in POOL_PAIRS:
                            pe.wait_ge(hc_pool, r * NPP + POOL_PAIRS.index(m) + 1)
                        else:
                            own = sum(1 for x in range(m + 1) if x not in POOL_PAIRS)
                            pe.wait_ge(hc_dve, r * PER + (m + 1 if k == 0 else NPAIR + own))
                        if m == 0 and r:
                            pe.wait_ge(y_sb, NC_ * (r - 1) + k + 1)
                        for n in (2 * m, 2 * m + 1):
                            ins = mm(yp[:, k, 0:T], c["ident"][:], h[k][:, n, :], start=n == 0, stop=n == NS - 1)
                        if k == 1:
                            ins.then_inc(y1_mm, 1)
                        elif m == NPAIR - 1:
                            ins.then_inc(y0_mm, 1)

                    def out_proj(r):
                        pe.wait_ge(y_sb, NC_ * (r + 1))
                        if r:
                            pe.wait_ge(summed, r)
                        for k in range(NC_):
                            ins = mm(op[:, 0, 0:T], W[r % 2]["out"][:, k, :], yz[:, k, :], start=k == 0, stop=k == NC_ - 1)
                        ins.then_inc(out_mm, 1)

                    in_proj(0)
                    x_proj(0)
                    dt_proj(0)
                    for r in range(R):
                        pe.wait_ge(split, r + 1)
                        for m in range(NPAIR):
                            spread(r, 0, m)
                            if r:
                                sum_states(r - 1, 1, m)
                        if r + 1 < R:
                            in_proj(r + 1)
                        for m in range(NPAIR):
                            spread(r, 1, m)
                        if r:
                            out_proj(r - 1)
                        if r + 1 < R:
                            x_proj(r + 1)
                            dt_proj(r + 1)
                        for m in range(NPAIR):
                            sum_states(r, 0, m)
                    for m in range(NPAIR):
                        sum_states(R - 1, 1, m)
                    out_proj(R - 1)

                @block.scalar
                def _(act):
                    ac = nc.scalar.activation

                    def take_uz(n):
                        if n % 2 == 0:
                            ac(tx[0][:], normed[:, seq(n)], ACT.Copy).then_inc(copied, 1)
                        else:
                            act.wait_ge(copied, n)
                            ac(tx[1][:], tx[0][:, ::-1], ACT.Copy).then_inc(copied, 1)
                        act.wait_ge(uz_mm, 2 * n + 1)
                        ac(up[n % 2][:, :, KC - 1:], pj[:, 0, :].rearrange("p (k t) -> p k t", k=NC_), ACT.Copy).then_inc(u_sb, 1)
                        act.wait_ge(uz_mm, 2 * n + 2)
                        if n >= 2:
                            act.wait_ge(y_sb, NC_ * (n - 1))
                        ac(zs[n % 2][:].rearrange("p k t -> p (k t)"), pj[:, 1, :], ACT.Silu).then_inc(z_sb, 1)

                    def take_u(n):
                        for k in range(NC_):
                            act.wait_ge(conved, NC_ * n + k + 1)
                            ac(u[n % 2][:, k, :], ex[n % 2][:, k, :], ACT.Silu, bias=W[n % 2]["cb"][:, k:k + 1]).then_inc(u_act, 1)
                        act.wait_ge(dbc_mm, n + 1)
                        ac(dbc[n % 2][:], pj[0:DR + BC, 0, 0:T], ACT.Copy).then_inc(dbc_sb, 1)

                    def softplus(n):
                        act.wait_ge(dt_mm, n + 1)
                        for k in range(NC_):
                            ac(ex[n % 2][:, k, :], pj[:, 1, k * T:(k + 1) * T], ACT.Abs,
                               bias=W[n % 2]["dtb"][:, k:k + 1]).then_inc(dt_abs, 1)
                        act.wait_ge(dt_abs, NC_ * (n + 1))
                        ac(ex[n % 2][:], ex[n % 2][:], ACT.Exp, scale=-1.0).then_inc(dt_exp, 1)
                        act.wait_ge(dt_exp, n + 1)
                        ac(ex[n % 2][:], ex[n % 2][:], ACT.Ln, bias=c["ones"][:, 0:1]).then_inc(dt_log, 1)

                    def decay(r, k, n):
                        ac(dA[k][:, n, 1:], dt[r % 2][:, k, 1:], ACT.Exp,
                           scale=W[r % 2]["A"][:, k, n:n + 1]).then_inc(dA_sb, 1)

                    take_uz(0)
                    take_u(0)
                    softplus(0)
                    for r in range(R):
                        act.wait_ge(dt_sb, r + 1)
                        if r:
                            act.wait_ge(scanned, NC_ * (r - 1) + 1)
                        for m in range(NPAIR):
                            decay(r, 0, 2 * m)
                            decay(r, 0, 2 * m + 1)
                            act.wait_ge(b_mm, r * NPAIR + m + 1)
                            act.wait_ge(hb0, r * NPAIR + m + 1)
                            if r * NPAIR + m >= 2:
                                act.wait_ge(hb1, r * NPAIR + m - 1)
                            ac(Bs[m % 2][:].rearrange("p k t -> p (k t)"), bc[:, bank_of(r, 0, m), :], ACT.Copy).then_inc(b_sb, 1)
                        if r + 1 < R:
                            take_uz(r + 1)
                        if r:
                            act.wait_ge(hc_dve, r * PER)
                            act.wait_ge(hc_pool, r * NPP)
                        for m in range(NPAIR):
                            act.wait_ge(c_mm, r * NPAIR + m + 1)
                            ac(Cs[:, 2 * m:2 * m + 2, :].rearrange("p k t -> p (k t)"), bc[:, bank_of(r, 1, m), :],
                               ACT.Copy).then_inc(c_sb, 1)
                        if r + 1 < R:
                            take_u(r + 1)
                        if r:
                            act.wait_ge(scanned, NC_ * r)
                        for n in range(NS):
                            decay(r, 1, n)
                        if r + 1 < R:
                            softplus(r + 1)

                @block.gpsimd
                def _(pool):
                    for r in range(R):
                        pool.wait_ge(dtu_sb, r + 1)
                        for m in range(NPAIR):
                            pool.wait_ge(b_sb, r * NPAIR + m + 1)
                            if r:
                                pool.wait_ge(y1_mm, (r - 1) * NPAIR + m + 1)
                            nc.gpsimd.tensor_tensor(h[1][:, 2 * m:2 * m + 2, :], Bs[m % 2][:],
                                                    dtu[r % 2][:, 1:2, :].broadcast_to([P, 2, T]), ALU.mult).then_inc(hb1, 1)
                        pool.wait_ge(scanned, NC_ * r + 2)
                        for m in POOL_PAIRS:
                            pool.wait_ge(c_sb, r * NPAIR + m + 1)
                            nc.gpsimd.tensor_tensor(h[1][:, 2 * m:2 * m + 2, :], h[1][:, 2 * m:2 * m + 2, :],
                                                    Cs[:, 2 * m:2 * m + 2, :], ALU.mult).then_inc(hc_pool, 1)

                @block.vector
                def _(dve):
                    link = Link(dve, step)
                    tt, ts, stt = nc.vector.tensor_tensor, nc.vector.tensor_scalar, nc.vector.scalar_tensor_tensor

                    def convolve(n):
                        dve.wait_ge(u_sb, n + 1)
                        w, src, dst = W[n % 2]["conv"], up[n % 2], ex[n % 2]
                        for k in range(NC_):
                            link(ts(dst[:, k, :], src[:, k, 0:T], w[:, k, 0:1], None, ALU.mult))
                            for j in range(1, KC):
                                ins = stt(out=dst[:, k, :], in0=src[:, k, j:j + T], scalar=w[:, k, j:j + 1],
                                          in1=dst[:, k, :], op0=ALU.mult, op1=ALU.add)
                                if j < KC - 1:
                                    link(ins)
                            ins.then_inc(conved, 1)

                    def split_bc(n):
                        dve.wait_ge(dbc_sb, n + 1)
                        if n >= 2:
                            dve.wait_ge(c_mm, (n - 1) * NPAIR)
                        src, q = dbc[n % 2][DR:, :], slice(DR, DR + BC)
                        link(nc.vector.tensor_copy(piece[q, 0, :], src))
                        link(tt(rest[q, :], src, piece[q, 0, :], ALU.subtract))
                        link(nc.vector.tensor_copy(piece[q, 1, :], rest[q, :]))
                        link(tt(parts[n % 2][2 * BC:, :], rest[q, :], piece[q, 1, :], ALU.subtract))
                        link(nc.vector.tensor_copy(parts[n % 2][0:BC, :], piece[q, 0, :]))
                        nc.vector.tensor_copy(parts[n % 2][BC:2 * BC, :], piece[q, 1, :]).then_inc(split, 1)

                    def finish_dt(n):
                        dve.wait_ge(dt_abs, NC_ * (n + 1))
                        for k in range(NC_):
                            ts(dt[n % 2][:, k, :], pj[:, 1, k * T:(k + 1) * T], W[n % 2]["dtb"][:, k:k + 1], 0.0, ALU.add,
                               ALU.max).then_inc(dt_max, 1)
                        dve.wait_ge(dt_max, NC_ * (n + 1))
                        dve.wait_ge(dt_log, n + 1)
                        tt(dt[n % 2][:], dt[n % 2][:], ex[n % 2][:], ALU.add).then_inc(dt_sb, 1)
                        dve.wait_ge(dt_sb, n + 1)
                        dve.wait_ge(u_act, NC_ * (n + 1))
                        tt(dtu[n % 2][:], dt[n % 2][:], u[n % 2][:], ALU.mult).then_inc(dtu_sb, 1)

                    def scan(r, k):
                        dve.wait_ge((hb0, hb1)[k], (r + 1) * NPAIR)
                        dve.wait_ge(dA_sb, (NC_ * r + k + 1) * NS)
                        flat = h[k][:].rearrange("p n t -> p (n t)")
                        nc.vector.tensor_tensor_scan(flat, dA[k][:].rearrange("p n t -> p (n t)"), flat, 0.0, ALU.mult,
                                                     ALU.add).then_inc(scanned, 1)

                    def times_c(r, k):
                        dve.wait_ge(scanned, NC_ * r + k + 1)
                        for m in range(NPAIR):
                            if k == 1 and m in POOL_PAIRS:
                                continue
                            dve.wait_ge(c_sb, r * NPAIR + m + 1)
                            tt(h[k][:, 2 * m:2 * m + 2, :], h[k][:, 2 * m:2 * m + 2, :], Cs[:, 2 * m:2 * m + 2, :],
                               ALU.mult).then_inc(hc_dve, 1)

                    def finish_y(r):
                        if r:
                            dve.wait_ge(out_mm, r)
                        for k in range(NC_):
                            dve.wait_ge((y0_mm, y1_mm)[k], r + 1 if k == 0 else NPAIR * (r + 1))
                            link(stt(out=yz[:, k, :], in0=u[r % 2][:, k, :], scalar=W[r % 2]["D"][:, k:k + 1],
                                     in1=yp[:, k, 0:T], op0=ALU.mult, op1=ALU.add))
                            tt(yz[:, k, :], yz[:, k, :], zs[r % 2][:, k, :], ALU.mult).then_inc(y_sb, 1)

                    def finish_out(r):
                        dve.wait_ge(out_mm, r + 1)
                        if r % 2 == 0:
                            tt(sum_[:], xn[:, seq(r)], op[:, 0, 0:T], ALU.add).then_inc(summed, 1)
                        else:
                            dve.wait_ge(summed, r)
                            tt(s_out[:, seq(r)], sum_[:], op[:, 0, 0:T][:, ::-1], ALU.add).then_inc(summed, 1)

                    convolve(0)
                    split_bc(0)
                    finish_dt(0)
                    for r in range(R):
                        dve.wait_ge(dtu_sb, r + 1)
                        if r:
                            dve.wait_ge(y0_mm, r)
                        for m in range(NPAIR):
                            dve.wait_ge(b_mm, r * NPAIR + m + 1)
                            tt(h[0][:, 2 * m:2 * m + 2, :], bc[:, bank_of(r, 0, m), :].rearrange("p (k t) -> p k t", k=2),
                               dtu[r % 2][:, 0:1, :].broadcast_to([P, 2, T]), ALU.mult).then_inc(hb0, 1)
                        if r:
                            finish_y(r - 1)
                        if r + 1 < R:
                            convolve(r + 1)
                        scan(r, 0)
                        if r + 1 < R:
                            split_bc(r + 1)
                        times_c(r, 0)
                        if r:
                            finish_out(r - 1)
                        scan(r, 1)
                        times_c(r, 1)
                        if r + 1 < R:
                            finish_dt(r + 1)
                    finish_y(R - 1)
                    finish_out(R - 1)
            s.barrier()


def l3_ffn(nc, c, d, xn, g_out):
    E, F, TOPK = 16, 176, 2
    CAP = int(np.ceil(1.25 * xn.shape[1] * TOPK / E))
    FH = F // 2
    NE = E + 1
    with Scope(nc, "f3") as s:
        wg, wu = s.sb("w_gate", [P, NE, F]), s.sb("w_up", [P, NE, F])
        wd = s.sb("w_down", [FH, NE, 2, P])
        rw, rb = s.sb("router_w", [P, E]), s.sb("router_b", [1, E])
        load(nc, s, [(wg[:, 0:E, :], d["w_gate"].rearrange("e p f -> p e f")), (wg[:, E, :], d["sw_gate"]),
                     (wu[:, 0:E, :], d["w_up"].rearrange("e p f -> p e f")), (wu[:, E, :], d["sw_up"]),
                     (wd[:, 0:E].rearrange("p e a n -> p (e a) n"),
                      d["w_down"].rearrange("e (a p) n -> p (e a) n", p=FH)),
                     (wd[:, E], d["sw_down"].rearrange("(a p) n -> p a n", p=FH)),
                     (rw[:], d["router_w"]), (rb[:], d["router_b"].rearrange("(a n) -> a n", a=1))])
        iota = make_iota(nc, s, E)
        tile_x = s.sb("x", [P, T])
        nmax, psum_, pinv = s.sb("neg_max", [P, 2]), s.sb("prob_sum", [P, 2]), s.sb("prob_inv", [P, 2])
        probs, chosen = s.sb("probs", [P, 2, E]), s.sb("chosen", [P, 2, E])
        m8, idx, idf = s.sb("top8", [P, 2, 8]), s.sb("idx", [P, 2, 8], U32), s.sb("idx_f", [P, 2, 8])
        gate = s.sb("gate", [P, 2, NE])
        seen = s.sb("seen", [P, E])
        NHB = 3
        sg = s.sb("silu", [FH, NHB, 2, T])
        hm = s.sb("hidden", [FH, NHB, 2, T])
        acc = s.sb("acc", [P, 2, P])
        gp, upp, op = s.banks("gate", 2), s.banks("up", 2), s.banks("o", 2)
        lp, cp = s.banks("logits", 1), s.banks("count", 1)
        copied, log_mm, maxed, exped, step, picked, cnt_mm, g_mm, u_mm, silued, hidden, o_mm, added, acc_mm = s.sems(
            "copied log_mm maxed exped step picked cnt_mm g_mm u_mm silued hidden o_mm added acc_mm")
        with nc.Block() as block:
            @block.vector
            def _(dve):
                nc.vector.memset(seen[:], 0.0)
                nc.vector.memset(gate[:], 1.0)
        s.barrier()
        with nc.Fori(0, xn.shape[1] // T) as b:
            with nc.Block() as block:
                order = [E] + list(range(E))

                @block.tensor
                def _(pe):
                    mm = nc.tensor.matmul
                    pe.wait_ge(copied, 1)
                    for t in range(2):
                        o = lp[:, 0, t * E:(t + 1) * E]
                        mm(o, tile_x[:, t * P:(t + 1) * P], rw[:], start=True, stop=False)
                        ins = mm(o, c["ones"][0:1, :], rb[:], start=False, stop=True)
                    ins.then_inc(log_mm, 1)

                    def raise_(i):
                        e = order[i]
                        for w, ps, done, used in ((wg, gp, g_mm, silued), (wu, upp, u_mm, hidden)):
                            if i >= 2:
                                pe.wait_ge(used, i - 1)
                            for a in range(2):
                                ins = mm(ps[0:FH, i % 2, a * T:(a + 1) * T], w[:, e, a * FH:(a + 1) * FH], tile_x[:],
                                         start=True, stop=True)
                            ins.then_inc(done, 1)

                    def lower(i):
                        e = order[i]
                        pe.wait_ge(hidden, i + 1)
                        if i >= 2:
                            pe.wait_ge(added, 2 * (i - 1))
                        for t in range(2):
                            for a in range(2):
                                ins = mm(op[:, i % 2, t * P:(t + 1) * P], hm[:, i % NHB, a, t * P:(t + 1) * P],
                                         wd[:, e, a, :], start=a == 0, stop=a == 1)
                        ins.then_inc(o_mm, 1)

                    for i in range(NE + 1):
                        if i < NE:
                            raise_(i)
                        if i == 1:
                            pe.wait_ge(picked, 2)
                            mm(cp[:, 0, 0:E], c["earlier"][:], chosen[:, 0, :], start=True, stop=False)
                            mm(cp[:, 0, 0:E], c["mean"][:], seen[:], start=False, stop=True)
                            mm(cp[:, 0, E:2 * E], c["earlier"][:], chosen[:, 1, :], start=True, stop=False)
                            mm(cp[:, 0, E:2 * E], c["mean"][:], seen[:], start=False, stop=False)
                            mm(cp[:, 0, E:2 * E], c["ones"][:], chosen[:, 0, :], start=False, stop=True)
                            for t in range(2):
                                ins = mm(cp[:, 0, 2 * E:3 * E], c["ones"][:], chosen[:, t, :], start=t == 0, stop=t == 1)
                            ins.then_inc(cnt_mm, 1)
                        if i >= 1:
                            lower(i - 1)
                    pe.wait_ge(added, 2 * NE)
                    for t in range(2):
                        ins = nc.tensor.transpose(op[:, 0, t * P:(t + 1) * P], acc[:, t, :], c["ident"][:])
                    ins.then_inc(acc_mm, 1)

                @block.scalar
                def _(act):
                    nc.scalar.activation(tile_x[:], xn[:, tokens(b)], ACT.Copy).then_inc(copied, 1)
                    for t in range(2):
                        act.wait_ge(maxed, 1)
                        nc.scalar.activation(probs[:, t, :], lp[:, 0, t * E:(t + 1) * E], ACT.Exp, bias=nmax[:, t:t + 1],
                                             accum_out=psum_[:, t:t + 1]).then_inc(exped, 1)
                    for i in range(NE):
                        act.wait_ge(g_mm, i + 1)
                        if i >= NHB:
                            act.wait_ge(hidden, i - NHB + 1)
                        nc.scalar.activation(sg[:, i % NHB].rearrange("p a t -> p (a t)"), gp[0:FH, i % 2, :],
                                             ACT.Silu).then_inc(silued, 1)

                @block.vector
                def _(dve):
                    link = Link(dve, step)
                    tt, ts = nc.vector.tensor_tensor, nc.vector.tensor_scalar
                    dve.wait_ge(log_mm, 1)
                    nc.vector.tensor_reduce(out=nmax[:], in_=lp[:, 0, 0:2 * E].rearrange("p (t e) -> p t e", t=2),
                                            axis=AX_X, op=ALU.max, negate=True).then_inc(maxed, 1)
                    dve.wait_ge(exped, 2)
                    link(nc.vector.reciprocal(pinv[:], psum_[:]))
                    for t in range(2):
                        link(ts(probs[:, t, :], probs[:, t, :], pinv[:, t:t + 1], None, ALU.mult))
                        top_experts(nc, link, m8[:, t, :], idx[:, t, :], idf[:, t, :], iota[:], chosen[:, t, :],
                                    probs[:, t, :], TOPK)
                        link(nc.vector.tensor_tensor_reduce(out=gate[:, t, 0:E], in0=chosen[:, t, :], in1=probs[:, t, :],
                                                            scale=1.0, scalar=0.0, op0=ALU.mult, op1=ALU.add,
                                                            accum_out=pinv[:, t:t + 1]))
                        link(ts(pinv[:, t:t + 1], pinv[:, t:t + 1], 1e-9, None, ALU.add))
                        link(nc.vector.reciprocal(pinv[:, t:t + 1], pinv[:, t:t + 1]))
                        ts(gate[:, t, 0:E], gate[:, t, 0:E], pinv[:, t:t + 1], None, ALU.mult).then_inc(picked, 1)

                    def combine(i):
                        e = order[i]
                        dve.wait_ge(o_mm, i + 1)
                        for t in range(2):
                            o = op[:, i % 2, t * P:(t + 1) * P]
                            if i == 0:
                                ins = nc.vector.tensor_copy(acc[:, t, :], o)
                            else:
                                dve.wait_ge(added, 2 * (i - 1) + t + 1)
                                ins = nc.vector.scalar_tensor_tensor(out=acc[:, t, :], in0=o, scalar=gate[:, t, e:e + 1],
                                                                     in1=acc[:, t, :], op0=ALU.mult, op1=ALU.add)
                            ins.then_inc(added, 1)

                    for i in range(NE + 1):
                        if i < NE:
                            dve.wait_ge(silued, i + 1)
                            dve.wait_ge(u_mm, i + 1)
                            if i >= NHB:
                                dve.wait_ge(o_mm, i - NHB + 1)
                            tt(hm[:, i % NHB].rearrange("p a t -> p (a t)"), sg[:, i % NHB].rearrange("p a t -> p (a t)"),
                               upp[0:FH, i % 2, :], ALU.mult).then_inc(hidden, 1)
                        if i == 1:
                            dve.wait_ge(cnt_mm, 1)
                            link(nc.vector.scalar_tensor_tensor(
                                out=gate[:, :, 0:E], in0=cp[:, 0, 0:2 * E].rearrange("p (t e) -> p t e", t=2),
                                scalar=float(CAP), in1=gate[:, :, 0:E], op0=ALU.is_lt, op1=ALU.mult))
                            link(tt(seen[:], seen[:], cp[:, 0, 2 * E:3 * E], ALU.add))
                        if i >= 1:
                            combine(i - 1)
                    dve.wait_ge(acc_mm, 1)
                    tt(g_out[:, tokens(b)], xn[:, tokens(b)], op[:, 0, 0:T], ALU.add)
            s.barrier()


TRANSPOSED = {
    "L0_attn_relpos_table", "L1_attn_W_q", "L1_attn_W_k", "L1_attn_W_v", "L1_ffn_slot_init", "L1_ffn_Wih", "L1_ffn_Whh",
    "L2_ffn_wp", "L3_attn_f_in_w", "L3_attn_f_xproj_w", "L3_attn_f_dt_w", "L3_attn_f_out_w", "L3_attn_b_in_w",
    "L3_attn_b_xproj_w", "L3_attn_b_dt_w", "L3_attn_b_out_w",
}


def build(nc, d, out):
    def part(prefix):
        return {k[len(prefix) + 1:]: v for k, v in d.items() if k.startswith(prefix + "_")}
    n = out.shape[1]
    with Scope(nc, "main") as m:
        x, xn, s, g = (m.sb(name, [P, n]) for name in ("x", "xn", "s", "g"))
        c = make_constants(nc, m)
        load(nc, m, [(x[:], d["x"])])
        gate_and_norm(nc, c, x, xn)
        l0_attention(nc, c, part("L0_attn"), xn, s)
        l0_ffn(nc, c, part("L0_ffn"), xn, g)
        gate_and_norm(nc, c, x, xn, s, g, gate=True)
        l1_attention(nc, c, part("L1_attn"), xn, s)
        l1_ffn(nc, c, part("L1_ffn"), xn, g)
        gate_and_norm(nc, c, x, xn, s, g, gate=True)
        l2_attention(nc, c, part("L2_attn"), xn, s)
        l2_ffn(nc, c, part("L2_ffn"), xn, g)
        gate_and_norm(nc, c, x, xn, s, g, gate=True)
        l3_attention(nc, c, part("L3_attn"), xn, s, g)
        l3_ffn(nc, c, part("L3_ffn"), xn, g)
        gate_and_norm(nc, c, x, xn, s, g, gate=True, norm=False, out=out)


def kernel(**inputs):
    import concourse.bacc as bacc
    from concourse.bass_utils import run_bass_kernel_spmd as run

    nc = bacc.Bacc("TRN2", target_bir_lowering=False, num_devices=1)
    x = np.asarray(inputs["L0_attn_x"])
    nb, t, f = x.shape
    arrays = {"x": np.ascontiguousarray(x.reshape(nb * t, f).T), "L2_ffn_trig": l2_ffn_tables(t)}
    for name, a in inputs.items():
        if name == "L0_attn_x":
            continue
        a = np.asarray(a)
        arrays[name + "T" if name in TRANSPOSED else name] = np.ascontiguousarray(a.T if name in TRANSPOSED else a)
    d = {k: nc.dram_tensor(k, a.shape, mybir.dt.from_np(a.dtype), kind="ExternalInput").ap() for k, a in arrays.items()}
    out = nc.dram_tensor("out", (f, nb * t), F32, kind="ExternalOutput").ap()
    build(nc, d, out)
    r = run(nc, [arrays], core_ids=[0])
    return np.ascontiguousarray(r.results[0]["out"].T).reshape(nb, t, f)
```
